# Optimizing a Trainium2 kernel written in Bass

```python
import numpy as np
import jax
import jax.numpy as jnp

def _softmax(x, axis=-1):
    return jax.nn.softmax(x, axis=axis)

def _gelu(x):
    return jax.nn.gelu(x, approximate=True)

def _silu(x):
    return jax.nn.silu(x)

def _sigmoid(x):
    return jax.nn.sigmoid(x)

def _layernorm(x, axis=-1, eps=1e-05):
    m = jnp.mean(x, axis=axis, keepdims=True)
    v = jnp.var(x, axis=axis, keepdims=True)
    return (x - m) / jnp.sqrt(v + eps)

def _scatter_add(tgt, idx, src, axis=0):
    return tgt.at[idx].add(src)

def _segment_sum(src, seg, n):
    return jax.ops.segment_sum(src, seg, n)
kernel_name = 'mk_decoder_postln_d1_seqx_r8_ae8476'

def setup_inputs(seed: int=0):
    np.random.seed(seed)
    _w = jnp.asarray

    def _rec_inputs():
        import jax
        import jax.numpy as jnp
        _rk = jax.random.key(seed)
        x = -0.0002928 + 1 * jax.random.normal(jax.random.fold_in(_rk, 1), (16, 56, 128), jnp.float32)
        _lenS = 56 - jax.random.randint(jax.random.fold_in(_rk, 7), (16,), 0, max(1, 56 // 4) + 1, jnp.int32)
        _lenS2 = 1500 - jax.random.randint(jax.random.fold_in(_rk, 8), (16,), 0, max(1, 1500 // 4) + 1, jnp.int32)
        _ctx_1024P = jax.random.normal(jax.random.fold_in(_rk, 11), (16, 16, 128), jnp.float32)
        _ctx_1024c = jax.random.dirichlet(jax.random.fold_in(_rk, 511), 0.3 * jnp.ones((16,), jnp.float32), (16, 1500))
        _ctx_1024t = jnp.einsum('bsk,bkd->bsd', _ctx_1024c, _ctx_1024P)
        _ctx_1024t = _ctx_1024t * jax.lax.rsqrt(jnp.mean(jnp.square(_ctx_1024t)) + 1e-12) * 0.953939
        ctx_1024 = -1.39393e-06 + 0.999914 * (_ctx_1024t + 0.3 * jax.random.normal(jax.random.fold_in(_rk, 611), (16, 1500, 128), jnp.float32))
        _validS = jnp.arange(56)[None, :] < _lenS[:, None]
        _validS2 = jnp.arange(1500)[None, :] < _lenS2[:, None]
        _causal = jnp.tril(jnp.ones((56, 56), dtype=bool))
        mask_1x1xSxS2_ff0 = jnp.where(jnp.ones((1, 1, 56, 1500), dtype=bool), 0.0, -1000000000.0).astype(jnp.float32)
        return (x, ctx_1024, mask_1x1xSxS2_ff0)
    x, ctx_1024, mask_1x1xSxS2_ff0 = _rec_inputs()

    def _L0_attn_setup():
        import jax, jax.numpy as jnp
        import numpy as np
        import math
        B, S, HID, H = (2, 256, 128, 16)
        D = HID // H

        def _get_slopes(n):
            start = 2 ** (-2 ** (-(math.log2(n) - 3)))
            return np.array([start * 2 ** (-i) for i in range(n)], dtype=np.float32)
        key = jax.random.key(seed)
        ks = jax.random.split(key, 9)
        sc = 1.0 / math.sqrt(HID)
        return {'x': jax.random.normal(ks[0], (B, S, HID), dtype=jnp.float32), 'Wq': jax.random.normal(ks[1], (HID, HID), dtype=jnp.float32) * sc, 'bq': jnp.zeros((HID,), dtype=jnp.float32), 'Wk': jax.random.normal(ks[2], (HID, HID), dtype=jnp.float32) * sc, 'bk': jnp.zeros((HID,), dtype=jnp.float32), 'Wv': jax.random.normal(ks[3], (HID, HID), dtype=jnp.float32) * sc, 'bv': jnp.zeros((HID,), dtype=jnp.float32), 'Wo': jax.random.normal(ks[4], (HID, HID), dtype=jnp.float32) * sc, 'bo': jnp.zeros((HID,), dtype=jnp.float32), 'slopes': jnp.asarray(_get_slopes(H))}
    _L0_attn_all = _L0_attn_setup()
    _L0_attn_in = {k: v for k, v in _L0_attn_all.items() if k in ('Wq', 'bq', 'Wk', 'bk', 'Wv', 'bv', 'Wo', 'bo', 'slopes')}
    del _L0_attn_all

    def _L0_xattn_setup():
        import jax, jax.numpy as jnp
        import numpy as np
        D_MODEL = 128
        N_HEADS = 16
        HEAD_DIM = D_MODEL // N_HEADS
        key = jax.random.key(seed)
        ks = jax.random.split(key, 12)
        B, S = (2, 256)
        s = 1.0 / np.sqrt(D_MODEL)
        return {'Q': jax.random.normal(ks[0], (B, S, D_MODEL), jnp.float32), 'K': jax.random.normal(ks[1], (B, S, D_MODEL), jnp.float32), 'V': jax.random.normal(ks[2], (B, S, D_MODEL), jnp.float32), 'mask': jnp.zeros((1, 1, S, S), jnp.float32), 'Wq': jax.random.normal(ks[3], (D_MODEL, D_MODEL), jnp.float32) * s, 'bq': jnp.zeros((D_MODEL,), jnp.float32), 'Wk': jax.random.normal(ks[4], (D_MODEL, D_MODEL), jnp.float32) * s, 'bk': jnp.zeros((D_MODEL,), jnp.float32), 'Wv': jax.random.normal(ks[5], (D_MODEL, D_MODEL), jnp.float32) * s, 'bv': jnp.zeros((D_MODEL,), jnp.float32), 'Wo': jax.random.normal(ks[6], (D_MODEL, D_MODEL), jnp.float32) * s, 'bo': jnp.zeros((D_MODEL,), jnp.float32)}
    _L0_xattn_all = _L0_xattn_setup()
    _L0_xattn_in = {k: v for k, v in _L0_xattn_all.items() if k in ('Wq', 'bq', 'Wk', 'bk', 'Wv', 'bv', 'Wo', 'bo')}
    del _L0_xattn_all

    def _L0_ffn_setup():
        import jax, jax.numpy as jnp
        import numpy as np
        D_MODEL = 128
        D_FF = 512
        N_EXPERTS = 8
        TOP_K = 2

        def _ffn(x, w1, b1, w2, b2):
            h = jax.nn.gelu(x @ w1.T + b1)
            return h @ w2.T + b2
        key = jax.random.key(seed)
        ks = jax.random.split(key, 12)
        s = 0.02
        x = jax.random.normal(ks[0], (4, 256, D_MODEL), dtype=jnp.float32)
        shared_w1 = jax.random.normal(ks[1], (D_FF, D_MODEL), dtype=jnp.float32) * s
        shared_b1 = jnp.zeros((D_FF,), dtype=jnp.float32)
        shared_w2 = jax.random.normal(ks[2], (D_MODEL, D_FF), dtype=jnp.float32) * s
        shared_b2 = jnp.zeros((D_MODEL,), dtype=jnp.float32)
        router_w = jax.random.normal(ks[3], (N_EXPERTS, D_MODEL), dtype=jnp.float32) * s
        router_b = jnp.zeros((N_EXPERTS,), dtype=jnp.float32)
        spec_w1 = jax.random.normal(ks[4], (N_EXPERTS, D_FF, D_MODEL), dtype=jnp.float32) * s
        spec_b1 = jnp.zeros((N_EXPERTS, D_FF), dtype=jnp.float32)
        spec_w2 = jax.random.normal(ks[5], (N_EXPERTS, D_MODEL, D_FF), dtype=jnp.float32) * s
        spec_b2 = jnp.zeros((N_EXPERTS, D_MODEL), dtype=jnp.float32)
        return dict(x=x, shared_w1=shared_w1, shared_b1=shared_b1, shared_w2=shared_w2, shared_b2=shared_b2, router_w=router_w, router_b=router_b, spec_w1=spec_w1, spec_b1=spec_b1, spec_w2=spec_w2, spec_b2=spec_b2)
    _L0_ffn_all = _L0_ffn_setup()
    _L0_ffn_in = {k: v for k, v in _L0_ffn_all.items() if k in ('shared_w1', 'shared_b1', 'shared_w2', 'shared_b2', 'router_w', 'router_b', 'spec_w1', 'spec_b1', 'spec_w2', 'spec_b2')}
    del _L0_ffn_all
    return {'x': x, 'ctx_1024': ctx_1024, 'mask_1x1xSxS2_ff0': mask_1x1xSxS2_ff0, 'L0_attn_Wq': _L0_attn_in['Wq'], 'L0_attn_bq': _L0_attn_in['bq'], 'L0_attn_Wk': _L0_attn_in['Wk'], 'L0_attn_bk': _L0_attn_in['bk'], 'L0_attn_Wv': _L0_attn_in['Wv'], 'L0_attn_bv': _L0_attn_in['bv'], 'L0_attn_Wo': _L0_attn_in['Wo'], 'L0_attn_bo': _L0_attn_in['bo'], 'L0_attn_slopes': _L0_attn_in['slopes'], 'L0_xattn_Wq': _L0_xattn_in['Wq'], 'L0_xattn_bq': _L0_xattn_in['bq'], 'L0_xattn_Wk': _L0_xattn_in['Wk'], 'L0_xattn_bk': _L0_xattn_in['bk'], 'L0_xattn_Wv': _L0_xattn_in['Wv'], 'L0_xattn_bv': _L0_xattn_in['bv'], 'L0_xattn_Wo': _L0_xattn_in['Wo'], 'L0_xattn_bo': _L0_xattn_in['bo'], 'L0_ffn_shared_w1': _L0_ffn_in['shared_w1'], 'L0_ffn_shared_b1': _L0_ffn_in['shared_b1'], 'L0_ffn_shared_w2': _L0_ffn_in['shared_w2'], 'L0_ffn_shared_b2': _L0_ffn_in['shared_b2'], 'L0_ffn_router_w': _L0_ffn_in['router_w'], 'L0_ffn_router_b': _L0_ffn_in['router_b'], 'L0_ffn_spec_w1': _L0_ffn_in['spec_w1'], 'L0_ffn_spec_b1': _L0_ffn_in['spec_b1'], 'L0_ffn_spec_w2': _L0_ffn_in['spec_w2'], 'L0_ffn_spec_b2': _L0_ffn_in['spec_b2']}

def reference(x, ctx_1024, mask_1x1xSxS2_ff0, L0_attn_Wq, L0_attn_bq, L0_attn_Wk, L0_attn_bk, L0_attn_Wv, L0_attn_bv, L0_attn_Wo, L0_attn_bo, L0_attn_slopes, L0_xattn_Wq, L0_xattn_bq, L0_xattn_Wk, L0_xattn_bk, L0_xattn_Wv, L0_xattn_bv, L0_xattn_Wo, L0_xattn_bo, L0_ffn_shared_w1, L0_ffn_shared_b1, L0_ffn_shared_w2, L0_ffn_shared_b2, L0_ffn_router_w, L0_ffn_router_b, L0_ffn_spec_w1, L0_ffn_spec_b1, L0_ffn_spec_w2, L0_ffn_spec_b2):
    import jax
    import jax.numpy as jnp

    def _L0_attn_ref(x, Wq, bq, Wk, bk, Wv, bv, Wo, bo, slopes):
        import jax, jax.numpy as jnp
        import numpy as np
        import math
        B, S, HID, H = (2, 256, 128, 16)
        D = HID // H

        def _get_slopes(n):
            start = 2 ** (-2 ** (-(math.log2(n) - 3)))
            return np.array([start * 2 ** (-i) for i in range(n)], dtype=np.float32)
        b, s, hid = x.shape
        h = slopes.shape[0]
        d = hid // h
        q = (x @ Wq.T + bq).reshape(b, s, h, d).transpose(0, 2, 1, 3)
        k = (x @ Wk.T + bk).reshape(b, s, h, d).transpose(0, 2, 1, 3)
        v = (x @ Wv.T + bv).reshape(b, s, h, d).transpose(0, 2, 1, 3)
        scores = jnp.einsum('bhqd,bhkd->bhqk', q, k) / jnp.sqrt(jnp.float32(d))
        pos = jnp.arange(s)
        dist = (pos[None, :] - pos[:, None]).astype(x.dtype)
        scores = scores + slopes[None, :, None, None] * dist[None, None]
        attn = jax.nn.softmax(scores, axis=-1)
        ctx = jnp.einsum('bhqk,bhkd->bhqd', attn, v)
        ctx = ctx.transpose(0, 2, 1, 3).reshape(b, s, hid)
        return ctx @ Wo.T + bo

    def _L0_xattn_ref(Q, K, V, mask, Wq, bq, Wk, bk, Wv, bv, Wo, bo):
        import jax, jax.numpy as jnp
        import numpy as np
        D_MODEL = 128
        N_HEADS = 16
        HEAD_DIM = D_MODEL // N_HEADS
        B, Sq, _ = Q.shape
        Sk = K.shape[1]
        q = (Q @ Wq.T + bq).reshape(B, Sq, N_HEADS, HEAD_DIM).transpose(0, 2, 1, 3)
        k = (K @ Wk.T + bk).reshape(B, Sk, N_HEADS, HEAD_DIM).transpose(0, 2, 1, 3)
        v = (V @ Wv.T + bv).reshape(B, Sk, N_HEADS, HEAD_DIM).transpose(0, 2, 1, 3)
        scores = jnp.einsum('bhqd,bhkd->bhqk', q, k) / jnp.sqrt(jnp.asarray(HEAD_DIM, q.dtype))
        scores = scores + mask
        attn = jax.nn.softmax(scores, axis=-1)
        out = jnp.einsum('bhqk,bhkd->bhqd', attn, v)
        out = out.transpose(0, 2, 1, 3).reshape(B, Sq, D_MODEL)
        return out @ Wo.T + bo

    def _L0_ffn_ref(x, shared_w1, shared_b1, shared_w2, shared_b2, router_w, router_b, spec_w1, spec_b1, spec_w2, spec_b2):
        import jax, jax.numpy as jnp
        import numpy as np
        D_MODEL = 128
        D_FF = 512
        N_EXPERTS = 8
        TOP_K = 2

        def _ffn(x, w1, b1, w2, b2):
            h = jax.nn.gelu(x @ w1.T + b1)
            return h @ w2.T + b2
        B, T, D = x.shape
        xf = x.reshape(-1, D)
        U = xf.shape[0]
        logits = xf @ router_w.T + router_b
        routing = jax.nn.softmax(logits, axis=-1)
        sel_w, sel_idx = jax.lax.top_k(routing, TOP_K)
        sel_w = sel_w / sel_w.sum(axis=-1, keepdims=True)
        comb = jnp.zeros_like(routing).at[jnp.arange(U)[:, None], sel_idx].set(sel_w)
        shared_out = _ffn(xf, shared_w1, shared_b1, shared_w2, shared_b2)

        def body(acc, params):
            w1, b1, w2, b2, we = params
            return (acc + we[:, None] * _ffn(xf, w1, b1, w2, b2), None)
        acc0 = jnp.zeros_like(shared_out)
        acc, _ = jax.lax.scan(body, acc0, (spec_w1, spec_b1, spec_w2, spec_b2, comb.T))
        return (shared_out + acc).reshape(B, T, D)
    x = _layernorm(x + _L0_attn_ref(x, L0_attn_Wq, L0_attn_bq, L0_attn_Wk, L0_attn_bk, L0_attn_Wv, L0_attn_bv, L0_attn_Wo, L0_attn_bo, L0_attn_slopes), axis=-1)
    x = _layernorm(x + _L0_xattn_ref(x, ctx_1024, ctx_1024, mask_1x1xSxS2_ff0, L0_xattn_Wq, L0_xattn_bq, L0_xattn_Wk, L0_xattn_bk, L0_xattn_Wv, L0_xattn_bv, L0_xattn_Wo, L0_xattn_bo), axis=-1)
    x = _layernorm(x + _L0_ffn_ref(x, L0_ffn_shared_w1, L0_ffn_shared_b1, L0_ffn_shared_w2, L0_ffn_shared_b2, L0_ffn_router_w, L0_ffn_router_b, L0_ffn_spec_w1, L0_ffn_spec_b1, L0_ffn_spec_w2, L0_ffn_spec_b2), axis=-1)
    return x

_drawn_inputs = setup_inputs


def setup_inputs(seed=0):
    import zlib

    import numpy as np

    out = dict(_drawn_inputs(seed))
    spreads = {'L0_attn_bq': (0.0, 0.385),
     'L0_attn_bk': (0.0, 0.8),
     'L0_attn_bv': (0.0, 0.1),
     'L0_attn_bo': (0.0, 0.1),
     'L0_xattn_bq': (0.0, 0.331),
     'L0_xattn_bk': (0.0, 0.8),
     'L0_xattn_bv': (0.0, 0.1),
     'L0_xattn_bo': (0.0, 0.1),
     'L0_ffn_shared_b1': (0.0, 0.348),
     'L0_ffn_shared_b2': (0.0, 0.1),
     'L0_ffn_router_b': (0.0, 0.1),
     'L0_ffn_spec_b1': (0.0, 0.455),
     'L0_ffn_spec_b2': (0.0, 0.1)}
    factors = {}
    for name, (base, spread) in spreads.items():
        noise = np.random.default_rng([zlib.crc32(name.encode()), seed]).standard_normal(out[name].shape)
        drawn = base * np.exp(spread * noise) if base else spread * noise
        out[name] = jnp.asarray(drawn.astype(out[name].dtype))
    for name, factor in factors.items():
        out[name] = (out[name] * factor).astype(out[name].dtype)
    return out
```

```python
from contextlib import ExitStack

import numpy as np

import concourse.bass as bass
from concourse import mybir

ALU = mybir.AluOpType
ACT = mybir.ActivationFunctionType
AX = mybir.AxisListType
F32 = mybir.dt.float32
BF16 = mybir.dt.bfloat16
I32 = mybir.dt.int32

P = 128
B = 16
S = 56
TOK = B * S
NT = TOK // P
HALF = TOK // 2
H = 16
DH = P // H
PAIRS = H // 2
PQ = 2 * S
SK = 1500
KW = 125
KT = SK // KW
KC = 500
NKC = SK // KC
SKP = SK + 4
VC = DH + 1
VW = H * VC + 24
F = 512
FC = F // P
E = 8
NE = E + 1
EPS = 1e-5
SCALE = float(DH) ** -0.5
K_PART = (0, 1, 0, 1, 2, 0)
Q_PART = (0, 0, 1, 1, 0, 2)
ROWS = 16 * len(K_PART)
HEADROOM = 50.0
GUARD = 54.0


def shape_constants():
    part = np.arange(P)
    eye = np.eye(P, dtype=np.float32)
    head = (part[:, None] // DH == np.arange(H)[None]).astype(np.float32)
    head2 = (2 * (part % PAIRS) + part // (P // 2))[:, None] == np.arange(H)[None]
    dist = np.zeros((P, S), np.float32)
    for at in (0, 64):
        dist[at:at + S] = np.arange(S)[None] - np.arange(S)[:, None]
    own = np.zeros((P, H, DH), np.float32)
    for r in range(PQ):
        own[r, (r // S)::2] = 1
    sel = np.zeros((P, 2, 4, P), np.float32)
    for h in range(H):
        tile, block = (h // 3, h % 3) if h < 12 else (h - 12, 3)
        first = 32 * tile + VC * (block if block < 3 else 0)
        for d in range(DH):
            sel[first + d, 0, block, h * DH + d] = 1
            sel[first + DH, 1, block, h * DH + d] = 1
    down = np.tile(np.arange(E, 0, -1, dtype=np.float32), (P, 1))
    diag = np.zeros((P, 2, S), np.float32)
    for r in range(16):
        diag[r, r // DH] = 1
    parts = [("eye", eye), ("head", head), ("head2", head2.astype(np.float32)), ("dist", dist),
             ("own", own.reshape(P, -1)), ("sel", sel.reshape(P, -1)), ("down", down),
             ("diag", diag.reshape(P, -1))]
    at, where = 0, {}
    for name, a in parts:
        where[name] = (at, a.shape[1])
        at += a.shape[1]
    return np.concatenate([a for _, a in parts], 1).astype(np.float32), where


CONSTANTS, CONST_AT = shape_constants()
NCONST = CONSTANTS.shape[1]
BQ1, BK1, BV1, BQ2, BK2, BV2 = range(6)
ROW_BO1, ROW_BO2, ROW_RB, ROW_SL = 0, P, 2 * P, 2 * P + E
NROW = 2 * P + E + H
WQ1, WK1, WV1, WO1, WQ2, WK2, WV2, WO2 = range(8)
W1_AT, W2_AT, B1_AT = 0, F, 2 * F
NW = 2 * F + FC


def build(nc, x, x_t, ctx_t, mask, w_t, bias_cols, rows, router_t, experts, b2, constants, out):
    with ExitStack() as top:
        def sem(name):
            return top.enter_context(nc.semaphore(name))

        def tensors(stack):
            return lambda name, shape, dt=F32: stack.enter_context(nc.sbuf_tensor(name, shape, dt))

        sb = tensors(top)
        ps = top.enter_context(nc.psum_tensor("ps", [P, 8, 512], F32))
        const = sb("const", [P, NCONST])
        wts = sb("wts", [P, 8, P])
        bias = sb("bias", [P, 6])
        row = sb("row", [P, NROW])
        xn = sb("xn", [P, NT, P])
        xt = sb("xt", [P, TOK])
        att = sb("att", [P, TOK])
        eps = sb("eps", [P, 1])

        def c(name):
            at, n = CONST_AT[name]
            return const[:, at:at + n]

        eye = c("eye")
        sel = c("sel").rearrange("p (k j m) -> p k j m", k=2, j=4)

        consts_in = sem("consts_in")
        x_in = sem("x_in")
        ctx_in = [sem("ctx_in_even"), sem("ctx_in_odd")]
        expert_in = [sem(f"expert_in_{i}") for i in range(3)]

        ctx_buf = [sb(f"ctx_{u}", [P, SK]) for u in range(2)]

        def load_ctx(sp, b, u):
            sp.dma_start(ctx_buf[u][:, :], ctx_t[bass.ds(b, 1)].rearrange("a d k -> d (a k)"))\
              .then_inc(ctx_in[u], 16)

        def self_attention():
            with ExitStack() as st:
                sa = tensors(st)
                q = sa("q1", [P, TOK])
                k = sa("k1", [P, TOK])
                alibi = sa("alibi", [P, H, S])
                q_now = [sa(f"q_now1_{u}", [P, 2, 64]) for u in range(2)]
                x_now = [sa(f"x_now1_{u}", [P, 2, 2, S]) for u in range(2)]
                k_heads = [sa(f"k_heads_{u}", [P, 2, H, S]) for u in range(2)]
                sc = [sa(f"sc1_{u}", [P, H, S]) for u in range(2)]
                p_t = [sa(f"p_t_{u}", [PQ, PAIRS, P]) for u in range(2)]
                v_own = [sa(f"v_own_{u}", [PQ, 2, H, VC]) for u in range(2)]
                row_max = [sa(f"row_max1_{u}", [P, H]) for u in range(2)]
                inv = sa("inv1", [P, H])
                o = sa("o1", [P, P])

                projected = sem("projected1")
                qk_ready = sem("qk_ready1")
                pads_zero = sem("pads_zero1")
                alibi_ready = sem("alibi_ready")
                ones_ready = sem("ones_ready1")
                staged = sem("staged1")
                heads_ready = sem("heads_ready1")
                v_done = sem("v_done1")
                v_ready = sem("v_ready1")
                scores_done = sem("scores_done1")
                scores_biased = sem("scores_biased1")
                max_ready = sem("max_ready1")
                shifted = sem("shifted1")
                exp_done = sem("exp_done1")
                turned = sem("turned1")
                p_t_ready = sem("p_t_ready1")
                pv_done = sem("pv_done1")
                inv_ready = sem("inv_ready1")
                normed = sem("normed1")
                o_turned = sem("o_turned1")
                att_ready = sem("att_ready1")

                n_pairs = B // 2

                def sweep(front, back):
                    def run(eng):
                        front(0, 0)
                        front(1, 1)
                        back(0, 0)
                        with eng.Fori(0, n_pairs // 2 - 1) as i:
                            for u in range(2):
                                j = 2 * i + 2 + u
                                front(j, u)
                                back(j - 1, 1 - u)
                        back(n_pairs - 1, 1)
                    return run

                def later(j, n):
                    return not isinstance(j, int) or j >= n

                with nc.Block() as block:
                    @block.sync
                    def _(sp):
                        sp.dma_start(xt[:, :], x_t).then_inc(x_in, 16)
                        sp.dma_start(wts[:, :, :], w_t).then_inc(x_in, 16)
                        sp.dma_start(bias[:, :], bias_cols).then_inc(x_in, 16)
                        sp.dma_start(const[:, :], constants).then_inc(consts_in, 16)
                        sp.dma_start(row[:, :], rows).then_inc(consts_in, 16)
                        sp.dma_start(xn[:, :, :], x.rearrange("(t p) d -> p t d", p=P)).then_inc(consts_in, 16)
                        load_ctx(sp, 0, 0)
                        load_ctx(sp, 1, 1)

                    @block.gpsimd
                    def _(pool):
                        for u in range(2):
                            nc.gpsimd.memset(q_now[u][:, :, S:64], 0.0).then_inc(pads_zero, 1)
                        nc.gpsimd.memset(eps[:, :], EPS).then_inc(pads_zero, 1)
                        pool.wait_ge(qk_ready, 4)
                        pool.wait_ge(consts_in, 48)

                        def front(j, u):
                            if later(j, 2):
                                pool.wait_ge(scores_done, j - 1)
                                pool.wait_ge(v_done, j - 1)
                            nc.gpsimd.tensor_copy(x_now[u][:, :, 0, :],
                                                  xt[:, bass.ds(j * PQ, PQ)].rearrange("p (b s) -> p b s", b=2))
                            nc.gpsimd.tensor_copy(x_now[u][:, :, 1, :],
                                                  xt[:, bass.ds(j * PQ, PQ)].rearrange("p (b s) -> p b s", b=2))
                            nc.gpsimd.tensor_copy(q_now[u][:, :, 0:S],
                                                  q[:, bass.ds(j * PQ, PQ)].rearrange("p (b s) -> p b s", b=2))\
                                     .then_inc(staged, 1)
                            for b in range(2):
                                ks = k[:, bass.ds(j * PQ + b * S, S)]
                                nc.gpsimd.tensor_tensor(k_heads[u][:, b], ks.unsqueeze(1).to_broadcast([P, H, S]),
                                                        c("head").unsqueeze(2).to_broadcast([P, H, S]),
                                                        ALU.mult).then_inc(heads_ready, 1)

                        def back(j, u):
                            pass

                        sweep(front, back)(pool)

                    @block.tensor
                    def _(pe):
                        pe.wait_ge(x_in, 48)
                        for n, w in enumerate((WQ1, WK1)):
                            for a in range(2):
                                nc.tensor.matmul(ps[:, 2 * n + a, 0:HALF], wts[:, w, :],
                                                 xt[:, a * HALF:(a + 1) * HALF],
                                                 start=True, stop=True).then_inc(projected, 1)
                        pe.wait_ge(pads_zero, 3)
                        pe.wait_ge(consts_in, 48)
                        pe.wait_ge(qk_ready, 4)

                        def front(j, u):
                            pe.wait_ge(staged, j + 1)
                            if later(j, 1):
                                pe.wait_ge(v_ready, j)
                            for b in range(2):
                                last = nc.tensor.matmul(ps[0:PQ, 6, b * P:(b + 1) * P],
                                                        x_now[u][:, b].rearrange("p r s -> p (r s)"),
                                                        wts[:, WV1, :], start=True, stop=True)
                            last.then_inc(v_done, 1)
                            pe.wait_ge(heads_ready, 2 * j + 2)
                            if later(j, 2):
                                pe.wait_ge(scores_biased, j - 1)
                            for a in range(2):
                                for b in range(2):
                                    last = nc.tensor.matmul(
                                        ps[64 * b:64 * b + 64, 2 * u + a, 0:HALF], q_now[u][:, b, :],
                                        k_heads[u][:, b, a * 8:a * 8 + 8, :].rearrange("p h s -> p (h s)"),
                                        start=True, stop=True)
                            last.then_inc(scores_done, 1)

                        def back(j, u):
                            pe.wait_ge(exp_done, j + 1)
                            if later(j, 1):
                                pe.wait_ge(p_t_ready, j)
                            for p in range(PAIRS):
                                last = nc.tensor.transpose(
                                    ps[0:PQ, 4 + p // 4, (p % 4) * P:(p % 4 + 1) * P],
                                    sc[u][:, 2 * p:2 * p + 2, :].rearrange("p h s -> p (h s)"), eye)
                            last.then_inc(turned, 1)
                            pe.wait_ge(p_t_ready, j + 1)
                            pe.wait_ge(v_ready, j + 1)
                            if later(j, 1):
                                pe.wait_ge(att_ready, j)
                            for p in range(PAIRS):
                                for b in range(2):
                                    last = nc.tensor.matmul(
                                        ps[64 * b:64 * b + 64, 7, 2 * VC * p:2 * VC * (p + 1)],
                                        p_t[u][:, p, 64 * b:64 * b + 64],
                                        v_own[u][:, b, 2 * p:2 * p + 2, :].rearrange("p h e -> p (h e)"),
                                        start=True, stop=True)
                            last.then_inc(pv_done, 1)
                            pe.wait_ge(normed, j + 1)
                            nc.tensor.transpose(ps[:, 7, 256:384], o[:, :], eye).then_inc(o_turned, 1)

                        sweep(front, back)(pe)

                    @block.scalar
                    def _(act):
                        def exp(j, u):
                            act.wait_ge(shifted, j + 1)
                            nc.scalar.activation(sc[u][:, :, :], sc[u][:, :, :], ACT.Exp).then_inc(exp_done, 1)

                        def copy(j, u):
                            act.wait_ge(turned, j + 1)
                            if later(j, 2):
                                act.wait_ge(pv_done, j - 1)
                            nc.scalar.copy(p_t[u][:, :, :].rearrange("p (a n) m -> p a (n m)", a=2),
                                           ps[0:PQ, 4:6, :]).then_inc(p_t_ready, 1)

                        exp(0, 0)
                        exp(1, 1)
                        copy(0, 0)
                        copy(1, 1)
                        with act.Fori(0, n_pairs // 2 - 1) as i:
                            for u in range(2):
                                j = 2 * i + 2 + u
                                exp(j, u)
                                copy(j, u)

                    @block.vector
                    def _(dve):
                        dve.wait_ge(x_in, 48)
                        dve.wait_ge(consts_in, 48)
                        for a in range(2):
                            dve.wait_ge(projected, a + 1)
                            nc.vector.tensor_scalar(q[:, a * HALF:(a + 1) * HALF], ps[:, a, 0:HALF],
                                                    bias[:, BQ1:BQ1 + 1], SCALE, ALU.add, ALU.mult)\
                                     .then_inc(qk_ready, 1)
                        for a in range(2):
                            dve.wait_ge(projected, a + 3)
                            nc.vector.tensor_scalar(k[:, a * HALF:(a + 1) * HALF], ps[:, 2 + a, 0:HALF],
                                                    bias[:, BK1:BK1 + 1], None, ALU.add).then_inc(qk_ready, 1)
                        nc.vector.tensor_tensor(alibi[:, :, :], c("dist").unsqueeze(1).to_broadcast([P, H, S]),
                                                row[:, ROW_SL:ROW_SL + H].unsqueeze(2).to_broadcast([P, H, S]),
                                                ALU.mult).then_inc(alibi_ready, 1)
                        own = c("own").rearrange("p (h d) -> p h d", d=DH)
                        for u in range(2):
                            for b in range(2):
                                nc.vector.tensor_copy(v_own[u][:, b, :, DH:VC], own[0:PQ, :, 0:1])\
                                         .then_inc(ones_ready, 1)
                        dve.wait_ge(ones_ready, 4)
                        dve.wait_ge(alibi_ready, 1)

                        def front(j, u):
                            dve.wait_ge(v_done, j + 1)
                            if later(j, 2):
                                dve.wait_ge(pv_done, j - 1)
                            for b in range(2):
                                last = nc.vector.tensor_tensor(
                                    v_own[u][:, b, :, 0:DH],
                                    ps[0:PQ, 6, b * P:(b + 1) * P].rearrange("p (h d) -> p h d", d=DH),
                                    own[0:PQ], ALU.mult)
                            last.then_inc(v_ready, 1)
                            dve.wait_ge(scores_done, j + 1)
                            if later(j, 2):
                                dve.wait_ge(turned, j - 1)
                            nc.vector.tensor_tensor(
                                sc[u][:, :, :].rearrange("p (a h) s -> p a (h s)", a=2),
                                ps[:, 2 * u:2 * u + 2, 0:HALF],
                                alibi[:, :, :].rearrange("p (a h) s -> p a (h s)", a=2), ALU.add)\
                                     .then_inc(scores_biased, 1)
                            dve.wait_ge(scores_biased, j + 1)
                            nc.vector.tensor_reduce(row_max[u][:, :], sc[u][:, :, :], AX.X, ALU.max)\
                                     .then_inc(max_ready, 1)
                            dve.wait_ge(max_ready, j + 1)
                            nc.vector.tensor_tensor(sc[u][:, :, :], sc[u][:, :, :],
                                                    row_max[u][:, :].unsqueeze(2).to_broadcast([P, H, S]),
                                                    ALU.subtract).then_inc(shifted, 1)

                        def back(j, u):
                            dve.wait_ge(pv_done, j + 1)
                            pv = ps[:, 7, 0:H * VC].rearrange("p (h e) -> p h e", e=VC)
                            nc.vector.reciprocal(inv[:, :].unsqueeze(2), pv[:, :, DH:VC]).then_inc(inv_ready, 1)
                            dve.wait_ge(inv_ready, j + 1)
                            if later(j, 1):
                                dve.wait_ge(o_turned, j)
                            nc.vector.tensor_tensor(o[:, :].rearrange("p (h d) -> p h d", d=DH), pv[:, :, 0:DH],
                                                    inv[:, :].unsqueeze(2).to_broadcast([P, H, DH]),
                                                    ALU.mult).then_inc(normed, 1)
                            dve.wait_ge(o_turned, j + 1)
                            nc.vector.tensor_scalar(
                                att[:, bass.ds(j * PQ, PQ)].rearrange("p (b s) -> p b s", b=2),
                                ps[:, 7, 256:384].rearrange("p (b s) -> p b s", b=2)[:, :, 0:S],
                                bias[:, BV1:BV1 + 1], None, ALU.add).then_inc(att_ready, 1)

                        sweep(front, back)(dve)

        def normalise(dve, act_done, named, y, target):
            stats, mv, rstd = named["stats"], named["mv"], named["rstd"]
            for t in range(NT):
                dve.wait_ge(named["y_ready"], 1 if t < 4 else 2)
                nc.vector.bn_stats(stats[:, t, :], y[:, t, :]).then_inc(named["stats_ready"], 1)
            for t in range(NT):
                dve.wait_ge(named["stats_ready"], t + 1)
                nc.vector.bn_aggr(mv[:, t, :], stats[:, t, :]).then_inc(named["mv_ready"], 1)
            dve.wait_ge(named["std_ready"], 1)
            nc.vector.reciprocal(rstd[:, :], named["std"][:, :]).then_inc(named["rstd_ready"], 1)
            dve.wait_ge(named["rstd_ready"], 1)
            for t in range(NT):
                nc.vector.tensor_scalar(target[:, t, :], y[:, t, :], mv[:, t, 0:1], rstd[:, t:t + 1],
                                        ALU.subtract, ALU.mult).then_inc(named["normal_ready"], 1)

        def deviation(act, named):
            act.wait_ge(named["mv_ready"], NT)
            nc.scalar.activation(named["std"][:, :], named["mv"][:, :, 1], ACT.Sqrt, bias=eps[:, 0:1])\
                     .then_inc(named["std_ready"], 1)

        def norm_names(tag, sx):
            named = {n: sem(f"{n}_{tag}") for n in
                     ("y_ready", "stats_ready", "mv_ready", "std_ready", "rstd_ready", "normal_ready")}
            named["stats"] = sx(f"stats_{tag}", [P, NT, 6])
            named["mv"] = sx(f"mv_{tag}", [P, NT, 2])
            named["std"] = sx(f"std_{tag}", [P, NT])
            named["rstd"] = sx(f"rstd_{tag}", [P, NT])
            return named

        def project_and_norm(tag, w, bo_at):
            with ExitStack() as st:
                sx = tensors(st)
                y = sx(f"y_{tag}", [P, NT, P])
                named = norm_names(tag, sx)
                with_bias = sem(f"with_bias_{tag}")
                product = sem(f"product_{tag}")
                turned = sem(f"turned_{tag}")
                xt_ready = sem(f"xt_ready_{tag}")
                with nc.Block() as block:
                    @block.gpsimd
                    def _(pool):
                        nc.gpsimd.tensor_tensor(xn[:, :, :], xn[:, :, :],
                                                row[:, bo_at:bo_at + P].unsqueeze(1).to_broadcast([P, NT, P]),
                                                ALU.add).then_inc(with_bias, 1)

                    @block.tensor
                    def _(pe):
                        for t in range(NT):
                            last = nc.tensor.matmul(ps[:, t // 4, (t % 4) * P:(t % 4 + 1) * P],
                                                    att[:, t * P:(t + 1) * P], wts[:, w, :],
                                                    start=True, stop=True)
                            if t in (3, NT - 1):
                                last.then_inc(product, 1)
                        for t in range(NT):
                            pe.wait_ge(named["normal_ready"], t + 1)
                            last = nc.tensor.transpose(ps[:, 2 + t // 4, (t % 4) * P:(t % 4 + 1) * P],
                                                       xn[:, t, :], eye)
                            if t in (3, NT - 1):
                                last.then_inc(turned, 1)

                    @block.scalar
                    def _(act):
                        deviation(act, named)
                        for n, (a, z) in enumerate(((0, 4), (4, NT))):
                            act.wait_ge(turned, n + 1)
                            nc.scalar.copy(xt[:, a * P:z * P], ps[:, 2 + n, 0:(z - a) * P]).then_inc(xt_ready, 1)

                    @block.vector
                    def _(dve):
                        dve.wait_ge(with_bias, 1)
                        for n, (a, z) in enumerate(((0, 4), (4, NT))):
                            dve.wait_ge(product, n + 1)
                            nc.vector.tensor_tensor(y[:, a:z, :], ps[:, n, 0:(z - a) * P].rearrange("p (t d) -> p t d", d=P),
                                                    xn[:, a:z, :], ALU.add).then_inc(named["y_ready"], 1)
                        normalise(dve, None, named, y, xn)

        def cross_attention(top_b):
            sx = tensors(top_b)
            q_stack = sx("q_stack", [ROWS, PAIRS, B * PQ], BF16)
            k_part = [sx(f"k_part_{u}", [P, 3, SKP], BF16) for u in range(2)]
            k_stack = [sx(f"k_stack_{u}", [ROWS, PAIRS, SKP], BF16) for u in range(2)]
            values = [sx(f"values_{u}", [P, KT, VW]) for u in range(2)]
            k_rest = sx("k_rest", [P, KC])
            k_max = [sx(f"k_max_{u}", [P, 1]) for u in range(2)]
            q_max = sx("q_max", [P, B])
            terms = sx("terms", [P, H])
            bound = sx("bound", [P, 1])
            worst = sx("worst", [P, 1])
            shift = [sx(f"shift_{u}", [P, 1]) for u in range(2)]
            ones = sx("ones", [P, P])
            mask_max = sx("mask_max", [P, 1])
            flag = sx("flag", [P, 1], I32)

            def k_matmul(pe, u, n, bank):
                return nc.tensor.matmul(ps[:, bank, 0:KC], wts[:, WK2, :], ctx_buf[u][:, n * KC:(n + 1) * KC],
                                        start=True, stop=True)

            def v_matmul(pe, u, n, bank):
                for i in range(4):
                    t = 4 * n + i
                    last = nc.tensor.matmul(ps[0:KW, bank, i * P:(i + 1) * P],
                                            ctx_buf[u][:, t * KW:(t + 1) * KW], wts[:, WV2, :],
                                            start=True, stop=True)
                return last

            def v_evacuate(u, n, bank):
                return nc.vector.tensor_copy(
                    values[u][0:KW, 4 * n:4 * n + 4, 0:H * VC].rearrange("p t (h e) -> p t h e", e=VC)[:, :, :, 0:DH],
                    ps[0:KW, bank, :].rearrange("p (t h d) -> p t h d", t=4, d=DH))

            def k_split(dve, u, n, bank, count, names):
                hi_ready, rest_ready, mid_ready, bank_read, parts_ready = names
                cols = slice(n * KC, (n + 1) * KC)
                nc.vector.tensor_scalar(k_part[u][:, 0, cols], ps[:, bank, 0:KC], bias[:, BK2:BK2 + 1], None,
                                        ALU.add).then_inc(hi_ready, 1)
                dve.wait_ge(hi_ready, count + 1)
                nc.vector.scalar_tensor_tensor(out=k_rest[:, :], in0=ps[:, bank, 0:KC],
                                               scalar=bias[:, BK2:BK2 + 1], in1=k_part[u][:, 0, cols],
                                               op0=ALU.add, op1=ALU.subtract).then_inc(rest_ready, 1)
                dve.wait_ge(rest_ready, count + 1)
                nc.vector.tensor_copy(k_part[u][:, 1, cols], k_rest[:, :]).then_inc(mid_ready, 1)
                dve.wait_ge(mid_ready, count + 1)
                nc.vector.tensor_tensor(k_part[u][:, 2, cols], k_rest[:, :], k_part[u][:, 1, cols],
                                        ALU.subtract).then_inc(parts_ready, 1)

            with ExitStack() as st:
                sq = tensors(st)
                q = sq("q2", [P, TOK])
                rest = sq("q_rest", [P, TOK])
                q_part = sq("q_part", [P, 3, TOK], BF16)
                q_wide = sq("q_wide", [P, 3, B, 2, S], BF16)
                mask_sb = sq("mask_rows", [PQ, SK])
                mask_in = sem("mask_in")
                projected = sem("projected2")
                q_ready = sem("q_ready2")
                hi_ready = sem("q_hi_ready")
                rest_ready = sem("q_rest_ready")
                mid_ready = sem("q_mid_ready")
                lo_ready = sem("q_lo_ready")
                spread_d = sem("q_spread_vector")
                zeroed = sem("q_wide_zero")
                stack_in = sem("q_stack_in")
                pads = sem("pads_ready2")
                mask_done = sem("mask_max_ready")
                with nc.Block() as block:
                    @block.sync
                    def _(sp):
                        sp.dma_start(mask_sb[:, :], mask).then_inc(mask_in, 16)
                        sp.wait_ge(zeroed, 1)
                        sp.wait_ge(spread_d, 6)
                        for n, part in enumerate(Q_PART):
                            sp.dma_start(q_stack[16 * n:16 * n + 16, :, :],
                                         q_wide[:, part].rearrange("p b h s -> p (b h s)")).then_inc(stack_in, 16)
                        sp.wait_ge(stack_in, 16 * len(Q_PART))

                    @block.tensor
                    def _(pe):
                        for a in range(2):
                            nc.tensor.matmul(ps[:, a, 0:HALF], wts[:, WQ2, :], xt[:, a * HALF:(a + 1) * HALF],
                                             start=True, stop=True).then_inc(projected, 1)

                    @block.gpsimd
                    def _(pool):
                        nc.gpsimd.memset(q_wide[:, :, :, :, :].rearrange("p a b h s -> p (a b h s)"), 0.0)\
                                 .then_inc(zeroed, 1)
                        for u in range(2):
                            nc.gpsimd.memset(k_part[u][:, :, SK:SKP], 0.0).then_inc(pads, 1)
                            nc.gpsimd.memset(values[u][:, :, H * VC:VW], 0.0).then_inc(pads, 1)
                            nc.gpsimd.memset(values[u][:, :, 0:H * VC].rearrange("p t (h e) -> p t h e", e=VC)[:, :, :, DH:VC],
                                             1.0).then_inc(pads, 1)
                        nc.gpsimd.memset(ones[:, :], 1.0).then_inc(pads, 1)
                        nc.gpsimd.memset(worst[:, :], 0.0).then_inc(pads, 1)

                    @block.vector
                    def _(dve):
                        halves = [slice(a * HALF, (a + 1) * HALF) for a in range(2)]
                        for a in range(2):
                            dve.wait_ge(projected, a + 1)
                            nc.vector.tensor_scalar(q[:, halves[a]], ps[:, a, 0:HALF], bias[:, BQ2:BQ2 + 1], SCALE,
                                                    ALU.add, ALU.mult).then_inc(q_ready, 1)
                        dve.wait_ge(q_ready, 2)
                        nc.vector.tensor_copy(q_part[:, 0, :], q[:, :]).then_inc(hi_ready, 1)
                        dve.wait_ge(hi_ready, 1)
                        nc.vector.tensor_tensor(rest[:, :], q[:, :], q_part[:, 0, :], ALU.subtract)\
                                 .then_inc(rest_ready, 1)
                        dve.wait_ge(rest_ready, 1)
                        nc.vector.tensor_copy(q_part[:, 1, :], rest[:, :]).then_inc(mid_ready, 1)
                        dve.wait_ge(mid_ready, 1)
                        nc.vector.tensor_tensor(q_part[:, 2, :], rest[:, :], q_part[:, 1, :], ALU.subtract)\
                                 .then_inc(lo_ready, 1)
                        dve.wait_ge(lo_ready, 1)
                        dve.wait_ge(zeroed, 1)
                        for part in range(3):
                            for h in range(2):
                                rows_ = slice(64 * h, 64 * h + 64)
                                nc.vector.tensor_copy(q_wide[rows_, part, :, h, :],
                                                      q_part[rows_, part, :].rearrange("p (b s) -> p b s", s=S))\
                                         .then_inc(spread_d, 1)
                        nc.vector.tensor_reduce(q_max[:, :], q[:, :].rearrange("p (b s) -> p b s", s=S), AX.X,
                                                ALU.max, apply_absolute_value=True).then_inc(mask_done, 1)
                        dve.wait_ge(mask_in, 16)
                        dve.wait_ge(pads, 8)
                        nc.vector.memset(mask_max[:, :], 0.0).then_inc(mask_done, 1)
                        dve.wait_ge(mask_done, 2)
                        nc.vector.tensor_reduce(mask_max[0:PQ, :], mask_sb[:, :], AX.X, ALU.max,
                                                apply_absolute_value=True).then_inc(mask_done, 1)

            with ExitStack() as st:
                sp_ = tensors(st)
                q_now = [sp_(f"q_now2_{u}", [ROWS, PAIRS, PQ], BF16) for u in range(2)]
                probs = [sp_(f"probs_{r}", [P, 2, HALF]) for r in range(3)]
                outs = sp_("outs", [P, 4, B, S])
                inv = sp_("inv2", [P, TOK])
                num = sp_("num2", [P, TOK])

                kstack_in = [sem("kstack_in_even"), sem("kstack_in_odd")]
                q_now_ready = sem("q_now_ready")
                proj_done = sem("proj_done")
                bank_read = sem("proj_bank_free")
                k_hi = sem("k_hi_ready")
                k_restr = sem("k_rest_ready")
                k_mid = sem("k_mid_ready")
                k_ready = sem("k_parts_ready")
                v_ready = sem("values_ready")
                kmax_ready = sem("k_max_ready")
                terms_ready = sem("terms_ready")
                bound_done = sem("bound_done")
                bound_ready = sem("bound_read")
                worst_ready = sem("worst_ready")
                shift_ready = sem("shift_ready")
                scores_done = sem("scores_done2")
                exp_done = sem("exp_done2")
                probs_free = sem("probs_free")
                pv_done = sem("pv_done2")
                out_free = sem("out_bank_free")
                summed = sem("heads_gathered")
                inv_ready = sem("inv_ready2")
                num_ready = sem("num_ready2")
                prod_ready = sem("prod_ready2")
                att_ready = sem("att_ready2")
                k_names = (k_hi, k_restr, k_mid, bank_read, k_ready)

                LOOP = B - 4

                def batches(eng, body):
                    with eng.Fori(0, LOOP // 2) as i:
                        for u in range(2):
                            body(2 * i + u, u, i, True, True, True)
                    for b in range(LOOP, B):
                        body(b, b % 2, b // 2, b + 3 < B, b + 2 < B, b + 1 < B)

                with nc.Block() as block:
                    @block.sync
                    def _(sp):
                        def kstack(u):
                            for n, part in enumerate(K_PART):
                                sp.dma_start(k_stack[u][16 * n:16 * n + 16, :, :], k_part[u][:, part, :])\
                                  .then_inc(kstack_in[u], 16)

                        for b in range(2):
                            sp.wait_ge(k_ready, 3 * (b + 1))
                            kstack(b)
                        sp.wait_ge(proj_done, 9)
                        load_ctx(sp, 2, 0)

                        def held(value):
                            return value if isinstance(value, int) else sp.snap(value)

                        def body(b, u, i, load, k_next, v_next):
                            third = held(b + 3)
                            values_made = held(6 * b + 12)
                            parts_made = held(3 * b + 9)
                            batch_scored = held(KT * b + KT)
                            if load:
                                sp.wait_ge(proj_done, values_made)
                                load_ctx(sp, third, 1 - u)
                            if k_next:
                                sp.wait_ge(k_ready, parts_made)
                                sp.wait_ge(scores_done, batch_scored)
                                kstack(u)
                        batches(sp, body)

                    @block.gpsimd
                    def _(pool):
                        def take(b, u):
                            nc.gpsimd.tensor_copy(q_now[u][:, :, :], q_stack[:, :, bass.ds(b * PQ, PQ)])\
                                     .then_inc(q_now_ready, 1)
                        take(0, 0)
                        take(1, 1)
                        with pool.Fori(0, B // 2 - 1) as i:
                            for u in range(2):
                                pool.wait_ge(scores_done, KT * (2 * i + 1 + u))
                                take(2 * i + 2 + u, u)

                    @block.tensor
                    def _(pe):
                        def scores(u, t):
                            for p in range(PAIRS):
                                last = nc.tensor.matmul(
                                    ps[:, 2 * (t % 2) + p // 4, (p % 4) * PQ:(p % 4 + 1) * PQ],
                                    k_stack[u][:, p, t * KW:t * KW + P], q_now[u][:, p, :],
                                    start=True, stop=True)
                            last.then_inc(scores_done, 1)

                        def product(b, u, t):
                            r = t % 3
                            flat = probs[r][0:KW].rearrange("p a n -> p (a n)")
                            for n in range(8):
                                g = n % 4
                                h, w, at = (3 * g, 3 * S, 0) if n < 4 else (12 + g, S, 3 * S)
                                last = nc.tensor.matmul(
                                    ps[32 * g:32 * g + 32, 4 + u, at:at + w],
                                    values[u][0:KW, t, VC * h:VC * h + 32], flat[:, h * S:h * S + w],
                                    start=(t == 0 and n < 4), stop=(t == KT - 1), skip_group_check=True)
                            last.then_inc(probs_free, 1)
                            return last

                        def unit(kind, u, n, m, bank):
                            pe.wait_ge(bank_read, m + 1)
                            last = (k_matmul if kind == "k" else v_matmul)(pe, u, n, bank)
                            last.then_inc(proj_done, 1)

                        pe.sem_inc(probs_free, 3)
                        for b in range(2):
                            pe.wait_ge(ctx_in[b], 16)
                            for n in range(3):
                                unit("k", b, n, 3 * b + n, 6 + (3 * b + n) % 2)
                        for n in range(3):
                            unit("v", 0, n, 6 + n, 6 + n % 2)
                        pe.wait_ge(out_free, 2)
                        pe.wait_ge(terms_ready, 1)
                        nc.tensor.matmul(ps[:, 4, 256:256 + H], ones[:, :], terms[:, :],
                                         start=True, stop=True).then_inc(bound_done, 1)
                        pe.wait_ge(kstack_in[0], 16 * len(K_PART))
                        pe.wait_ge(q_now_ready, 1)
                        scores(0, 0)
                        scores(0, 1)

                        def body(b, u, i, load, k_next, v_next):
                            for t in range(KT):
                                if t == 0:
                                    pe.wait_ge(v_ready, 3 * b + 3)
                                    pe.wait_ge(out_free, b + 1)
                                pe.wait_ge(exp_done, KT * b + t + 1)
                                product(b, u, t)
                                if t + 2 < KT:
                                    scores(u, t + 2)
                                elif v_next:
                                    if t + 2 == KT:
                                        pe.wait_ge(kstack_in[1 - u],
                                                   16 * len(K_PART) * (i + u + 1))
                                        pe.wait_ge(q_now_ready, b + 2)
                                    scores(1 - u, t + 2 - KT)
                                if v_next and t in (1, 2, 3):
                                    unit("v", 1 - u, t - 1, 6 * b + 9 + t - 1, 6 + t % 2)
                                if v_next and t == 4:
                                    pe.wait_ge(out_free, b + 2)
                                    pe.wait_ge(terms_ready, b + 2)
                                    nc.tensor.matmul(ps[:, 5 - u, 256:256 + H], ones[:, :], terms[:, :],
                                                     start=True, stop=True).then_inc(bound_done, 1)
                                if k_next and t in (5, 6, 7):
                                    if t == 5:
                                        pe.wait_ge(ctx_in[u], 16 * (i + 2))
                                    unit("k", u, t - 5, 6 * b + 12 + t - 5, 6 + (t - 1) % 2)
                        batches(pe, body)

                        pe.wait_ge(out_free, B + 2)
                        for kind in range(2):
                            for a in range(2):
                                for j in range(4):
                                    last = nc.tensor.matmul(
                                        ps[:, 2 * kind + a, 0:HALF], sel[:, kind, j, :],
                                        outs[:, j, 8 * a:8 * a + 8, :].rearrange("p b s -> p (b s)"),
                                        start=(j == 0), stop=(j == 3))
                                last.then_inc(summed, 1)

                    @block.scalar
                    def _(act):
                        def body(b, u, i, load, k_next, v_next):
                            for t in range(KT):
                                if t == 0:
                                    act.wait_ge(shift_ready, b + 1)
                                act.wait_ge(scores_done, KT * b + t + 1)
                                act.wait_ge(probs_free, KT * b + t + 1)
                                s = 2 * (t % 2)
                                nc.scalar.activation(probs[t % 3][:, :, :], ps[:, s:s + 2, 0:HALF], ACT.Exp,
                                                     bias=shift[u][:, 0:1]).then_inc(exp_done, 1)
                        batches(act, body)

                    @block.vector
                    def _(dve):
                        def k_unit(u, n, m, count, bank):
                            dve.wait_ge(proj_done, m + 1)
                            k_split(dve, u, n, bank, count, k_names)
                            dve.sem_inc(bank_read, 1)

                        def largest_k(b, u):
                            dve.wait_ge(k_ready, 3 * b + 3)
                            nc.vector.tensor_reduce(k_max[u][:, :], k_part[u][:, 0, 0:SK], AX.X, ALU.max,
                                                    apply_absolute_value=True).then_inc(kmax_ready, 1)

                        def bound_terms(b, u):
                            dve.wait_ge(kmax_ready, b + 1)
                            nc.vector.tensor_scalar(terms[:, :], c("head2"), k_max[u][:, 0:1],
                                                    q_max[:, bass.ds(b, 1)], ALU.mult, ALU.mult)\
                                     .then_inc(terms_ready, 1)

                        def take_bound(b, u):
                            dve.wait_ge(bound_done, b + 1)
                            nc.vector.tensor_reduce(bound[:, :], ps[:, 4 + u, 256:256 + H], AX.X, ALU.max)\
                                     .then_inc(bound_ready, 1)
                            dve.wait_ge(bound_ready, b + 1)
                            nc.vector.tensor_tensor(worst[:, :], worst[:, :], bound[:, :], ALU.max)\
                                     .then_inc(worst_ready, 1)
                            nc.vector.tensor_scalar(shift[u][:, :], bound[:, :], -1.01, HEADROOM, ALU.mult, ALU.add)\
                                     .then_inc(shift_ready, 1)

                        def evacuate(b, u):
                            dve.wait_ge(probs_free, KT * b + KT + 3)
                            nc.vector.tensor_copy(outs[:, :, bass.ds(b, 1), :].rearrange("p j b s -> p j (b s)"),
                                                  ps[:, 4 + u, 0:4 * S].rearrange("p (j s) -> p j s", s=S))\
                                     .then_inc(out_free, 1)
                        dve.sem_inc(bank_read, 2)
                        dve.sem_inc(out_free, 2)
                        for b in range(2):
                            for n in range(3):
                                k_unit(b, n, 3 * b + n, 3 * b + n, 6 + (3 * b + n) % 2)
                            largest_k(b, b)
                        for n in range(3):
                            dve.wait_ge(proj_done, 7 + n)
                            v_evacuate(0, n, 6 + n % 2).then_inc(v_ready, 1)
                            dve.wait_ge(v_ready, n + 1)
                            dve.sem_inc(bank_read, 1)
                        bound_terms(0, 0)
                        take_bound(0, 0)

                        def body(b, u, i, load, k_next, v_next, first=False):
                            if not first:
                                evacuate(b - 1, 1 - u)
                            if v_next:
                                bound_terms(b + 1, 1 - u)
                                for n in range(3):
                                    dve.wait_ge(proj_done, 6 * b + 10 + n)
                                    v_evacuate(1 - u, n, 6 + (n + 1) % 2).then_inc(v_ready, 1)
                                    dve.wait_ge(v_ready, 3 * b + 4 + n)
                                    dve.sem_inc(bank_read, 1)
                                take_bound(b + 1, 1 - u)
                            if k_next:
                                for n in range(3):
                                    if n == 0:
                                        dve.wait_ge(kstack_in[u], 16 * len(K_PART) * (i + 1))
                                    k_unit(u, n, 6 * b + 12 + n, 3 * b + 6 + n, 6 + n % 2)
                                largest_k(b + 2, u)
                        body(0, 0, 0, True, True, True, first=True)
                        body(1, 1, 0, True, True, True)
                        with dve.Fori(1, LOOP // 2) as i:
                            for u in range(2):
                                body(2 * i + u, u, i, True, True, True)
                        for b in range(LOOP, B):
                            body(b, b % 2, b // 2, b + 3 < B, b + 2 < B, b + 1 < B)
                        evacuate(B - 1, 1)

                        for a in range(2):
                            cols = slice(a * HALF, (a + 1) * HALF)
                            dve.wait_ge(summed, 3 + a)
                            nc.vector.reciprocal(inv[:, cols], ps[:, 2 + a, 0:HALF]).then_inc(inv_ready, 1)
                            dve.wait_ge(inv_ready, a + 1)
                            nc.vector.tensor_tensor(num[:, cols], ps[:, a, 0:HALF], inv[:, cols], ALU.mult)\
                                     .then_inc(prod_ready, 1)
                            dve.wait_ge(prod_ready, a + 1)
                            nc.vector.tensor_scalar(att[:, cols], num[:, cols], bias[:, BV2:BV2 + 1], None,
                                                    ALU.add).then_inc(att_ready, 1)

            bad = sx("bad", [P, 2])
            flag_f = sx("flag_f", [P, 1])
            bad_ready = sem("bad_ready")
            counted = sem("counted")
            flag_ready = sem("flag_ready")
            with nc.Block() as block:
                @block.vector
                def _(dve):
                    nc.vector.tensor_scalar(bad[:, 0:1], worst[:, :], GUARD, None, ALU.is_le).then_inc(bad_ready, 1)
                    nc.vector.tensor_scalar(bad[:, 1:2], mask_max[:, :], 0.0, None, ALU.is_equal)\
                             .then_inc(bad_ready, 1)
                    dve.wait_ge(counted, 1)
                    nc.vector.tensor_reduce(flag_f[:, :], ps[:, 0, 0:2], AX.X, ALU.min).then_inc(flag_ready, 1)
                    dve.wait_ge(flag_ready, 1)
                    nc.vector.tensor_scalar(flag[:, :], flag_f[:, :], P - 0.5, None, ALU.is_lt)\
                             .then_inc(flag_ready, 1)
                    dve.wait_ge(flag_ready, 2)

                @block.tensor
                def _(pe):
                    pe.wait_ge(bad_ready, 2)
                    nc.tensor.matmul(ps[:, 0, 0:2], ones[:, :], bad[:, :], start=True, stop=True)\
                             .then_inc(counted, 1)
            return flag, q_stack, k_part, k_stack, values, k_matmul, v_matmul, v_evacuate, k_split

        def general_cross_attention(shared):
            _, q_stack, k_part, k_stack, values, k_matmul, v_matmul, v_evacuate, k_split = shared
            with ExitStack() as st:
                sg = tensors(st)
                mask_sb = sg("mask_g", [PQ, SK])
                s_all = sg("s_all", [PQ, SK])
                p_t = sg("p_t_g", [KW, KT, PQ])
                row_max = sg("row_max_g", [PQ, 1])
                total = sg("total_g", [PQ, 1])
                zero_total = sg("zero_total_g", [PQ, 1])
                zero_ready = sem("zero_ready_g")
                inv = sg("inv_g", [PQ, 1])
                picked = sg("picked_g", [16, 2, S])
                folded = sg("folded_g", [16, S])
                scratch = nc.dram_tensor("attention_scratch", [P, TOK], F32).ap()

                mask_in = sem("mask_in_g")
                ctx_g = sem("ctx_in_g")
                proj = sem("proj_done_g")
                k_hi, k_restr, k_mid, k_ready, v_ready = (sem(f"{n}_g") for n in
                                                          ("k_hi", "k_rest", "k_mid", "k_parts", "values"))
                stack_in = sem("kstack_in_g")
                scores_done = sem("scores_done_g")
                masked = sem("masked_g")
                max_ready = sem("max_ready_g")
                exp_done = sem("exp_done_g")
                inv_ready = sem("inv_ready_g")
                scaled = sem("scaled_g")
                turned = sem("turned_g")
                p_t_ready = sem("p_t_ready_g")
                pv_done = sem("pv_done_g")
                picked_ready = sem("picked_ready_g")
                folded_ready = sem("folded_ready_g")
                stored = sem("stored_g")
                back_in = sem("attention_back")
                bias_added = sem("bias_added_g")
                names = (k_hi, k_restr, k_mid, None, k_ready)

                v_flat = values[0][0:KW, :, 0:P]

                with nc.Block() as block:
                    @block.sync
                    def _(sp):
                        sp.dma_start(mask_sb[:, :], mask).then_inc(mask_in, 16)

                        def body(b):
                            def held(value):
                                return value if isinstance(value, int) else sp.snap(value)

                            attended, parts_made = held(PAIRS * b), held(3 * b + 3)
                            columns = held(b * S)
                            folds = [held(PAIRS * b + p + 1) for p in range(PAIRS)]
                            if not isinstance(b, int):
                                sp.wait_ge(pv_done, attended)
                            sp.dma_start(ctx_buf[0][:, :], ctx_t[bass.ds(b, 1)].rearrange("a d k -> d (a k)"))\
                              .then_inc(ctx_g, 16)
                            sp.wait_ge(k_ready, parts_made)
                            for n, part in enumerate(K_PART):
                                sp.dma_start(k_stack[0][16 * n:16 * n + 16, :, :], k_part[0][:, part, :])\
                                  .then_inc(stack_in, 16)
                            for p in range(PAIRS):
                                sp.wait_ge(folded_ready, folds[p])
                                sp.dma_start(scratch[16 * p:16 * p + 16, bass.ds(columns, S)], folded[:, :])\
                                  .then_inc(stored, 16)
                        body(0)
                        with sp.Fori(1, B) as b:
                            body(b)
                        sp.wait_ge(stored, 16 * PAIRS * B)
                        sp.dma_start(att[:, :], scratch).then_inc(back_in, 16)

                    @block.gpsimd
                    def _(pool):
                        nc.gpsimd.memset(zero_total[:, :], 0.0).then_inc(zero_ready, 1)

                    @block.tensor
                    def _(pe):
                        def body(b):
                            pe.wait_ge(ctx_g, 16 * b + 16)
                            for n in range(3):
                                if n == 2 or not isinstance(b, int):
                                    pe.wait_ge(k_ready, 3 * b + n - 1 if n < 2 else 3 * b + 1)
                                k_matmul(pe, 0, n, 6 + n % 2).then_inc(proj, 1)
                            for n in range(3):
                                if n == 0:
                                    pe.wait_ge(k_ready, 3 * b + 3)
                                if n == 2:
                                    pe.wait_ge(v_ready, 3 * b + 1)
                                v_matmul(pe, 0, n, 6 + n % 2).then_inc(proj, 1)
                            pe.wait_ge(stack_in, 16 * len(K_PART) * (b + 1))
                            for p in range(PAIRS):
                                j = PAIRS * b + p
                                if p or not isinstance(b, int):
                                    pe.wait_ge(masked, j)
                                for n in range(NKC):
                                    last = nc.tensor.matmul(ps[0:PQ, n, 0:KC],
                                                            q_stack[:, p, bass.ds(b * PQ, PQ)],
                                                            k_stack[0][:, p, n * KC:(n + 1) * KC],
                                                            start=True, stop=True)
                                last.then_inc(scores_done, 1)
                                pe.wait_ge(scaled, j + 1)
                                for t in range(KT):
                                    last = nc.tensor.transpose(ps[0:KW, 3 + t // 4, (t % 4) * PQ:(t % 4 + 1) * PQ],
                                                               s_all[:, t * KW:(t + 1) * KW], eye[0:PQ, 0:PQ])
                                last.then_inc(turned, 1)
                                pe.wait_ge(p_t_ready, j + 1)
                                pe.wait_ge(v_ready, 3 * b + 3)
                                for t in range(KT):
                                    last = nc.tensor.matmul(
                                        ps[0:16, 6, 0:PQ],
                                        v_pair(p, t), p_t[:, t, :], start=(t == 0), stop=(t == KT - 1))
                                last.then_inc(pv_done, 1)
                                pe.wait_ge(picked_ready, j + 1)

                        def v_pair(p, t):
                            return v_flat[:, t, 16 * p:16 * p + 16]
                        body(0)
                        with pe.Fori(1, B) as b:
                            body(b)

                    @block.scalar
                    def _(act):
                        def body(b):
                            for p in range(PAIRS):
                                act.wait_ge(max_ready, PAIRS * b + p + 1)
                                nc.scalar.activation(s_all[:, :], s_all[:, :], ACT.Exp, bias=row_max[:, 0:1],
                                                     accum_out=total[:, 0:1]).then_inc(exp_done, 1)
                        body(0)
                        with act.Fori(1, B) as b:
                            body(b)

                    @block.vector
                    def _(dve):
                        dve.wait_ge(mask_in, 16)
                        diag = c("diag").rearrange("p (h s) -> p h s", h=2)

                        def body(b):
                            if not isinstance(b, int):
                                dve.wait_ge(stack_in, 16 * len(K_PART) * b)
                            for n in range(3):
                                dve.wait_ge(proj, 6 * b + n + 1)
                                k_split(dve, 0, n, 6 + n % 2, 3 * b + n, names)
                            for n in range(3):
                                dve.wait_ge(proj, 6 * b + 4 + n)
                                nc.vector.tensor_copy(values[0][0:KW, 4 * n:4 * n + 4, 0:P],
                                                      ps[0:KW, 6 + n % 2, :].rearrange("p (t m) -> p t m", t=4))\
                                         .then_inc(v_ready, 1)
                            for p in range(PAIRS):
                                j = PAIRS * b + p
                                dve.wait_ge(scores_done, j + 1)
                                nc.vector.tensor_tensor(s_all[:, :].rearrange("p (n k) -> p n k", k=KC),
                                                        ps[0:PQ, 0:NKC, 0:KC],
                                                        mask_sb[:, :].rearrange("p (n k) -> p n k", k=KC),
                                                        ALU.add).then_inc(masked, 1)
                                dve.wait_ge(masked, j + 1)
                                nc.vector.tensor_reduce(row_max[:, :], s_all[:, :], AX.X, ALU.max, negate=True)\
                                         .then_inc(max_ready, 1)
                                dve.wait_ge(exp_done, j + 1)
                                nc.vector.reciprocal(inv[:, :], total[:, :]).then_inc(inv_ready, 1)
                                dve.wait_ge(inv_ready, j + 1)
                                nc.vector.tensor_scalar(s_all[:, :], s_all[:, :], inv[:, 0:1], None, ALU.mult)\
                                         .then_inc(scaled, 1)
                                dve.wait_ge(turned, j + 1)
                                nc.vector.tensor_copy(p_t[:, :, :].rearrange("p (a n) m -> p a (n m)", a=3),
                                                      ps[0:KW, 3:6, 0:4 * PQ]).then_inc(p_t_ready, 1)
                                dve.wait_ge(pv_done, j + 1)
                                if p or not isinstance(b, int):
                                    dve.wait_ge(stored, 16 * j)
                                nc.vector.tensor_tensor(picked[:, :, :],
                                                        ps[0:16, 6, 0:PQ].rearrange("p (h s) -> p h s", h=2),
                                                        diag[0:16], ALU.mult).then_inc(picked_ready, 1)
                                dve.wait_ge(picked_ready, j + 1)
                                nc.vector.tensor_tensor(folded[:, :], picked[:, 0, :], picked[:, 1, :], ALU.add)\
                                         .then_inc(folded_ready, 1)
                        body(0)
                        with dve.Fori(1, B) as b:
                            body(b)
                        dve.wait_ge(back_in, 16)
                        nc.vector.tensor_scalar(att[:, :], att[:, :], bias[:, BV2:BV2 + 1], None, ALU.add)\
                                 .then_inc(bias_added, 1)

        def feed_forward(w_exp):
            with ExitStack() as st:
                sf = tensors(st)
                hid = [sf(f"hid_{u}", [P, FC, TOK]) for u in range(3)]
                acc = sf("acc", [P, NT, P])
                rt = sf("router", [P, E])
                b2_sb = sf("b2", [NE, P])
                logit = sf("logit", [P, NT, E])
                best = sf("best", [P, NT, 1])
                prob = sf("prob", [P, NT, E])
                total = sf("total", [P, NT, 1])
                hit = sf("hit", [P, NT, E])
                first = sf("first", [P, NT, E])
                comb = sf("comb", [P, NT, NE])
                comb_t = sf("comb_t", [NE, NT, P])
                named = norm_names("out", sf)

                small_in = sem("small_in")
                logits_done = sem("logits_done")
                chain = sem("router_steps")
                exp_done = sem("router_exp_done")
                comb_ready = sem("comb_ready")
                comb_turned = sem("comb_turned")
                comb_t_ready = sem("comb_t_ready")
                b2_done = sem("b2_done")
                acc_start = sem("acc_start")
                up_done = sem("up_done")
                gelu_done = sem("gelu_done")
                down_done = sem("down_done")
                acc_done = sem("acc_done")
                stored = sem("stored")

                with nc.Block() as block:
                    @block.sync
                    def _(sp):
                        sp.dma_start(rt[:, :], router_t).then_inc(small_in, 16)
                        sp.dma_start(b2_sb[:, :], b2).then_inc(small_in, 16)
                        with sp.Fori(0, NE // 3 - 1) as i:
                            for r in range(3):
                                network = sp.snap(3 * i + r + 3)
                                read = sp.snap(6 * i + 2 * r + 2)
                                sp.wait_ge(down_done, read)
                                sp.dma_start(w_exp[r][:, :], experts[bass.ds(network, 1)]
                                             .rearrange("a p n -> p (a n)")).then_inc(expert_in[r], 16)
                        for n, (a, z) in enumerate(((0, 4), (4, NT))):
                            sp.wait_ge(named["normal_ready"], z)
                            sp.dma_start(out[a * P:z * P].rearrange("(t p) d -> p t d", p=P), xn[:, a:z, :])\
                              .then_inc(stored, 16)
                        sp.wait_ge(stored, 32)

                    @block.tensor
                    def _(pe):
                        pe.wait_ge(small_in, 32)
                        for t in range(NT):
                            last = nc.tensor.matmul(ps[:, 7, t * E:(t + 1) * E], xt[:, t * P:(t + 1) * P], rt[:, :],
                                                    start=True, stop=True)
                        last.then_inc(logits_done, 1)

                        def up(e, r, i):
                            pe.wait_ge(expert_in[r], 16 * (i + 1))
                            for n in range(2 * FC):
                                f, a = n // 2, n % 2
                                if n >= 4 or not isinstance(e, int) or e >= 1:
                                    pe.wait_ge(gelu_done, 8 * e + n - 3)
                                nc.tensor.matmul(ps[:, n % 4, 0:HALF],
                                                 w_exp[r][:, W1_AT + f * P:W1_AT + (f + 1) * P],
                                                 xt[:, a * HALF:(a + 1) * HALF],
                                                 start=True, stop=True).then_inc(up_done, 1)

                        def down(e, r):
                            pe.wait_ge(gelu_done, 8 * e + 8)
                            for n, (a, z) in enumerate(((0, 4), (4, NT))):
                                if n == 0:
                                    if isinstance(e, int) and e == 0:
                                        pe.wait_ge(acc_start, 1)
                                    else:
                                        pe.wait_ge(acc_done, 2 * e - 1)
                                elif not (isinstance(e, int) and e == 0):
                                    pe.wait_ge(acc_done, 2 * e)
                                for t in range(a, z):
                                    for f in range(FC):
                                        last = nc.tensor.matmul(
                                            ps[:, 4 + n, (t - a) * P:(t - a + 1) * P],
                                            hid[r][:, f, t * P:(t + 1) * P],
                                            w_exp[r][:, W2_AT + f * P:W2_AT + (f + 1) * P],
                                            start=(f == 0), stop=(f == FC - 1))
                                last.then_inc(down_done, 1)

                        up(0, 0, 0)
                        pe.wait_ge(comb_ready, 1)
                        for t in range(NT):
                            last = nc.tensor.transpose(ps[0:NE, 4 + t // 4, (t % 4) * P:(t % 4 + 1) * P],
                                                       comb[:, t, :], eye)
                        last.then_inc(comb_turned, 1)
                        pe.wait_ge(comb_t_ready, 1)
                        for t in range(NT):
                            last = nc.tensor.matmul(ps[:, 4 + t // 4, (t % 4) * P:(t % 4 + 1) * P],
                                                    comb_t[:, t, :], b2_sb[:, :], start=True, stop=True)
                        last.then_inc(b2_done, 1)
                        up(1, 1, 0)
                        down(0, 0)
                        up(2, 2, 0)
                        down(1, 1)
                        with pe.Fori(1, NE // 3) as i:
                            for r in range(3):
                                up(3 * i + r, r, i)
                                down(3 * i + r - 1, (r + 2) % 3)
                        down(NE - 1, 2)

                    @block.scalar
                    def _(act):
                        act.wait_ge(chain, 3)
                        nc.scalar.activation(prob[:, :, :], logit[:, :, :], ACT.Exp).then_inc(exp_done, 1)

                        def gelu(e, r, i):
                            for n in range(2 * FC):
                                f, a = n // 2, n % 2
                                act.wait_ge(up_done, 8 * e + n + 1)
                                if n == 0 and not (isinstance(e, int) and e < 3):
                                    act.wait_ge(down_done, 2 * e - 4)
                                nc.scalar.activation(hid[r][:, f, a * HALF:(a + 1) * HALF], ps[:, n % 4, 0:HALF],
                                                     ACT.Gelu_apprx_tanh,
                                                     bias=w_exp[r][:, B1_AT + f:B1_AT + f + 1]).then_inc(gelu_done, 1)
                        for r in range(3):
                            gelu(r, r, 0)
                        with act.Fori(1, NE // 3) as i:
                            for r in range(3):
                                gelu(3 * i + r, r, i)
                        deviation(act, named)

                    @block.vector
                    def _(dve):
                        steps = [0]

                        def step(ins):
                            ins.then_inc(chain, 1)
                            steps[0] += 1
                            dve.wait_ge(chain, steps[0])

                        def wide(a):
                            return a[:, :, :].to_broadcast([P, NT, E])

                        dve.wait_ge(logits_done, 1)
                        step(nc.vector.tensor_tensor(logit[:, :, :], ps[:, 7, 0:NT * E].rearrange("p (t e) -> p t e", e=E),
                                                     row[:, ROW_RB:ROW_RB + E].unsqueeze(1).to_broadcast([P, NT, E]),
                                                     ALU.add))
                        step(nc.vector.tensor_reduce(best[:, :, 0], logit[:, :, :], AX.X, ALU.max))
                        step(nc.vector.tensor_tensor(logit[:, :, :], logit[:, :, :], wide(best), ALU.subtract))
                        dve.wait_ge(exp_done, 1)
                        step(nc.vector.tensor_reduce(total[:, :, 0], prob[:, :, :], AX.X, ALU.add))
                        step(nc.vector.reciprocal(best[:, :, :], total[:, :, :]))
                        step(nc.vector.tensor_tensor(prob[:, :, :], prob[:, :, :], wide(best), ALU.mult))
                        down_ = c("down").unsqueeze(1).to_broadcast([P, NT, E])

                        def pick(left, into):
                            step(nc.vector.tensor_reduce(best[:, :, 0], left[:, :, :], AX.X, ALU.max))
                            step(nc.vector.tensor_tensor(hit[:, :, :], left[:, :, :], wide(best), ALU.is_equal))
                            step(nc.vector.tensor_tensor(hit[:, :, :], hit[:, :, :], down_, ALU.mult))
                            step(nc.vector.tensor_reduce(best[:, :, 0], hit[:, :, :], AX.X, ALU.max))
                            step(nc.vector.tensor_tensor(into[:, :, :], hit[:, :, :], wide(best), ALU.is_equal))

                        pick(prob, first)
                        step(nc.vector.scalar_tensor_tensor(out=logit[:, :, :], in0=first[:, :, :], scalar=-2.0,
                                                            in1=prob[:, :, :], op0=ALU.mult, op1=ALU.add))
                        pick(logit, hit)
                        step(nc.vector.tensor_tensor(first[:, :, :], first[:, :, :], hit[:, :, :], ALU.add))
                        step(nc.vector.tensor_tensor(prob[:, :, :], prob[:, :, :], first[:, :, :], ALU.mult))
                        step(nc.vector.tensor_reduce(total[:, :, 0], prob[:, :, :], AX.X, ALU.add))
                        step(nc.vector.reciprocal(best[:, :, :], total[:, :, :]))
                        step(nc.vector.memset(comb[:, :, E:NE], 1.0))
                        nc.vector.tensor_tensor(comb[:, :, 0:E], prob[:, :, :], wide(best), ALU.mult)\
                                 .then_inc(comb_ready, 1)
                        dve.wait_ge(comb_turned, 1)
                        step(nc.vector.tensor_copy(comb_t[:, 0:4, :].rearrange("p t m -> p (t m)"), ps[0:NE, 4, :]))
                        nc.vector.tensor_copy(comb_t[:, 4:NT, :].rearrange("p t m -> p (t m)"), ps[0:NE, 5, 0:3 * P])\
                                 .then_inc(comb_t_ready, 1)
                        dve.wait_ge(b2_done, 1)
                        step(nc.vector.tensor_tensor(acc[:, 0:4, :], ps[:, 4, :].rearrange("p (t d) -> p t d", d=P),
                                                     xn[:, 0:4, :], ALU.add))
                        nc.vector.tensor_tensor(acc[:, 4:NT, :], ps[:, 5, 0:3 * P].rearrange("p (t d) -> p t d", d=P),
                                                xn[:, 4:NT, :], ALU.add).then_inc(acc_start, 1)
                        dve.wait_ge(acc_start, 1)

                        def add(e, last=False):
                            for n, (a, z) in enumerate(((0, 4), (4, NT))):
                                dve.wait_ge(down_done, 2 * e + n + 1)
                                if not (isinstance(e, int) and e == 0):
                                    dve.wait_ge(acc_done, 2 * e + n - 1)
                                for t in range(a, z):
                                    ins = nc.vector.scalar_tensor_tensor(
                                        out=acc[:, t, :], in0=ps[:, 4 + n, (t - a) * P:(t - a + 1) * P],
                                        scalar=comb[:, t, bass.ds(e, 1)], in1=acc[:, t, :],
                                        op0=ALU.mult, op1=ALU.add)
                                ins.then_inc(acc_done, 1)
                                if last:
                                    dve.wait_ge(acc_done, 2 * e + n + 1)
                                    dve.sem_inc(named["y_ready"], 1)
                        add(0)
                        with dve.Fori(1, NE - 1) as e:
                            add(e)
                        add(NE - 1, last=True)
                        normalise(dve, None, named, acc, xn)

        self_attention()
        project_and_norm("self", WO1, ROW_BO1)
        with ExitStack() as cross:
            shared = cross_attention(cross)
            again = nc.values_load(shared[0][0:1, 0:1], min_val=0, max_val=1)
            with nc.If(again > 0):
                general_cross_attention(shared)
        w_exp = [sb(f"w_exp_{r}", [P, NW]) for r in range(3)]
        with nc.Block() as block:
            @block.sync
            def _(sp):
                for r in range(3):
                    sp.dma_start(w_exp[r][:, :], experts[r]).then_inc(expert_in[r], 16)
        project_and_norm("cross", WO2, ROW_BO2)
        feed_forward(w_exp)


def kernel(x, ctx_1024, mask_1x1xSxS2_ff0, L0_attn_Wq, L0_attn_bq, L0_attn_Wk, L0_attn_bk, L0_attn_Wv,
           L0_attn_bv, L0_attn_Wo, L0_attn_bo, L0_attn_slopes, L0_xattn_Wq, L0_xattn_bq, L0_xattn_Wk,
           L0_xattn_bk, L0_xattn_Wv, L0_xattn_bv, L0_xattn_Wo, L0_xattn_bo, L0_ffn_shared_w1,
           L0_ffn_shared_b1, L0_ffn_shared_w2, L0_ffn_shared_b2, L0_ffn_router_w, L0_ffn_router_b,
           L0_ffn_spec_w1, L0_ffn_spec_b1, L0_ffn_spec_w2, L0_ffn_spec_b2):
    import concourse.bacc as bacc
    from concourse.bass_utils import run_bass_kernel_spmd

    def of(a):
        return np.asarray(a)

    order = np.array([(2 * (p % PAIRS) + p // 64) * DH + (p // PAIRS) % DH for p in range(P)])
    x2 = of(x).reshape(TOK, P)
    wq2, wk2 = of(L0_xattn_Wq)[order], of(L0_xattn_Wk)[order]
    w_t = np.stack([of(w).T for w in (L0_attn_Wq, L0_attn_Wk, L0_attn_Wv, L0_attn_Wo, wq2, wk2,
                                      L0_xattn_Wv, L0_xattn_Wo)], 1)
    bias_cols = np.stack([of(L0_attn_bq), of(L0_attn_bk), of(L0_attn_bv), of(L0_xattn_bq)[order],
                          of(L0_xattn_bk)[order], of(L0_xattn_bv)], 1)
    rows = np.concatenate([of(L0_attn_bo), of(L0_xattn_bo), of(L0_ffn_router_b), of(L0_attn_slopes)])
    w1 = np.concatenate([of(L0_ffn_spec_w1), of(L0_ffn_shared_w1)[None]])
    w2 = np.concatenate([of(L0_ffn_spec_w2), of(L0_ffn_shared_w2)[None]])
    b1 = np.concatenate([of(L0_ffn_spec_b1), of(L0_ffn_shared_b1)[None]])
    b2 = np.concatenate([of(L0_ffn_spec_b2), of(L0_ffn_shared_b2)[None]])
    experts = np.concatenate([
        w1.transpose(0, 2, 1),
        w2.transpose(0, 2, 1).reshape(NE, FC, P, P).transpose(0, 2, 1, 3).reshape(NE, P, F),
        b1.reshape(NE, FC, P).transpose(0, 2, 1)], 2)
    arrays = {
        "x": x2, "x_t": x2.T, "ctx_t": of(ctx_1024).transpose(0, 2, 1),
        "mask": np.tile(of(mask_1x1xSxS2_ff0).reshape(S, SK), (2, 1)),
        "w_t": w_t, "bias_cols": bias_cols, "rows": np.tile(rows[None], (P, 1)),
        "router_t": of(L0_ffn_router_w).T, "experts": experts, "b2": b2, "constants": CONSTANTS,
    }
    arrays = {f"in_{n}": np.ascontiguousarray(a) for n, a in arrays.items()}
    nc = bacc.Bacc("TRN2", target_bir_lowering=False, num_devices=1)
    args = [nc.dram_tensor(n, a.shape, mybir.dt.from_np(a.dtype), kind="ExternalInput").ap()
            for n, a in arrays.items()]
    out = nc.dram_tensor("out_0", (TOK, P), F32, kind="ExternalOutput").ap()
    build(nc, *args, out)
    r = run_bass_kernel_spmd(nc, [arrays], core_ids=[0])
    return r.results[0]["out_0"].reshape(B, S, P)
```

```python
from contextlib import ExitStack

import numpy as np

import concourse.bass as bass
from concourse import mybir

ALU = mybir.AluOpType
ACT = mybir.ActivationFunctionType
AX = mybir.AxisListType
F32 = mybir.dt.float32
F32R = mybir.dt.float32r
BF16 = mybir.dt.bfloat16
I32 = mybir.dt.int32

P = 128
B = 16
S = 56
TOK = B * S
NT = TOK // P
HALF = TOK // 2
H = 16
DH = P // H
PAIRS = H // 2
PQ = 2 * S
SK = 1500
KW = 125
KT = SK // KW
KC = 500
NKC = SK // KC
SKP = SK + 4
VC = DH + 1
VW = H * VC + 24
F = 512
FC = F // P
E = 8
NE = E + 1
EPS = 1e-5
SCALE = float(DH) ** -0.5
K_PART = (0, 1, 0, 1, 2, 0)
Q_PART = (0, 0, 1, 1, 0, 2)
ROWS = 16 * len(K_PART)
HEADROOM = 50.0
GUARD = 54.0


def shape_constants():
    part = np.arange(P)
    eye = np.eye(P, dtype=np.float32)
    head = (part[:, None] // DH == np.arange(H)[None]).astype(np.float32)
    head2 = (2 * (part % PAIRS) + part // (P // 2))[:, None] == np.arange(H)[None]
    dist = np.zeros((P, S), np.float32)
    for at in (0, 64):
        dist[at:at + S] = np.arange(S)[None] - np.arange(S)[:, None]
    own = np.zeros((P, H, DH), np.float32)
    for r in range(PQ):
        own[r, (r // S)::2] = 1
    sel = np.zeros((P, 2, 4, P), np.float32)
    for h in range(H):
        tile, block = (h // 3, h % 3) if h < 12 else (h - 12, 3)
        first = 32 * tile + VC * (block if block < 3 else 0)
        for d in range(DH):
            sel[first + d, 0, block, h * DH + d] = 1
            sel[first + DH, 1, block, h * DH + d] = 1
    down = np.tile(np.arange(E, 0, -1, dtype=np.float32), (P, 1))
    diag = np.zeros((P, 2, S), np.float32)
    for r in range(16):
        diag[r, r // DH] = 1
    parts = [("eye", eye), ("head", head), ("head2", head2.astype(np.float32)), ("dist", dist),
             ("own", own.reshape(P, -1)), ("sel", sel.reshape(P, -1)), ("down", down),
             ("diag", diag.reshape(P, -1))]
    at, where = 0, {}
    for name, a in parts:
        where[name] = (at, a.shape[1])
        at += a.shape[1]
    return np.concatenate([a for _, a in parts], 1).astype(np.float32), where


CONSTANTS, CONST_AT = shape_constants()
NCONST = CONSTANTS.shape[1]
BQ1, BK1, BV1, BQ2, BK2, BV2 = range(6)
ROW_BO1, ROW_BO2, ROW_RB, ROW_SL = 0, P, 2 * P, 2 * P + E
NROW = 2 * P + E + H
WQ1, WK1, WV1, WO1, WQ2, WK2, WV2, WO2 = range(8)
W1_AT, W2_AT, B1_AT = 0, F, 2 * F
NW = 2 * F + FC


def build(nc, x, x_t, ctx_t, mask, w_t, bias_cols, rows, router_t, experts, b2, constants, out):
    with ExitStack() as top:
        def sem(name):
            return top.enter_context(nc.semaphore(name))

        def tensors(stack):
            return lambda name, shape, dt=F32: stack.enter_context(nc.sbuf_tensor(name, shape, dt))

        sb = tensors(top)
        ps = top.enter_context(nc.psum_tensor("ps", [P, 8, 512], F32))
        const = sb("const", [P, NCONST])
        wts = sb("wts", [P, 8, P])
        bias = sb("bias", [P, 6])
        row = sb("row", [P, NROW])
        xn = sb("xn", [P, NT, P])
        xt = sb("xt", [P, TOK])
        att = sb("att", [P, TOK])
        eps = sb("eps", [P, 1])
        ones = sb("ones", [P, P])

        def c(name):
            at, n = CONST_AT[name]
            return const[:, at:at + n]

        eye = c("eye")
        sel = c("sel").rearrange("p (k j m) -> p k j m", k=2, j=4)

        consts_in = sem("consts_in")
        x_in = sem("x_in")
        ctx_in = [sem("ctx_in_even"), sem("ctx_in_odd")]
        expert_in = [sem(f"expert_in_{i}") for i in range(3)]

        attention_memory = top.enter_context(ExitStack())
        sm = tensors(attention_memory)
        ctx_buf = [sm(f"ctx_{u}", [P, SK]) for u in range(2)]
        ctx_part = sm("ctx_part", [P, 2, SK], F32R)
        wk_part = sm("wk_part", [P, 2, P], F32R)
        k_part = [sm(f"k_part_{u}", [P, 3, SKP], BF16) for u in range(2)]
        values = [sm(f"values_{u}", [P, KT, VW]) for u in range(2)]
        worst = sm("worst", [P, 1])
        k_rest = [sm(f"k_rest_{r}", [P, KC]) for r in range(2)]
        k_full = [sm(f"k_full_{r}", [P, KC]) for r in range(2)]
        mask_max = sm("mask_max", [P, 1])
        q_max = sm("q_max", [P, B])
        q_stack = sm("q_stack", [ROWS, PAIRS, B * PQ], BF16)
        q_wide = sm("q_wide", [P, 3, B, 2, S], BF16)
        ctx_split = sem("ctx_split")
        mask_in = sem("mask_in")

        def split_r(eng, whole, hi, lo, done, count):
            eng.tensor_tensor(hi, whole, ones[:, 0:1].to_broadcast([P, whole.shape[1]]), ALU.mult).then_inc(done, 1)
            eng.wait_ge(done, count + 1)
            eng.tensor_tensor(lo, whole, hi.bitcast(F32), ALU.subtract).then_inc(done, 1)

        PARTS = ((0, 0), (0, 1), (1, 0))

        def load_ctx(sp, b, u):
            sp.dma_start(ctx_buf[u][:, :], ctx_t[bass.ds(b, 1)].rearrange("a d k -> d (a k)"))\
              .then_inc(ctx_in[u], 16)

        def add_output_bias(at):
            return nc.gpsimd.tensor_tensor(xn[:, :, :], xn[:, :, :],
                                           row[:, at:at + P].unsqueeze(1).to_broadcast([P, NT, P]), ALU.add)

        early_done = sem("early_units_done")
        full_ready = sem("early_k_full")
        hi0 = sem("early_k_hi")
        rest0 = sem("early_k_rest")
        mid0 = sem("early_k_mid")
        k0_ready = sem("early_k_parts")

        def early_k(pe, m):
            if m % 3 == 0:
                pe.wait_ge(ctx_in[m // 3], 16)
            nc.tensor.matmul(ps[:, 2 + m, 0:KC], wts[:, WK2, :],
                             ctx_buf[m // 3][:, (m % 3) * KC:(m % 3 + 1) * KC],
                             start=True, stop=True).then_inc(early_done, 1)

        def early_hi(act, m):
            act.wait_ge(early_done, m + 1)
            if m >= 2:
                act.wait_ge(k0_ready, m - 1)
            nc.scalar.activation(k_full[m % 2][:, :], ps[:, 2 + m, 0:KC], ACT.Identity,
                                 bias=bias[:, BK2:BK2 + 1]).then_inc(full_ready, 1)
            nc.scalar.activation(k_part[m // 3][:, 0, (m % 3) * KC:(m % 3 + 1) * KC],
                                 ps[:, 2 + m, 0:KC], ACT.Identity,
                                 bias=bias[:, BK2:BK2 + 1]).then_inc(hi0, 1)

        def early_mid(act, m):
            act.wait_ge(rest0, m + 1)
            nc.scalar.copy(k_part[m // 3][:, 1, (m % 3) * KC:(m % 3 + 1) * KC],
                           k_rest[m % 2][:, :]).then_inc(mid0, 1)

        def early_rest(pool, m):
            if m > 1:
                pool.wait_ge(k0_ready, m - 1)
            pool.wait_ge(hi0, m + 1)
            nc.gpsimd.tensor_tensor(k_rest[m % 2][:, :], k_full[m % 2][:, :],
                                    k_part[m // 3][:, 0, (m % 3) * KC:(m % 3 + 1) * KC],
                                    ALU.subtract).then_inc(rest0, 1)

        def early_lo(pool, m):
            cols = slice((m % 3) * KC, (m % 3 + 1) * KC)
            pool.wait_ge(mid0, m + 1)
            nc.gpsimd.tensor_tensor(k_part[m // 3][:, 2, cols], k_rest[m % 2][:, :],
                                    k_part[m // 3][:, 1, cols], ALU.subtract).then_inc(k0_ready, 1)

        def self_attention():
            with ExitStack() as st:
                sa = tensors(st)
                q = sa("q1", [P, TOK])
                k = sa("k1", [P, TOK])
                alibi = sa("alibi", [P, H, S])
                q_now = [sa(f"q_now1_{u}", [P, 2, 64]) for u in range(2)]
                x_now = [sa(f"x_now1_{u}", [P, 2, 2, S]) for u in range(2)]
                k_heads = [sa(f"k_heads_{u}", [P, 2, H, S]) for u in range(2)]
                sc = [sa(f"sc1_{u}", [P, H, S]) for u in range(2)]
                p_t = [sa(f"p_t_{u}", [PQ, PAIRS, P]) for u in range(2)]
                v_own = [sa(f"v_own_{u}", [PQ, 2, H, VC]) for u in range(2)]
                row_max = [sa(f"row_max1_{u}", [P, H]) for u in range(2)]
                inv = sa("inv1", [P, H])
                o = [sa(f"o1_{u}", [P, P]) for u in range(2)]
                mask_sb = sa("mask_rows", [PQ, SK])

                pads = sem("pads_ready2")
                wk_split = sem("wk_split")
                ones_set = sem("ones_set")
                mask_done = sem("mask_max_ready")
                projected = sem("projected1")
                qk_ready = sem("qk_ready1")
                pads_zero = sem("pads_zero1")
                alibi_ready = sem("alibi_ready")
                ones_ready = sem("ones_ready1")
                x_staged = sem("x_staged1")
                q_staged = sem("q_staged1")
                heads_ready = sem("heads_ready1")
                v_done = sem("v_done1")
                v_ready = sem("v_ready1")
                scores_done = sem("scores_done1")
                scores_biased = sem("scores_biased1")
                max_ready = sem("max_ready1")
                shifted = sem("shifted1")
                exp_done = sem("exp_done1")
                turned = sem("turned1")
                p_t_ready = sem("p_t_ready1")
                pv_done = sem("pv_done1")
                inv_ready = sem("inv_ready1")
                normed = sem("normed1")
                o_turned = sem("o_turned1")
                att_ready = sem("att_ready1")

                n_pairs = B // 2

                def sweep(step):
                    def run(eng):
                        for j in range(3):
                            step(j, j % 2)
                        with eng.Fori(1, n_pairs // 2 - 1) as i:
                            for u in range(2):
                                step(2 * i + 1 + u, 1 - u)
                        for j in range(n_pairs - 1, n_pairs + 2):
                            step(j, j % 2)
                    return run

                def there(j, k):
                    return not isinstance(j, int) or 0 <= j + k < n_pairs

                with nc.Block() as block:
                    @block.sync
                    def _(sp):
                        sp.dma_start(xt[:, :], x_t).then_inc(x_in, 16)
                        sp.dma_start(wts[:, :, :], w_t).then_inc(x_in, 16)
                        sp.dma_start(bias[:, :], bias_cols).then_inc(x_in, 16)
                        sp.dma_start(const[:, :], constants).then_inc(consts_in, 16)
                        sp.dma_start(row[:, :], rows).then_inc(consts_in, 16)
                        sp.dma_start(xn[:, :, :], x.rearrange("(t p) d -> p t d", p=P)).then_inc(consts_in, 16)
                        sp.dma_start(mask_sb[:, :], mask).then_inc(mask_in, 16)
                        load_ctx(sp, 0, 0)
                        load_ctx(sp, 1, 1)

                    @block.gpsimd
                    def _(pool):
                        for u in range(2):
                            nc.gpsimd.memset(q_now[u][:, :, S:64], 0.0).then_inc(pads_zero, 1)
                        nc.gpsimd.memset(eps[:, :], EPS).then_inc(pads_zero, 1)
                        nc.gpsimd.memset(ones[:, :], 1.0).then_inc(ones_set, 1)
                        pool.wait_ge(ones_set, 1)
                        nc.gpsimd.memset(q_wide[:, :, :, :, :].rearrange("p a b h s -> p (a b h s)"), 0.0)\
                                 .then_inc(pads, 1)
                        pool.wait_ge(consts_in, 48)
                        pool.wait_ge(qk_ready, 2)

                        def stage_x(j, u):
                            if there(j, -2):
                                pool.wait_ge(v_done, j - 1)
                            for twice in range(2):
                                last = nc.gpsimd.tensor_copy(
                                    x_now[u][:, :, twice, :],
                                    xt[:, bass.ds(j * PQ, PQ)].rearrange("p (b s) -> p b s", b=2))
                            last.then_inc(x_staged, 1)

                        def step(j, u):
                            if isinstance(j, int) and j == 1:
                                pool.wait_ge(qk_ready, 4)
                            if there(j, 0):
                                if there(j, -2):
                                    pool.wait_ge(scores_done, j - 1)
                                nc.gpsimd.tensor_copy(q_now[u][:, :, 0:S],
                                                      q[:, bass.ds(j * PQ, PQ)].rearrange("p (b s) -> p b s", b=2))\
                                         .then_inc(q_staged, 1)
                                for b in range(2):
                                    ks = k[:, bass.ds(j * PQ + b * S, S)]
                                    nc.gpsimd.tensor_tensor(k_heads[u][:, b], ks.unsqueeze(1).to_broadcast([P, H, S]),
                                                            c("head").unsqueeze(2).to_broadcast([P, H, S]),
                                                            ALU.mult).then_inc(heads_ready, 1)
                            if there(j, 1):
                                stage_x(j + 1, 1 - u)

                        stage_x(0, 0)
                        sweep(step)(pool)
                        add_output_bias(ROW_BO1).then_inc(pads, 1)

                        split_r(pool, wts[:, WK2, :], wk_part[:, 0, :], wk_part[:, 1, :], wk_split, 0)
                        for u in range(2):
                            nc.gpsimd.memset(k_part[u][:, :, SK:SKP], 0.0).then_inc(pads, 1)
                            nc.gpsimd.memset(values[u][:, :, H * VC:VW], 0.0).then_inc(pads, 1)
                            nc.gpsimd.memset(values[u][:, :, 0:H * VC].rearrange("p t (h e) -> p t h e", e=VC)[:, :, :, DH:VC],
                                             1.0).then_inc(pads, 1)
                        nc.gpsimd.memset(worst[:, :], 0.0).then_inc(pads, 1)
                        early_rest(pool, 0)
                        early_lo(pool, 0)

                    @block.tensor
                    def _(pe):
                        pe.wait_ge(x_in, 48)
                        for a in range(2):
                            for n, w in enumerate((WQ1, WK1)):
                                nc.tensor.matmul(ps[:, 2 * n + a, 0:HALF], wts[:, w, :],
                                                 xt[:, a * HALF:(a + 1) * HALF],
                                                 start=True, stop=True).then_inc(projected, 1)
                        pe.wait_ge(pads_zero, 3)
                        pe.wait_ge(consts_in, 48)

                        def product_v(j, u):
                            pe.wait_ge(x_staged, j + 1)
                            if there(j, -1):
                                pe.wait_ge(v_ready, j)
                            if there(j, -4):
                                pe.wait_ge(att_ready, j - 3)
                            for b in range(2):
                                last = nc.tensor.matmul(ps[0:PQ, 6, b * P:(b + 1) * P],
                                                        x_now[u][:, b].rearrange("p r s -> p (r s)"),
                                                        wts[:, WV1, :], start=True, stop=True)
                            last.then_inc(v_done, 1)

                        def step(j, u):
                            if there(j, 0):
                                pe.wait_ge(q_staged, j + 1)
                                if isinstance(j, int) and j == 0:
                                    pe.wait_ge(qk_ready, 4)
                                pe.wait_ge(heads_ready, 2 * j + 2)
                                if there(j, -2):
                                    pe.wait_ge(scores_biased, j - 1)
                                for a in range(2):
                                    for b in range(2):
                                        last = nc.tensor.matmul(
                                            ps[64 * b:64 * b + 64, 2 * u + a, 0:HALF], q_now[u][:, b, :],
                                            k_heads[u][:, b, a * 8:a * 8 + 8, :].rearrange("p h s -> p (h s)"),
                                            start=True, stop=True)
                                last.then_inc(scores_done, 1)
                            if isinstance(j, int) and j == n_pairs:
                                pe.wait_ge(scores_biased, n_pairs)
                                early_k(pe, 0)
                            if there(j, -1):
                                pe.wait_ge(exp_done, j)
                                if there(j, -2):
                                    pe.wait_ge(p_t_ready, j - 1)
                                for p in range(PAIRS):
                                    last = nc.tensor.transpose(
                                        ps[0:PQ, 4 + p // 4, (p % 4) * P:(p % 4 + 1) * P],
                                        sc[1 - u][:, 2 * p:2 * p + 2, :].rearrange("p h s -> p (h s)"), eye)
                                last.then_inc(turned, 1)
                            if there(j, 1):
                                product_v(j + 1, 1 - u)
                            if there(j, -2):
                                pe.wait_ge(normed, j - 1)
                                if not there(j, 1):
                                    pe.wait_ge(v_ready, n_pairs)
                                    pe.wait_ge(att_ready, j - 2)
                                nc.tensor.transpose(ps[:, 6, 256:384], o[u][:, :], eye).then_inc(o_turned, 1)
                            if there(j, -1):
                                pe.wait_ge(p_t_ready, j)
                                pe.wait_ge(v_ready, j)
                                if there(j, -2):
                                    pe.wait_ge(normed, j - 1)
                                for p in range(PAIRS):
                                    for b in range(2):
                                        last = nc.tensor.matmul(
                                            ps[64 * b:64 * b + 64, 7, 2 * VC * p:2 * VC * (p + 1)],
                                            p_t[1 - u][:, p, 64 * b:64 * b + 64],
                                            v_own[1 - u][:, b, 2 * p:2 * p + 2, :].rearrange("p h e -> p (h e)"),
                                            start=True, stop=True)
                                last.then_inc(pv_done, 1)
                            if isinstance(j, int) and j == n_pairs:
                                early_k(pe, 1)

                        product_v(0, 0)
                        sweep(step)(pe)
                        pe.wait_ge(p_t_ready, n_pairs)
                        early_k(pe, 2)

                    @block.scalar
                    def _(act):
                        def step(j, u):
                            if there(j, -1):
                                act.wait_ge(turned, j)
                                if there(j, -3):
                                    act.wait_ge(pv_done, j - 2)
                                nc.scalar.copy(p_t[1 - u][:, :, :].rearrange("p (a n) m -> p a (n m)", a=2),
                                               ps[0:PQ, 4:6, :]).then_inc(p_t_ready, 1)
                            if there(j, 0):
                                act.wait_ge(shifted, j + 1)
                                nc.scalar.activation(sc[u][:, :, :], sc[u][:, :, :], ACT.Exp).then_inc(exp_done, 1)

                        sweep(step)(act)
                        early_hi(act, 0)
                        early_mid(act, 0)

                    @block.vector
                    def _(dve):
                        nc.vector.memset(mask_max[:, :], 0.0).then_inc(mask_done, 1)
                        dve.wait_ge(x_in, 48)
                        for a in range(2):
                            dve.wait_ge(projected, 2 * a + 1)
                            nc.vector.tensor_scalar(q[:, a * HALF:(a + 1) * HALF], ps[:, a, 0:HALF],
                                                    bias[:, BQ1:BQ1 + 1], SCALE, ALU.add, ALU.mult)\
                                     .then_inc(qk_ready, 1)
                            dve.wait_ge(projected, 2 * a + 2)
                            nc.vector.tensor_scalar(k[:, a * HALF:(a + 1) * HALF], ps[:, 2 + a, 0:HALF],
                                                    bias[:, BK1:BK1 + 1], None, ALU.add).then_inc(qk_ready, 1)
                        dve.wait_ge(consts_in, 48)
                        nc.vector.tensor_tensor(alibi[:, :, :], c("dist").unsqueeze(1).to_broadcast([P, H, S]),
                                                row[:, ROW_SL:ROW_SL + H].unsqueeze(2).to_broadcast([P, H, S]),
                                                ALU.mult).then_inc(alibi_ready, 1)
                        own = c("own").rearrange("p (h d) -> p h d", d=DH)
                        for u in range(2):
                            for b in range(2):
                                nc.vector.tensor_copy(v_own[u][:, b, :, DH:VC], own[0:PQ, :, 0:1])\
                                         .then_inc(ones_ready, 1)
                        dve.wait_ge(ones_ready, 4)
                        dve.wait_ge(alibi_ready, 1)
                        dve.wait_ge(mask_in, 16)
                        dve.wait_ge(mask_done, 1)
                        nc.vector.tensor_reduce(mask_max[0:PQ, :], mask_sb[:, :], AX.X, ALU.max,
                                                apply_absolute_value=True).then_inc(mask_done, 1)

                        def take_v(j, u):
                            dve.wait_ge(v_done, j + 1)
                            if there(j, -2):
                                dve.wait_ge(pv_done, j - 1)
                            for b in range(2):
                                last = nc.vector.tensor_tensor(
                                    v_own[u][:, b, :, 0:DH],
                                    ps[0:PQ, 6, b * P:(b + 1) * P].rearrange("p (h d) -> p h d", d=DH),
                                    own[0:PQ], ALU.mult)
                            last.then_inc(v_ready, 1)

                        def step(j, u):
                            if there(j, 0):
                                dve.wait_ge(scores_done, j + 1)
                                if there(j, -2):
                                    dve.wait_ge(turned, j - 1)
                                nc.vector.tensor_tensor(
                                    sc[u][:, :, :].rearrange("p (a h) s -> p a (h s)", a=2),
                                    ps[:, 2 * u:2 * u + 2, 0:HALF],
                                    alibi[:, :, :].rearrange("p (a h) s -> p a (h s)", a=2), ALU.add)\
                                         .then_inc(scores_biased, 1)
                                dve.wait_ge(scores_biased, j + 1)
                                nc.vector.tensor_reduce(row_max[u][:, :], sc[u][:, :, :], AX.X, ALU.max)\
                                         .then_inc(max_ready, 1)
                                dve.wait_ge(max_ready, j + 1)
                                nc.vector.tensor_tensor(sc[u][:, :, :], sc[u][:, :, :],
                                                        row_max[u][:, :].unsqueeze(2).to_broadcast([P, H, S]),
                                                        ALU.subtract).then_inc(shifted, 1)
                            if there(j, -2):
                                dve.wait_ge(o_turned, j - 1)
                                nc.vector.tensor_scalar(
                                    att[:, bass.ds((j - 2) * PQ, PQ)].rearrange("p (b s) -> p b s", b=2),
                                    ps[:, 6, 256:384].rearrange("p (b s) -> p b s", b=2)[:, :, 0:S],
                                    bias[:, BV1:BV1 + 1], None, ALU.add).then_inc(att_ready, 1)
                            if there(j, -1):
                                dve.wait_ge(pv_done, j)
                                pv = ps[:, 7, 0:H * VC].rearrange("p (h e) -> p h e", e=VC)
                                nc.vector.reciprocal(inv[:, :].unsqueeze(2), pv[:, :, DH:VC]).then_inc(inv_ready, 1)
                                dve.wait_ge(inv_ready, j)
                                if there(j, -3):
                                    dve.wait_ge(o_turned, j - 2)
                                nc.vector.tensor_tensor(o[1 - u][:, :].rearrange("p (h d) -> p h d", d=DH),
                                                        pv[:, :, 0:DH],
                                                        inv[:, :].unsqueeze(2).to_broadcast([P, H, DH]),
                                                        ALU.mult).then_inc(normed, 1)
                            if there(j, 1):
                                take_v(j + 1, 1 - u)

                        take_v(0, 0)
                        sweep(step)(dve)

        def normalise(dve, named, y, target):
            stats, mv, rstd = named["stats"], named["mv"], named["rstd"]
            for t in range(NT):
                dve.wait_ge(named["y_ready"], 1 if t < 4 else 2)
                nc.vector.bn_stats(stats[:, t, :], y[:, t, :]).then_inc(named["stats_ready"], 1)
            for t in range(NT):
                dve.wait_ge(named["stats_ready"], t + 1)
                nc.vector.bn_aggr(mv[:, t, :], stats[:, t, :]).then_inc(named["mv_ready"], 1)
            dve.wait_ge(named["std_ready"], 1)
            nc.vector.reciprocal(rstd[:, :], named["std"][:, :]).then_inc(named["rstd_ready"], 1)
            dve.wait_ge(named["rstd_ready"], 1)
            for t in range(NT):
                nc.vector.tensor_scalar(target[:, t, :], y[:, t, :], mv[:, t, 0:1], rstd[:, t:t + 1],
                                        ALU.subtract, ALU.mult).then_inc(named["normal_ready"], 1)

        def deviation(act, named):
            act.wait_ge(named["mv_ready"], NT)
            nc.scalar.activation(named["std"][:, :], named["mv"][:, :, 1], ACT.Sqrt, bias=eps[:, 0:1])\
                     .then_inc(named["std_ready"], 1)

        def norm_names(tag, sx):
            named = {n: sem(f"{n}_{tag}") for n in
                     ("y_ready", "stats_ready", "mv_ready", "std_ready", "rstd_ready", "normal_ready")}
            named["stats"] = sx(f"stats_{tag}", [P, NT, 6])
            named["mv"] = sx(f"mv_{tag}", [P, NT, 2])
            named["std"] = sx(f"std_{tag}", [P, NT])
            named["rstd"] = sx(f"rstd_{tag}", [P, NT])
            return named

        PARTS_OF_X = ((0, 4), (4, NT))

        class Projection:
            def __init__(self, tag, w, y, named):
                self.w, self.y, self.named = w, y, named
                self.hi_ready, self.lo_ready = sem(f"x_hi_{tag}"), sem(f"x_lo_{tag}")
                self.product, self.turned, self.xt_ready = (sem(f"{n}_{tag}") for n in ("product", "turned", "xt_ready"))

            def multiply(self):
                for n, (a, z) in enumerate(PARTS_OF_X):
                    for t in range(a, z):
                        last = nc.tensor.matmul(ps[:, n, (t - a) * P:(t - a + 1) * P], att[:, t * P:(t + 1) * P],
                                                wts[:, self.w, :], start=True, stop=True)
                    last.then_inc(self.product, 1)

            def turn(self, pe):
                for n, (a, z) in enumerate(PARTS_OF_X):
                    for t in range(a, z):
                        pe.wait_ge(self.named["normal_ready"], t + 1)
                        last = nc.tensor.transpose(ps[:, 2 + n, (t - a) * P:(t - a + 1) * P], xn[:, t, :], eye)
                    last.then_inc(self.turned, 1)

            def take_turned(self, act, xt_hi=None):
                for n, (a, z) in enumerate(PARTS_OF_X):
                    act.wait_ge(self.turned, n + 1)
                    nc.scalar.copy(xt[:, a * P:z * P], ps[:, 2 + n, 0:(z - a) * P]).then_inc(self.xt_ready, 1)
                    if xt_hi is not None:
                        nc.scalar.copy(xt_hi[:, a * P:z * P], ps[:, 2 + n, 0:(z - a) * P]).then_inc(self.hi_ready, 1)

            def normalise(self, dve):
                for n, (a, z) in enumerate(PARTS_OF_X):
                    dve.wait_ge(self.product, n + 1)
                    nc.vector.tensor_tensor(self.y[:, a:z, :], ps[:, n, 0:(z - a) * P].rearrange("p (t d) -> p t d", d=P),
                                            xn[:, a:z, :], ALU.add).then_inc(self.named["y_ready"], 1)
                normalise(dve, self.named, self.y, xn)

        def cross_attention(top_b):
            sx = tensors(top_b)
            k_stack = [sx(f"k_stack_{u}", [ROWS, PAIRS, SKP], BF16) for u in range(2)]
            k_max = [sx(f"k_max_{u}", [P, 1]) for u in range(2)]
            terms = sx("terms", [P, H])
            bound = sx("bound", [P, 1])
            shift = [sx(f"shift_{u}", [P, 1]) for u in range(2)]
            flag = sx("flag", [P, 1], I32)

            def k_matmul(u, n, bank):
                for w, x_ in PARTS:
                    last = nc.tensor.matmul(ps[:, bank, 0:KC], wk_part[:, w, :],
                                            ctx_part[:, x_, n * KC:(n + 1) * KC],
                                            start=(w + x_ == 0), stop=(w == 1))
                return last

            def v_matmul(u, n, bank):
                for i in range(4):
                    t = 4 * n + i
                    last = nc.tensor.matmul(ps[0:KW, bank, i * P:(i + 1) * P],
                                            ctx_buf[u][:, t * KW:(t + 1) * KW], wts[:, WV2, :],
                                            start=True, stop=True)
                return last

            def v_evacuate(copy, u, n, bank):
                return copy(
                    values[u][0:KW, 4 * n:4 * n + 4, 0:H * VC].rearrange("p t (h e) -> p t h e", e=VC)[:, :, :, 0:DH],
                    ps[0:KW, bank, :].rearrange("p (t h d) -> p t h d", t=4, d=DH))

            def k_split(dve, u, n, bank, count, names):
                hi_ready, rest_ready, mid_ready, bank_read, parts_ready = names
                cols = slice(n * KC, (n + 1) * KC)
                nc.vector.tensor_scalar(k_part[u][:, 0, cols], ps[:, bank, 0:KC], bias[:, BK2:BK2 + 1], None,
                                        ALU.add).then_inc(hi_ready, 1)
                dve.wait_ge(hi_ready, count + 1)
                nc.vector.scalar_tensor_tensor(out=k_rest[0][:, :], in0=ps[:, bank, 0:KC],
                                               scalar=bias[:, BK2:BK2 + 1], in1=k_part[u][:, 0, cols],
                                               op0=ALU.add, op1=ALU.subtract).then_inc(rest_ready, 1)
                dve.wait_ge(rest_ready, count + 1)
                nc.vector.tensor_copy(k_part[u][:, 1, cols], k_rest[0][:, :]).then_inc(mid_ready, 1)
                dve.wait_ge(mid_ready, count + 1)
                nc.vector.tensor_tensor(k_part[u][:, 2, cols], k_rest[0][:, :], k_part[u][:, 1, cols],
                                        ALU.subtract).then_inc(parts_ready, 1)

            with ExitStack() as st:
                sp_ = tensors(st)
                named = norm_names("self", sp_)
                q_now = [sp_(f"q_now2_{u}", [ROWS, PAIRS, PQ], BF16) for u in range(2)]
                probs = [sp_(f"probs_{r}", [P, 2, HALF]) for r in range(3)]
                outs = sp_("outs", [P, 4, B, S])
                inv, num = xt, att
                y = outs[:, 0, :, :].rearrange("p b s -> p (b s)").rearrange("p (t d) -> p t d", d=P)
                q = outs[:, 1, :, :]
                q_rest = outs[:, 2, :, :]
                first = Projection("self", WO1, y, named)

                q_projected = sem("q_projected2")
                q_ready = sem("q_ready2")
                q_hi = sem("q_hi_ready")
                q_restr = sem("q_rest_ready")
                q_mid = sem("q_mid_ready")
                q_lo = sem("q_lo_ready")
                qmax_ready = sem("q_max_ready")
                stack_in = [sem("q_stack_first_in"), sem("q_stack_rest_in")]
                v0_ready = sem("early_values")
                x_biased = sem("x_biased2")
                Q_CHUNKS = ((0, 2), (2, B))

                kstack_in = [sem("kstack_in_even"), sem("kstack_in_odd")]
                q_now_ready = sem("q_now_ready")
                proj_done = sem("proj_done")
                bank_read = sem("proj_bank_free")
                k_hi = sem("k_hi_ready")
                k_restr = sem("k_rest_ready")
                k_mid = sem("k_mid_ready")
                k_ready = sem("k_parts_ready")
                v_ready = sem("values_ready")
                kmax_ready = sem("k_max_ready")
                terms_ready = sem("terms_ready")
                bound_done = sem("bound_done")
                bound_ready = sem("bound_read")
                worst_ready = sem("worst_ready")
                shift_ready = sem("shift_ready")
                scores_done = sem("scores_done2")
                exp_done = sem("exp_done2")
                probs_free = sem("probs_free")
                pv_done = sem("pv_done2")
                out_free = sem("out_bank_free")
                summed = sem("heads_gathered")
                inv_ready = sem("inv_ready2")
                num_ready = sem("num_ready2")
                prod_ready = sem("prod_ready2")
                att_ready = sem("att_ready2")
                k_names = (k_hi, k_restr, k_mid, bank_read, k_ready)

                LOOP = B - 4

                def batches(eng, body, peel=False):
                    if peel:
                        for b in range(2):
                            body(b, b, 0, True, True, True)
                    with eng.Fori(1 if peel else 0, LOOP // 2) as i:
                        for u in range(2):
                            body(2 * i + u, u, i, True, True, True)
                    for b in range(LOOP, B):
                        body(b, b % 2, b // 2, b + 3 < B, b + 2 < B, b + 1 < B)

                with nc.Block() as block:
                    @block.sync
                    def _(sp):
                        def kstack(u):
                            for n, part in enumerate(K_PART):
                                sp.dma_start(k_stack[u][16 * n:16 * n + 16, :, :], k_part[u][:, part, :])\
                                  .then_inc(kstack_in[u], 16)

                        def qstack(chunk):
                            a, z = Q_CHUNKS[chunk]
                            sp.wait_ge(q_lo, 2 * chunk + 2)
                            for n, part in enumerate(Q_PART):
                                sp.dma_start(q_stack[16 * n:16 * n + 16, :, a * PQ:z * PQ],
                                             q_wide[:, part, a:z].rearrange("p b h s -> p (b h s)"))\
                                  .then_inc(stack_in[chunk], 16)

                        sp.wait_ge(k0_ready, 3)
                        kstack(0)
                        qstack(0)
                        sp.wait_ge(k0_ready, 6)
                        kstack(1)
                        sp.wait_ge(early_done, 9)
                        load_ctx(sp, 2, 0)
                        qstack(1)

                        def held(value):
                            return value if isinstance(value, int) else sp.snap(value)

                        def body(b, u, i, load, k_next, v_next):
                            third = held(b + 3)
                            values_made = held(6 * b + 3)
                            parts_made = held(3 * b + 3)
                            batch_scored = held(KT * b + KT)
                            if load:
                                sp.wait_ge(proj_done, values_made)
                                load_ctx(sp, third, 1 - u)
                            if k_next:
                                sp.wait_ge(k_ready, parts_made)
                                sp.wait_ge(scores_done, batch_scored)
                                kstack(u)
                        batches(sp, body)

                    @block.gpsimd
                    def _(pool):
                        def take(b, u):
                            nc.gpsimd.tensor_copy(q_now[u][:, :, :], q_stack[:, :, bass.ds(b * PQ, PQ)])\
                                     .then_inc(q_now_ready, 1)
                        early_rest(pool, 1)
                        for m in range(2, 6):
                            early_rest(pool, m)
                            early_lo(pool, m - 1)
                        early_lo(pool, 5)
                        pool.wait_ge(first.turned, 2)
                        add_output_bias(ROW_BO2).then_inc(x_biased, 1)

                        def split_ctx(b, u):
                            split_r(pool, ctx_buf[u][:, :], ctx_part[:, 0, :], ctx_part[:, 1, :], ctx_split,
                                    2 * (b - 2))
                        pool.wait_ge(ctx_in[0], 32)
                        split_ctx(2, 0)
                        pool.wait_ge(stack_in[1], 16 * len(Q_PART))

                        def body(b, u, i):
                            if not isinstance(b, int) or b + 3 < B:
                                pool.wait_ge(proj_done, 6 * b + 6)
                                pool.wait_ge(ctx_in[1 - u], 16 * (i + 2 + u))
                                split_ctx(b + 3, 1 - u)
                            if not isinstance(b, int) or b >= 2:
                                pool.wait_ge(scores_done, KT * (b + 1))
                            take(b + 2, u)
                        for u in range(2):
                            body(u, u, 0)
                        with pool.Fori(1, B // 2 - 2) as i:
                            for u in range(2):
                                body(2 * i + u, u, i)
                        for u in range(2):
                            body(B - 4 + u, u, B // 2 - 2)

                    @block.tensor
                    def _(pe):
                        def scores(u, t, b=None):
                            for p in range(PAIRS):
                                last = nc.tensor.matmul(
                                    ps[:, 2 * (t % 2) + p // 4, (p % 4) * PQ:(p % 4 + 1) * PQ],
                                    k_stack[u][:, p, t * KW:t * KW + P], q_now[u][:, p, :] if b is None else q_stack[:, p, b * PQ:(b + 1) * PQ],
                                    start=True, stop=True)
                            last.then_inc(scores_done, 1)

                        def product(b, u, t):
                            r = t % 3
                            flat = probs[r][0:KW].rearrange("p a n -> p (a n)")
                            for n in range(8):
                                g = n % 4
                                h, w, at = (3 * g, 3 * S, 0) if n < 4 else (12 + g, S, 3 * S)
                                last = nc.tensor.matmul(
                                    ps[32 * g:32 * g + 32, 4 + u, at:at + w],
                                    values[u][0:KW, t, VC * h:VC * h + 32], flat[:, h * S:h * S + w],
                                    start=(t == 0 and n < 4), stop=(t == KT - 1), skip_group_check=True)
                            last.then_inc(probs_free, 1)
                            return last

                        def unit(kind, u, n, m, bank):
                            pe.wait_ge(bank_read, m + 1)
                            last = (k_matmul if kind == "k" else v_matmul)(u, n, bank)
                            last.then_inc(proj_done, 1)

                        def early_v(n):
                            pe.wait_ge(hi0, n + 3)
                            v_matmul(0, n, 4 + n).then_inc(early_done, 1)

                        pe.sem_inc(probs_free, 3)
                        first.multiply()
                        for m in range(3, 6):
                            early_k(pe, m)
                        pe.wait_ge(hi0, 2)
                        first.turn(pe)
                        for a in range(2):
                            pe.wait_ge(first.xt_ready, a + 1)
                            nc.tensor.matmul(ps[:, a, 0:HALF], wts[:, WQ2, :], xt[:, a * HALF:(a + 1) * HALF],
                                             start=True, stop=True).then_inc(q_projected, 1)
                        for n in range(3):
                            early_v(n)
                        pe.wait_ge(v0_ready, 3)
                        pe.wait_ge(out_free, 2)
                        pe.wait_ge(terms_ready, 1)
                        nc.tensor.matmul(ps[:, 4, 256:256 + H], ones[:, :], terms[:, :],
                                         start=True, stop=True).then_inc(bound_done, 1)
                        pe.wait_ge(kstack_in[0], 16 * len(K_PART))
                        pe.wait_ge(stack_in[0], 16 * len(Q_PART))
                        pe.wait_ge(q_ready, 2)
                        scores(0, 0, 0)
                        scores(0, 1, 0)

                        def body(b, u, i, load, k_next, v_next):
                            for t in range(KT):
                                if t == 0:
                                    if not isinstance(b, int) or b > 0:
                                        pe.wait_ge(v_ready, 3 * b)
                                    pe.wait_ge(out_free, b + 1)
                                pe.wait_ge(exp_done, KT * b + t + 1)
                                static = isinstance(b, int)
                                if t + 2 < KT:
                                    scores(u, t + 2, b if static and b < 2 else None)
                                elif v_next:
                                    if t + 2 == KT:
                                        pe.wait_ge(kstack_in[1 - u],
                                                   16 * len(K_PART) * (i + u + 1))
                                        if not static or b > 0:
                                            pe.wait_ge(q_now_ready, b)
                                    scores(1 - u, t + 2 - KT, 1 if static and b == 0 else None)
                                product(b, u, t)
                                if v_next and t in (1, 2, 3):
                                    unit("v", 1 - u, t - 1, 6 * b + t - 1, 6 + t % 2)
                                if v_next and t == 4:
                                    pe.wait_ge(out_free, b + 2)
                                    pe.wait_ge(terms_ready, b + 2)
                                    nc.tensor.matmul(ps[:, 5 - u, 256:256 + H], ones[:, :], terms[:, :],
                                                     start=True, stop=True).then_inc(bound_done, 1)
                                if k_next and t in (5, 6, 7):
                                    if t == 5:
                                        pe.wait_ge(ctx_split, 2 * b + 2)
                                    unit("k", u, t - 5, 6 * b + 3 + t - 5, 6 + (t - 1) % 2)
                        batches(pe, body, peel=True)

                        pe.wait_ge(out_free, B + 2)
                        for kind in range(2):
                            for a in range(2):
                                for j in range(4):
                                    last = nc.tensor.matmul(
                                        ps[:, 2 * kind + a, 0:HALF], sel[:, kind, j, :],
                                        outs[:, j, 8 * a:8 * a + 8, :].rearrange("p b s -> p (b s)"),
                                        start=(j == 0), stop=(j == 3))
                                last.then_inc(summed, 1)

                    @block.scalar
                    def _(act):
                        early_hi(act, 1)
                        early_hi(act, 2)
                        early_mid(act, 1)
                        early_mid(act, 2)
                        deviation(act, named)
                        first.take_turned(act)
                        for m in range(3, 6):
                            early_hi(act, m)
                            early_mid(act, m)
                        for n in range(3):
                            act.wait_ge(early_done, 7 + n)
                            v_evacuate(nc.scalar.copy, 0, n, 4 + n).then_inc(v0_ready, 1)

                        def body(b, u, i, load, k_next, v_next):
                            for t in range(KT):
                                if t == 0:
                                    act.wait_ge(shift_ready, b + 1)
                                act.wait_ge(scores_done, KT * b + t + 1)
                                act.wait_ge(probs_free, KT * b + t + 1)
                                s = 2 * (t % 2)
                                nc.scalar.activation(probs[t % 3][:, :, :], ps[:, s:s + 2, 0:HALF], ACT.Exp,
                                                     bias=shift[u][:, 0:1]).then_inc(exp_done, 1)
                        batches(act, body)

                    @block.vector
                    def _(dve):
                        def k_unit(u, n, m, count, bank):
                            dve.wait_ge(proj_done, m + 1)
                            k_split(dve, u, n, bank, count, k_names)
                            dve.sem_inc(bank_read, 1)

                        def largest_k(b, u):
                            dve.wait_ge(k_ready, 3 * b - 3)
                            nc.vector.tensor_reduce(k_max[u][:, :], k_part[u][:, 0, 0:SK], AX.X, ALU.max,
                                                    apply_absolute_value=True).then_inc(kmax_ready, 1)

                        def early_largest_k(b):
                            dve.wait_ge(hi0, 3 * b + 3)
                            nc.vector.tensor_reduce(k_max[b][:, :], k_part[b][:, 0, 0:SK], AX.X, ALU.max,
                                                    apply_absolute_value=True).then_inc(kmax_ready, 1)

                        def bound_terms(b, u):
                            dve.wait_ge(kmax_ready, b + 1)
                            nc.vector.tensor_scalar(terms[:, :], c("head2"), k_max[u][:, 0:1],
                                                    q_max[:, bass.ds(b, 1)], ALU.mult, ALU.mult)\
                                     .then_inc(terms_ready, 1)

                        def take_bound(b, u):
                            dve.wait_ge(bound_done, b + 1)
                            nc.vector.tensor_reduce(bound[:, :], ps[:, 4 + u, 256:256 + H], AX.X, ALU.max)\
                                     .then_inc(bound_ready, 1)
                            dve.wait_ge(bound_ready, b + 1)
                            nc.vector.tensor_tensor(worst[:, :], worst[:, :], bound[:, :], ALU.max)\
                                     .then_inc(worst_ready, 1)
                            nc.vector.tensor_scalar(shift[u][:, :], bound[:, :], -1.01, HEADROOM, ALU.mult, ALU.add)\
                                     .then_inc(shift_ready, 1)

                        def evacuate(b, u):
                            dve.wait_ge(probs_free, KT * b + KT + 3)
                            nc.vector.tensor_copy(outs[:, :, bass.ds(b, 1), :].rearrange("p j b s -> p j (b s)"),
                                                  ps[:, 4 + u, 0:4 * S].rearrange("p (j s) -> p j s", s=S))\
                                     .then_inc(out_free, 1)
                        dve.sem_inc(bank_read, 2)
                        dve.sem_inc(out_free, 2)
                        first.normalise(dve)
                        early_largest_k(0)
                        for a in range(2):
                            dve.wait_ge(q_projected, a + 1)
                            nc.vector.tensor_scalar(q[:, 8 * a:8 * a + 8, :].rearrange("p b s -> p (b s)"),
                                                    ps[:, a, 0:HALF], bias[:, BQ2:BQ2 + 1], SCALE,
                                                    ALU.add, ALU.mult).then_inc(q_ready, 1)

                        def split_q(chunk):
                            a, z = Q_CHUNKS[chunk]
                            halves = [(slice(64 * h, 64 * h + 64), h) for h in range(2)]
                            for rows_, h in halves:
                                nc.vector.tensor_copy(q_wide[rows_, 0, a:z, h, :], q[rows_, a:z, :]).then_inc(q_hi, 1)
                            dve.wait_ge(q_hi, 2 * chunk + 2)
                            for rows_, h in halves:
                                nc.vector.tensor_tensor(q_rest[rows_, a:z, :], q[rows_, a:z, :],
                                                        q_wide[rows_, 0, a:z, h, :], ALU.subtract).then_inc(q_restr, 1)
                            dve.wait_ge(q_restr, 2 * chunk + 2)
                            for rows_, h in halves:
                                nc.vector.tensor_copy(q_wide[rows_, 1, a:z, h, :], q_rest[rows_, a:z, :])\
                                         .then_inc(q_mid, 1)
                            dve.wait_ge(q_mid, 2 * chunk + 2)
                            for rows_, h in halves:
                                nc.vector.tensor_tensor(q_wide[rows_, 2, a:z, h, :], q_rest[rows_, a:z, :],
                                                        q_wide[rows_, 1, a:z, h, :], ALU.subtract).then_inc(q_lo, 1)

                        dve.wait_ge(q_ready, 2)
                        split_q(0)
                        nc.vector.tensor_reduce(q_max[:, :], q, AX.X, ALU.max, apply_absolute_value=True)\
                                 .then_inc(qmax_ready, 1)
                        dve.wait_ge(qmax_ready, 1)
                        bound_terms(0, 0)
                        take_bound(0, 0)
                        split_q(1)
                        early_largest_k(1)

                        def body(b, u, i, load, k_next, v_next, first=False):
                            if not first:
                                evacuate(b - 1, 1 - u)
                            if v_next:
                                bound_terms(b + 1, 1 - u)
                                for n in range(3):
                                    dve.wait_ge(proj_done, 6 * b + 1 + n)
                                    v_evacuate(nc.vector.tensor_copy, 1 - u, n, 6 + (n + 1) % 2).then_inc(v_ready, 1)
                                    dve.wait_ge(v_ready, 3 * b + 1 + n)
                                    dve.sem_inc(bank_read, 1)
                                take_bound(b + 1, 1 - u)
                            if k_next:
                                for n in range(3):
                                    if n == 0:
                                        dve.wait_ge(kstack_in[u], 16 * len(K_PART) * (i + 1))
                                    k_unit(u, n, 6 * b + 3 + n, 3 * b + n, 6 + n % 2)
                                largest_k(b + 2, u)
                        body(0, 0, 0, True, True, True, first=True)
                        body(1, 1, 0, True, True, True)
                        with dve.Fori(1, LOOP // 2) as i:
                            for u in range(2):
                                body(2 * i + u, u, i, True, True, True)
                        for b in range(LOOP, B):
                            body(b, b % 2, b // 2, b + 3 < B, b + 2 < B, b + 1 < B)
                        evacuate(B - 1, 1)

                        for a in range(2):
                            cols = slice(a * HALF, (a + 1) * HALF)
                            dve.wait_ge(summed, 3 + a)
                            nc.vector.reciprocal(inv[:, cols], ps[:, 2 + a, 0:HALF]).then_inc(inv_ready, 1)
                            dve.wait_ge(inv_ready, a + 1)
                            nc.vector.tensor_tensor(num[:, cols], ps[:, a, 0:HALF], inv[:, cols], ALU.mult)\
                                     .then_inc(prod_ready, 1)
                            dve.wait_ge(prod_ready, a + 1)
                            nc.vector.tensor_scalar(att[:, cols], num[:, cols], bias[:, BV2:BV2 + 1], None,
                                                    ALU.add).then_inc(att_ready, 1)

            bad = sx("bad", [P, 2])
            flag_f = sx("flag_f", [P, 1])
            bad_ready = sem("bad_ready")
            counted = sem("counted")
            flag_ready = sem("flag_ready")
            with nc.Block() as block:
                @block.vector
                def _(dve):
                    nc.vector.tensor_scalar(bad[:, 0:1], worst[:, :], GUARD, None, ALU.is_le).then_inc(bad_ready, 1)
                    nc.vector.tensor_scalar(bad[:, 1:2], mask_max[:, :], 0.0, None, ALU.is_equal)\
                             .then_inc(bad_ready, 1)
                    dve.wait_ge(counted, 1)
                    nc.vector.tensor_reduce(flag_f[:, :], ps[:, 0, 0:2], AX.X, ALU.min).then_inc(flag_ready, 1)
                    dve.wait_ge(flag_ready, 1)
                    nc.vector.tensor_scalar(flag[:, :], flag_f[:, :], P - 0.5, None, ALU.is_lt)\
                             .then_inc(flag_ready, 1)
                    dve.wait_ge(flag_ready, 2)

                @block.tensor
                def _(pe):
                    pe.wait_ge(bad_ready, 2)
                    nc.tensor.matmul(ps[:, 0, 0:2], ones[:, :], bad[:, :], start=True, stop=True)\
                             .then_inc(counted, 1)
            return flag, k_stack, k_split

        def general_cross_attention(shared):
            _, k_stack, k_split = shared
            with ExitStack() as st:
                sg = tensors(st)
                mask_sb = sg("mask_g", [PQ, SK])
                s_all = sg("s_all", [PQ, SK])
                p_t = sg("p_t_g", [KW, KT, PQ])
                row_max = sg("row_max_g", [PQ, 1])
                total = sg("total_g", [PQ, 1])
                zero_total = sg("zero_total_g", [PQ, 1])
                zero_ready = sem("zero_ready_g")
                inv = sg("inv_g", [PQ, 1])
                picked = sg("picked_g", [16, 2, S])
                folded = sg("folded_g", [16, S])
                scratch = nc.dram_tensor("attention_scratch", [P, TOK], F32).ap()

                mask_in = sem("mask_in_g")
                ctx_g = sem("ctx_in_g")
                proj = sem("proj_done_g")
                k_hi, k_restr, k_mid, k_ready, v_ready = (sem(f"{n}_g") for n in
                                                          ("k_hi", "k_rest", "k_mid", "k_parts", "values"))
                stack_in = sem("kstack_in_g")
                scores_done = sem("scores_done_g")
                masked = sem("masked_g")
                max_ready = sem("max_ready_g")
                exp_done = sem("exp_done_g")
                inv_ready = sem("inv_ready_g")
                scaled = sem("scaled_g")
                turned = sem("turned_g")
                p_t_ready = sem("p_t_ready_g")
                pv_done = sem("pv_done_g")
                picked_ready = sem("picked_ready_g")
                folded_ready = sem("folded_ready_g")
                stored = sem("stored_g")
                back_in = sem("attention_back")
                bias_added = sem("bias_added_g")
                names = (k_hi, k_restr, k_mid, None, k_ready)

                v_flat = values[0][0:KW, :, 0:P]

                with nc.Block() as block:
                    @block.sync
                    def _(sp):
                        sp.dma_start(mask_sb[:, :], mask).then_inc(mask_in, 16)

                        def body(b):
                            def held(value):
                                return value if isinstance(value, int) else sp.snap(value)

                            attended, parts_made = held(PAIRS * b), held(3 * b + 3)
                            columns = held(b * S)
                            folds = [held(PAIRS * b + p + 1) for p in range(PAIRS)]
                            if not isinstance(b, int):
                                sp.wait_ge(pv_done, attended)
                            sp.dma_start(ctx_buf[0][:, :], ctx_t[bass.ds(b, 1)].rearrange("a d k -> d (a k)"))\
                              .then_inc(ctx_g, 16)
                            sp.wait_ge(k_ready, parts_made)
                            for n, part in enumerate(K_PART):
                                sp.dma_start(k_stack[0][16 * n:16 * n + 16, :, :], k_part[0][:, part, :])\
                                  .then_inc(stack_in, 16)
                            for p in range(PAIRS):
                                sp.wait_ge(folded_ready, folds[p])
                                sp.dma_start(scratch[16 * p:16 * p + 16, bass.ds(columns, S)], folded[:, :])\
                                  .then_inc(stored, 16)
                        body(0)
                        with sp.Fori(1, B) as b:
                            body(b)
                        sp.wait_ge(stored, 16 * PAIRS * B)
                        sp.dma_start(att[:, :], scratch).then_inc(back_in, 16)

                    @block.gpsimd
                    def _(pool):
                        nc.gpsimd.memset(zero_total[:, :], 0.0).then_inc(zero_ready, 1)

                    @block.tensor
                    def _(pe):
                        def body(b):
                            pe.wait_ge(ctx_g, 16 * b + 16)
                            for n in range(3):
                                if n == 2 or not isinstance(b, int):
                                    pe.wait_ge(k_ready, 3 * b + n - 1 if n < 2 else 3 * b + 1)
                                nc.tensor.matmul(ps[:, 6 + n % 2, 0:KC], wts[:, WK2, :],
                                                 ctx_buf[0][:, n * KC:(n + 1) * KC],
                                                 start=True, stop=True).then_inc(proj, 1)
                            for n in range(3):
                                if n == 0:
                                    pe.wait_ge(k_ready, 3 * b + 3)
                                if n == 2:
                                    pe.wait_ge(v_ready, 3 * b + 1)
                                for t in range(4 * n, 4 * n + 4):
                                    last = nc.tensor.matmul(ps[0:KW, 6 + n % 2, (t % 4) * P:(t % 4 + 1) * P],
                                                            ctx_buf[0][:, t * KW:(t + 1) * KW], wts[:, WV2, :],
                                                            start=True, stop=True)
                                last.then_inc(proj, 1)
                            pe.wait_ge(stack_in, 16 * len(K_PART) * (b + 1))
                            for p in range(PAIRS):
                                j = PAIRS * b + p
                                if p or not isinstance(b, int):
                                    pe.wait_ge(masked, j)
                                for n in range(NKC):
                                    last = nc.tensor.matmul(ps[0:PQ, n, 0:KC],
                                                            q_stack[:, p, bass.ds(b * PQ, PQ)],
                                                            k_stack[0][:, p, n * KC:(n + 1) * KC],
                                                            start=True, stop=True)
                                last.then_inc(scores_done, 1)
                                pe.wait_ge(scaled, j + 1)
                                for t in range(KT):
                                    last = nc.tensor.transpose(ps[0:KW, 3 + t // 4, (t % 4) * PQ:(t % 4 + 1) * PQ],
                                                               s_all[:, t * KW:(t + 1) * KW], eye[0:PQ, 0:PQ])
                                last.then_inc(turned, 1)
                                pe.wait_ge(p_t_ready, j + 1)
                                pe.wait_ge(v_ready, 3 * b + 3)
                                for t in range(KT):
                                    last = nc.tensor.matmul(
                                        ps[0:16, 6, 0:PQ],
                                        v_pair(p, t), p_t[:, t, :], start=(t == 0), stop=(t == KT - 1))
                                last.then_inc(pv_done, 1)
                                pe.wait_ge(picked_ready, j + 1)

                        def v_pair(p, t):
                            return v_flat[:, t, 16 * p:16 * p + 16]
                        body(0)
                        with pe.Fori(1, B) as b:
                            body(b)

                    @block.scalar
                    def _(act):
                        def body(b):
                            for p in range(PAIRS):
                                act.wait_ge(max_ready, PAIRS * b + p + 1)
                                nc.scalar.activation(s_all[:, :], s_all[:, :], ACT.Exp, bias=row_max[:, 0:1],
                                                     accum_out=total[:, 0:1]).then_inc(exp_done, 1)
                        body(0)
                        with act.Fori(1, B) as b:
                            body(b)

                    @block.vector
                    def _(dve):
                        dve.wait_ge(mask_in, 16)
                        diag = c("diag").rearrange("p (h s) -> p h s", h=2)

                        def body(b):
                            if not isinstance(b, int):
                                dve.wait_ge(stack_in, 16 * len(K_PART) * b)
                            for n in range(3):
                                dve.wait_ge(proj, 6 * b + n + 1)
                                k_split(dve, 0, n, 6 + n % 2, 3 * b + n, names)
                            for n in range(3):
                                dve.wait_ge(proj, 6 * b + 4 + n)
                                nc.vector.tensor_copy(values[0][0:KW, 4 * n:4 * n + 4, 0:P],
                                                      ps[0:KW, 6 + n % 2, :].rearrange("p (t m) -> p t m", t=4))\
                                         .then_inc(v_ready, 1)
                            for p in range(PAIRS):
                                j = PAIRS * b + p
                                dve.wait_ge(scores_done, j + 1)
                                nc.vector.tensor_tensor(s_all[:, :].rearrange("p (n k) -> p n k", k=KC),
                                                        ps[0:PQ, 0:NKC, 0:KC],
                                                        mask_sb[:, :].rearrange("p (n k) -> p n k", k=KC),
                                                        ALU.add).then_inc(masked, 1)
                                dve.wait_ge(masked, j + 1)
                                nc.vector.tensor_reduce(row_max[:, :], s_all[:, :], AX.X, ALU.max, negate=True)\
                                         .then_inc(max_ready, 1)
                                dve.wait_ge(exp_done, j + 1)
                                nc.vector.reciprocal(inv[:, :], total[:, :]).then_inc(inv_ready, 1)
                                dve.wait_ge(inv_ready, j + 1)
                                nc.vector.tensor_scalar(s_all[:, :], s_all[:, :], inv[:, 0:1], None, ALU.mult)\
                                         .then_inc(scaled, 1)
                                dve.wait_ge(turned, j + 1)
                                nc.vector.tensor_copy(p_t[:, :, :].rearrange("p (a n) m -> p a (n m)", a=3),
                                                      ps[0:KW, 3:6, 0:4 * PQ]).then_inc(p_t_ready, 1)
                                dve.wait_ge(pv_done, j + 1)
                                if p or not isinstance(b, int):
                                    dve.wait_ge(stored, 16 * j)
                                nc.vector.tensor_tensor(picked[:, :, :],
                                                        ps[0:16, 6, 0:PQ].rearrange("p (h s) -> p h s", h=2),
                                                        diag[0:16], ALU.mult).then_inc(picked_ready, 1)
                                dve.wait_ge(picked_ready, j + 1)
                                nc.vector.tensor_tensor(folded[:, :], picked[:, 0, :], picked[:, 1, :], ALU.add)\
                                         .then_inc(folded_ready, 1)
                        body(0)
                        with dve.Fori(1, B) as b:
                            body(b)
                        dve.wait_ge(back_in, 16)
                        nc.vector.tensor_scalar(att[:, :], att[:, :], bias[:, BV2:BV2 + 1], None, ALU.add)\
                                 .then_inc(bias_added, 1)

        def feed_forward(w_exp, w1_part, xt_part):
            with ExitStack() as st:
                sf = tensors(st)
                hid = [sf(f"hid_{u}", [P, FC, TOK]) for u in range(3)]
                acc = sf("acc", [P, NT, P])
                rt = sf("router", [P, E])
                b2_sb = sf("b2", [NE, P])
                logit = sf("logit", [P, NT, E])
                best = sf("best", [P, NT, 1])
                prob = sf("prob", [P, NT, E])
                total = sf("total", [P, NT, 1])
                hit = sf("hit", [P, NT, E])
                first = sf("first", [P, NT, E])
                comb = sf("comb", [P, NT, NE])
                comb_t = sf("comb_t", [NE, NT, P])
                named = norm_names("out", sf)

                small_in = sem("small_in")
                logits_done = sem("logits_done")
                chain = sem("router_steps")
                exp_done = sem("router_exp_done")
                comb_ready = sem("comb_ready")
                comb_turned = sem("comb_turned")
                comb_t_ready = sem("comb_t_ready")
                b2_done = sem("b2_done")
                acc_start = sem("acc_start")
                w1_split = sem("w1_split")
                up_done = sem("up_done")
                gelu_done = sem("gelu_done")
                down_done = sem("down_done")
                acc_done = sem("acc_done")
                stored = sem("stored")

                with nc.Block() as block:
                    @block.sync
                    def _(sp):
                        sp.dma_start(rt[:, :], router_t).then_inc(small_in, 16)
                        sp.dma_start(b2_sb[:, :], b2).then_inc(small_in, 16)
                        with sp.Fori(0, NE // 3 - 1) as i:
                            for r in range(3):
                                network = sp.snap(3 * i + r + 3)
                                read = sp.snap(6 * i + 2 * r + 2)
                                sp.wait_ge(down_done, read)
                                sp.dma_start(w_exp[r][:, :], experts[bass.ds(network, 1)]
                                             .rearrange("a p n -> p (a n)")).then_inc(expert_in[r], 16)
                        for n, (a, z) in enumerate(((0, 4), (4, NT))):
                            sp.wait_ge(named["normal_ready"], z)
                            sp.dma_start(out[a * P:z * P].rearrange("(t p) d -> p t d", p=P), xn[:, a:z, :])\
                              .then_inc(stored, 16)
                        sp.wait_ge(stored, 32)

                    @block.tensor
                    def _(pe):
                        pe.wait_ge(small_in, 32)
                        for t in range(NT):
                            last = nc.tensor.matmul(ps[:, 7, t * E:(t + 1) * E], xt[:, t * P:(t + 1) * P], rt[:, :],
                                                    start=True, stop=True)
                        last.then_inc(logits_done, 1)

                        def up(e, r, i):
                            pe.wait_ge(w1_split, 2 * e + 2)
                            for n in range(2 * FC):
                                f, a = n // 2, n % 2
                                if n >= 4 or not isinstance(e, int) or e >= 1:
                                    pe.wait_ge(gelu_done, 8 * e + n - 3)
                                for w, x_ in PARTS:
                                    last = nc.tensor.matmul(ps[:, n % 4, 0:HALF],
                                                            w1_part[r][:, w, f * P:(f + 1) * P],
                                                            xt_part[:, x_, a * HALF:(a + 1) * HALF],
                                                            start=(w + x_ == 0), stop=(w == 1))
                                last.then_inc(up_done, 1)

                        def down(e, r):
                            pe.wait_ge(gelu_done, 8 * e + 8)
                            for n, (a, z) in enumerate(((0, 4), (4, NT))):
                                if n == 0:
                                    if isinstance(e, int) and e == 0:
                                        pe.wait_ge(acc_start, 1)
                                    else:
                                        pe.wait_ge(acc_done, 2 * e - 1)
                                elif not (isinstance(e, int) and e == 0):
                                    pe.wait_ge(acc_done, 2 * e)
                                for t in range(a, z):
                                    for f in range(FC):
                                        last = nc.tensor.matmul(
                                            ps[:, 4 + n, (t - a) * P:(t - a + 1) * P],
                                            hid[r][:, f, t * P:(t + 1) * P],
                                            w_exp[r][:, W2_AT + f * P:W2_AT + (f + 1) * P],
                                            start=(f == 0), stop=(f == FC - 1))
                                last.then_inc(down_done, 1)

                        up(0, 0, 0)
                        pe.wait_ge(comb_ready, 1)
                        for t in range(NT):
                            last = nc.tensor.transpose(ps[0:NE, 4 + t // 4, (t % 4) * P:(t % 4 + 1) * P],
                                                       comb[:, t, :], eye)
                        last.then_inc(comb_turned, 1)
                        pe.wait_ge(comb_t_ready, 1)
                        for t in range(NT):
                            last = nc.tensor.matmul(ps[:, 4 + t // 4, (t % 4) * P:(t % 4 + 1) * P],
                                                    comb_t[:, t, :], b2_sb[:, :], start=True, stop=True)
                        last.then_inc(b2_done, 1)
                        up(1, 1, 0)
                        down(0, 0)
                        up(2, 2, 0)
                        down(1, 1)
                        with pe.Fori(1, NE // 3) as i:
                            for r in range(3):
                                up(3 * i + r, r, i)
                                down(3 * i + r - 1, (r + 2) % 3)
                        down(NE - 1, 2)

                    @block.gpsimd
                    def _(pool):
                        def split(e, r, i):
                            if not (isinstance(e, int) and e < 3):
                                pool.wait_ge(up_done, 8 * e - 16)
                            pool.wait_ge(expert_in[r], 16 * (i + 1))
                            split_r(pool, w_exp[r][:, W1_AT:W1_AT + F], w1_part[r][:, 0, :], w1_part[r][:, 1, :],
                                    w1_split, 2 * e)
                        for r in range(3):
                            split(r, r, 0)
                        with pool.Fori(1, NE // 3) as i:
                            for r in range(3):
                                split(3 * i + r, r, i)

                    @block.scalar
                    def _(act):
                        act.wait_ge(chain, 3)
                        nc.scalar.activation(prob[:, :, :], logit[:, :, :], ACT.Exp).then_inc(exp_done, 1)

                        def gelu(e, r, i):
                            for n in range(2 * FC):
                                f, a = n // 2, n % 2
                                act.wait_ge(up_done, 8 * e + n + 1)
                                if n == 0 and not (isinstance(e, int) and e < 3):
                                    act.wait_ge(down_done, 2 * e - 4)
                                nc.scalar.activation(hid[r][:, f, a * HALF:(a + 1) * HALF], ps[:, n % 4, 0:HALF],
                                                     ACT.Gelu_apprx_tanh,
                                                     bias=w_exp[r][:, B1_AT + f:B1_AT + f + 1]).then_inc(gelu_done, 1)
                        for r in range(3):
                            gelu(r, r, 0)
                        with act.Fori(1, NE // 3) as i:
                            for r in range(3):
                                gelu(3 * i + r, r, i)
                        deviation(act, named)

                    @block.vector
                    def _(dve):
                        steps = [0]

                        def step(ins):
                            ins.then_inc(chain, 1)
                            steps[0] += 1
                            dve.wait_ge(chain, steps[0])

                        def wide(a):
                            return a[:, :, :].to_broadcast([P, NT, E])

                        dve.wait_ge(logits_done, 1)
                        step(nc.vector.tensor_tensor(logit[:, :, :], ps[:, 7, 0:NT * E].rearrange("p (t e) -> p t e", e=E),
                                                     row[:, ROW_RB:ROW_RB + E].unsqueeze(1).to_broadcast([P, NT, E]),
                                                     ALU.add))
                        step(nc.vector.tensor_reduce(best[:, :, 0], logit[:, :, :], AX.X, ALU.max))
                        step(nc.vector.tensor_tensor(logit[:, :, :], logit[:, :, :], wide(best), ALU.subtract))
                        dve.wait_ge(exp_done, 1)
                        step(nc.vector.tensor_reduce(total[:, :, 0], prob[:, :, :], AX.X, ALU.add))
                        step(nc.vector.reciprocal(best[:, :, :], total[:, :, :]))
                        step(nc.vector.tensor_tensor(prob[:, :, :], prob[:, :, :], wide(best), ALU.mult))
                        down_ = c("down").unsqueeze(1).to_broadcast([P, NT, E])

                        def pick(left, into):
                            step(nc.vector.tensor_reduce(best[:, :, 0], left[:, :, :], AX.X, ALU.max))
                            step(nc.vector.tensor_tensor(hit[:, :, :], left[:, :, :], wide(best), ALU.is_equal))
                            step(nc.vector.tensor_tensor(hit[:, :, :], hit[:, :, :], down_, ALU.mult))
                            step(nc.vector.tensor_reduce(best[:, :, 0], hit[:, :, :], AX.X, ALU.max))
                            step(nc.vector.tensor_tensor(into[:, :, :], hit[:, :, :], wide(best), ALU.is_equal))

                        pick(prob, first)
                        step(nc.vector.scalar_tensor_tensor(out=logit[:, :, :], in0=first[:, :, :], scalar=-2.0,
                                                            in1=prob[:, :, :], op0=ALU.mult, op1=ALU.add))
                        pick(logit, hit)
                        step(nc.vector.tensor_tensor(first[:, :, :], first[:, :, :], hit[:, :, :], ALU.add))
                        step(nc.vector.tensor_tensor(prob[:, :, :], prob[:, :, :], first[:, :, :], ALU.mult))
                        step(nc.vector.tensor_reduce(total[:, :, 0], prob[:, :, :], AX.X, ALU.add))
                        step(nc.vector.reciprocal(best[:, :, :], total[:, :, :]))
                        step(nc.vector.memset(comb[:, :, E:NE], 1.0))
                        nc.vector.tensor_tensor(comb[:, :, 0:E], prob[:, :, :], wide(best), ALU.mult)\
                                 .then_inc(comb_ready, 1)
                        dve.wait_ge(comb_turned, 1)
                        step(nc.vector.tensor_copy(comb_t[:, 0:4, :].rearrange("p t m -> p (t m)"), ps[0:NE, 4, :]))
                        nc.vector.tensor_copy(comb_t[:, 4:NT, :].rearrange("p t m -> p (t m)"), ps[0:NE, 5, 0:3 * P])\
                                 .then_inc(comb_t_ready, 1)
                        dve.wait_ge(b2_done, 1)
                        step(nc.vector.tensor_tensor(acc[:, 0:4, :], ps[:, 4, :].rearrange("p (t d) -> p t d", d=P),
                                                     xn[:, 0:4, :], ALU.add))
                        nc.vector.tensor_tensor(acc[:, 4:NT, :], ps[:, 5, 0:3 * P].rearrange("p (t d) -> p t d", d=P),
                                                xn[:, 4:NT, :], ALU.add).then_inc(acc_start, 1)
                        dve.wait_ge(acc_start, 1)

                        def add(e, last=False):
                            for n, (a, z) in enumerate(((0, 4), (4, NT))):
                                dve.wait_ge(down_done, 2 * e + n + 1)
                                if not (isinstance(e, int) and e == 0):
                                    dve.wait_ge(acc_done, 2 * e + n - 1)
                                for t in range(a, z):
                                    ins = nc.vector.scalar_tensor_tensor(
                                        out=acc[:, t, :], in0=ps[:, 4 + n, (t - a) * P:(t - a + 1) * P],
                                        scalar=comb[:, t, bass.ds(e, 1)], in1=acc[:, t, :],
                                        op0=ALU.mult, op1=ALU.add)
                                ins.then_inc(acc_done, 1)
                                if last:
                                    dve.wait_ge(acc_done, 2 * e + n + 1)
                                    dve.sem_inc(named["y_ready"], 1)
                        add(0)
                        with dve.Fori(1, NE - 1) as e:
                            add(e)
                        add(NE - 1, last=True)
                        normalise(dve, named, acc, xn)

        self_attention()
        with ExitStack() as cross:
            shared = cross_attention(cross)
            again = nc.values_load(shared[0][0:1, 0:1], min_val=0, max_val=1)
            with nc.If(again > 0):
                general_cross_attention(shared)
        attention_memory.close()
        w_exp = [sb(f"w_exp_{r}", [P, NW]) for r in range(3)]
        w1_part = [sb(f"w1_part_{r}", [P, 2, F], F32R) for r in range(3)]
        xt_part = sb("xt_part", [P, 2, TOK], F32R)
        with ExitStack() as st:
            y, named = tensors(st)("y_cross", [P, NT, P]), norm_names("cross", tensors(st))
            second = Projection("cross", WO2, y, named)
            with nc.Block() as block:
                @block.sync
                def _(sp):
                    for r in range(3):
                        sp.dma_start(w_exp[r][:, :], experts[r]).then_inc(expert_in[r], 16)

                @block.tensor
                def _(pe):
                    second.multiply()
                    second.turn(pe)

                @block.scalar
                def _(act):
                    deviation(act, named)
                    second.take_turned(act, xt_part[:, 0, :])

                @block.vector
                def _(dve):
                    second.normalise(dve)
                    for n, (a, z) in enumerate(PARTS_OF_X):
                        dve.wait_ge(second.xt_ready, n + 1)
                        dve.wait_ge(second.hi_ready, n + 1)
                        nc.vector.tensor_tensor(xt_part[:, 1, a * P:z * P], xt[:, a * P:z * P],
                                                xt_part[:, 0, a * P:z * P].bitcast(F32), ALU.subtract)\
                                 .then_inc(second.lo_ready, 1)
        feed_forward(w_exp, w1_part, xt_part)


def kernel(x, ctx_1024, mask_1x1xSxS2_ff0, L0_attn_Wq, L0_attn_bq, L0_attn_Wk, L0_attn_bk, L0_attn_Wv,
           L0_attn_bv, L0_attn_Wo, L0_attn_bo, L0_attn_slopes, L0_xattn_Wq, L0_xattn_bq, L0_xattn_Wk,
           L0_xattn_bk, L0_xattn_Wv, L0_xattn_bv, L0_xattn_Wo, L0_xattn_bo, L0_ffn_shared_w1,
           L0_ffn_shared_b1, L0_ffn_shared_w2, L0_ffn_shared_b2, L0_ffn_router_w, L0_ffn_router_b,
           L0_ffn_spec_w1, L0_ffn_spec_b1, L0_ffn_spec_w2, L0_ffn_spec_b2):
    import concourse.bacc as bacc
    from concourse.bass_utils import run_bass_kernel_spmd

    def of(a):
        return np.asarray(a)

    order = np.array([(2 * (p % PAIRS) + p // 64) * DH + (p // PAIRS) % DH for p in range(P)])
    x2 = of(x).reshape(TOK, P)
    wq2, wk2 = of(L0_xattn_Wq)[order], of(L0_xattn_Wk)[order]
    w_t = np.stack([of(w).T for w in (L0_attn_Wq, L0_attn_Wk, L0_attn_Wv, L0_attn_Wo, wq2, wk2,
                                      L0_xattn_Wv, L0_xattn_Wo)], 1)
    bias_cols = np.stack([of(L0_attn_bq), of(L0_attn_bk), of(L0_attn_bv), of(L0_xattn_bq)[order],
                          of(L0_xattn_bk)[order], of(L0_xattn_bv)], 1)
    rows = np.concatenate([of(L0_attn_bo), of(L0_xattn_bo), of(L0_ffn_router_b), of(L0_attn_slopes)])
    w1 = np.concatenate([of(L0_ffn_spec_w1), of(L0_ffn_shared_w1)[None]])
    w2 = np.concatenate([of(L0_ffn_spec_w2), of(L0_ffn_shared_w2)[None]])
    b1 = np.concatenate([of(L0_ffn_spec_b1), of(L0_ffn_shared_b1)[None]])
    b2 = np.concatenate([of(L0_ffn_spec_b2), of(L0_ffn_shared_b2)[None]])
    experts = np.concatenate([
        w1.transpose(0, 2, 1),
        w2.transpose(0, 2, 1).reshape(NE, FC, P, P).transpose(0, 2, 1, 3).reshape(NE, P, F),
        b1.reshape(NE, FC, P).transpose(0, 2, 1)], 2)
    arrays = {
        "x": x2, "x_t": x2.T, "ctx_t": of(ctx_1024).transpose(0, 2, 1),
        "mask": np.tile(of(mask_1x1xSxS2_ff0).reshape(S, SK), (2, 1)),
        "w_t": w_t, "bias_cols": bias_cols, "rows": np.tile(rows[None], (P, 1)),
        "router_t": of(L0_ffn_router_w).T, "experts": experts, "b2": b2, "constants": CONSTANTS,
    }
    arrays = {f"in_{n}": np.ascontiguousarray(a) for n, a in arrays.items()}
    nc = bacc.Bacc("TRN2", target_bir_lowering=False, num_devices=1)
    args = [nc.dram_tensor(n, a.shape, mybir.dt.from_np(a.dtype), kind="ExternalInput").ap()
            for n, a in arrays.items()]
    out = nc.dram_tensor("out_0", (TOK, P), F32, kind="ExternalOutput").ap()
    build(nc, *args, out)
    r = run_bass_kernel_spmd(nc, [arrays], core_ids=[0])
    return r.results[0]["out_0"].reshape(B, S, P)
```

```python
from contextlib import ExitStack

import numpy as np

import concourse.bass as bass
from concourse import mybir

ALU = mybir.AluOpType
ACT = mybir.ActivationFunctionType
AX = mybir.AxisListType
F32 = mybir.dt.float32
F32R = mybir.dt.float32r
BF16 = mybir.dt.bfloat16
I32 = mybir.dt.int32

P = 128
B = 16
S = 56
TOK = B * S
NT = TOK // P
HALF = TOK // 2
H = 16
DH = P // H
PAIRS = H // 2
PQ = 2 * S
SK = 1500
KW = 125
KT = SK // KW
KC = 500
NKC = SK // KC
SKP = SK + 4
VC = DH + 1
VW = H * VC + 24
F = 512
FC = F // P
E = 8
NE = E + 1
EPS = 1e-5
SCALE = float(DH) ** -0.5
K_PART = (0, 1, 0, 1, 2, 0)
Q_PART = (0, 0, 1, 1, 0, 2)
ROWS = 16 * len(K_PART)
HEADROOM = 50.0
GUARD = 54.0


def head_rows(h):
    tile, block = (h // 3, h % 3) if h < 12 else (h - 12, 3)
    return 32 * tile + VC * (block if block < 3 else 0), block


def shape_constants():
    part = np.arange(P)
    eye = np.eye(P, dtype=np.float32)
    head = (part[:, None] // DH == np.arange(H)[None]).astype(np.float32)
    head2 = (2 * (part % PAIRS) + part // (P // 2))[:, None] == np.arange(H)[None]
    dist = np.zeros((P, S), np.float32)
    for at in (0, 64):
        dist[at:at + S] = np.arange(S)[None] - np.arange(S)[:, None]
    own = np.zeros((P, H, DH), np.float32)
    for r in range(PQ):
        own[r, (r // S)::2] = 1
    sel = np.zeros((P, 2, 4, P), np.float32)
    for h in range(H):
        first, block = head_rows(h)
        for d in range(DH):
            sel[first + d, 0, block, h * DH + d] = 1
            sel[first + DH, 1, block, h * DH + d] = 1
    down = np.tile(np.arange(E, 0, -1, dtype=np.float32), (P, 1))
    diag = np.zeros((P, 2, S), np.float32)
    for r in range(16):
        diag[r, r // DH] = 1
    parts = [("eye", eye), ("head", head), ("head2", head2.astype(np.float32)), ("dist", dist),
             ("own", own.reshape(P, -1)), ("sel", sel.reshape(P, -1)), ("down", down),
             ("diag", diag.reshape(P, -1))]
    at, where = 0, {}
    for name, a in parts:
        where[name] = (at, a.shape[1])
        at += a.shape[1]
    return np.concatenate([a for _, a in parts], 1).astype(np.float32), where


CONSTANTS, CONST_AT = shape_constants()
NCONST = CONSTANTS.shape[1]
BQ1, BK1, BV1, BQ2, BK2, BV2 = range(6)
ROW_BO1, ROW_BO2, ROW_RB, ROW_SL = 0, P, 2 * P, 2 * P + E
NROW = 2 * P + E + H
WQ1, WK1, WV1, WO1, WQ2, WK2, WV2, WO2 = range(8)
W1_AT, W2_AT = 0, F
NW = 2 * F


def build(nc, x, x_t, ctx_t, mask, w_t, bias_cols, rows, router_t, experts, b1, b2, constants, out):
    with ExitStack() as top:
        def sem(name):
            return top.enter_context(nc.semaphore(name))

        def tensors(stack):
            return lambda name, shape, dt=F32: stack.enter_context(nc.sbuf_tensor(name, shape, dt))

        sb = tensors(top)
        ps = top.enter_context(nc.psum_tensor("ps", [P, 8, 512], F32))
        const = sb("const", [P, NCONST])
        wts = sb("wts", [P, 8, P])
        bias = sb("bias", [P, 6])
        row = sb("row", [P, NROW])
        xn = sb("xn", [P, NT, P])
        xt = sb("xt", [P, TOK])
        att = sb("att", [P, TOK])
        ones = sb("ones", [P, P])
        eps = sb("eps", [P, 1])

        def c(name):
            at, n = CONST_AT[name]
            return const[:, at:at + n]

        eye = c("eye")
        sel = c("sel").rearrange("p (k j m) -> p k j m", k=2, j=4)

        consts_in = sem("consts_in")
        x_in = sem("x_in")
        ctx_in = [sem("ctx_in_even"), sem("ctx_in_odd")]
        expert_in = [sem(f"expert_in_{i}") for i in range(3)]

        outs = sb("outs", [P, 4, B, S])
        flag = sb("flag", [P, 1], I32)
        big = sb("contexts_or_experts", [P, 3 * NW])
        ctx_buf = [big[:, u * 3 * NW // 2:u * 3 * NW // 2 + SK] for u in range(2)]
        w_exp = [big[:, r * NW:(r + 1) * NW] for r in range(3)]

        attention_memory = top.enter_context(ExitStack())
        sm = tensors(attention_memory)
        ctx_part = sm("ctx_part", [P, 2, SK], F32R)
        wk_part = sm("wk_part", [P, 2, P], F32R)
        k_part = [sm(f"k_part_{u}", [P, 3, SKP], BF16) for u in range(2)]
        values = [sm(f"values_{u}", [P, KT, VW]) for u in range(2)]
        worst = sm("worst", [P, 1])
        k_rest = [sm(f"k_rest_{r}", [P, KC]) for r in range(2)]
        k_full = [sm(f"k_full_{r}", [P, KC]) for r in range(2)]
        mask_max = sm("mask_max", [P, 1])
        q_max = sm("q_max", [P, B])
        q_stack = sm("q_stack", [ROWS, PAIRS, B * PQ], BF16)
        q_wide = sm("q_wide", [P, 3, B, 2, S], BF16)
        ctx_split = sem("ctx_split")
        mask_in = sem("mask_in")

        def split_r(pool, whole, hi, lo, done, count):
            nc.gpsimd.tensor_tensor(hi, whole, ones[:, 0:1].to_broadcast([P, whole.shape[1]]), ALU.mult).then_inc(done, 1)
            pool.wait_ge(done, count + 1)
            nc.gpsimd.tensor_tensor(lo, whole, hi.bitcast(F32), ALU.subtract).then_inc(done, 1)

        PARTS = ((0, 0), (0, 1), (1, 0))

        def load_ctx(sp, b, u):
            sp.dma_start(ctx_buf[u][:, :], ctx_t[bass.ds(b, 1)].rearrange("a d k -> d (a k)"))\
              .then_inc(ctx_in[u], 16)

        def add_output_bias(at):
            return nc.gpsimd.tensor_tensor(xn[:, :, :], xn[:, :, :],
                                           row[:, at:at + P].unsqueeze(1).to_broadcast([P, NT, P]), ALU.add)

        early_done = sem("early_units_done")
        hi0 = sem("early_k_hi")
        rest0 = sem("early_k_rest")
        mid0 = sem("early_k_mid")
        k0_ready = sem("early_k_parts")

        def early_k(pe, m):
            if m % 3 == 0:
                pe.wait_ge(ctx_in[m // 3], 16)
            nc.tensor.matmul(ps[:, 2 + m, 0:KC], wts[:, WK2, :],
                             ctx_buf[m // 3][:, (m % 3) * KC:(m % 3 + 1) * KC],
                             start=True, stop=True).then_inc(early_done, 1)

        def early_hi(act, m):
            act.wait_ge(early_done, m + 1)
            if m >= 2:
                act.wait_ge(k0_ready, m - 1)
            nc.scalar.activation(k_full[m % 2][:, :], ps[:, 2 + m, 0:KC], ACT.Identity,
                                 bias=bias[:, BK2:BK2 + 1])
            nc.scalar.activation(k_part[m // 3][:, 0, (m % 3) * KC:(m % 3 + 1) * KC],
                                 ps[:, 2 + m, 0:KC], ACT.Identity,
                                 bias=bias[:, BK2:BK2 + 1]).then_inc(hi0, 1)

        def early_mid(act, m):
            act.wait_ge(rest0, m + 1)
            nc.scalar.copy(k_part[m // 3][:, 1, (m % 3) * KC:(m % 3 + 1) * KC],
                           k_rest[m % 2][:, :]).then_inc(mid0, 1)

        def early_rest(pool, m):
            if m > 1:
                pool.wait_ge(k0_ready, m - 1)
            pool.wait_ge(hi0, m + 1)
            nc.gpsimd.tensor_tensor(k_rest[m % 2][:, :], k_full[m % 2][:, :],
                                    k_part[m // 3][:, 0, (m % 3) * KC:(m % 3 + 1) * KC],
                                    ALU.subtract).then_inc(rest0, 1)

        def early_lo(pool, m):
            cols = slice((m % 3) * KC, (m % 3 + 1) * KC)
            pool.wait_ge(mid0, m + 1)
            nc.gpsimd.tensor_tensor(k_part[m // 3][:, 2, cols], k_rest[m % 2][:, :],
                                    k_part[m // 3][:, 1, cols], ALU.subtract).then_inc(k0_ready, 1)

        def self_attention():
            with ExitStack() as st:
                sa = tensors(st)
                q = sa("q1", [P, TOK])
                k = sa("k1", [P, TOK])
                alibi = sa("alibi", [P, H, S])
                q_now = [sa(f"q_now1_{u}", [P, 2, 64]) for u in range(2)]
                x_now = [sa(f"x_now1_{u}", [P, 2, 2, S]) for u in range(2)]
                k_heads = [sa(f"k_heads_{u}", [P, 2, H, S]) for u in range(2)]
                sc = [sa(f"sc1_{u}", [P, H, S]) for u in range(2)]
                p_t = [sa(f"p_t_{u}", [PQ, PAIRS, P]) for u in range(2)]
                v_own = [sa(f"v_own_{u}", [PQ, 2, H, VC]) for u in range(2)]
                row_max = [sa(f"row_max1_{u}", [P, H]) for u in range(2)]
                inv = sa("inv1", [P, H])
                o = [sa(f"o1_{u}", [P, P]) for u in range(2)]
                mask_sb = sa("mask_rows", [PQ, SK])

                wk_split = sem("wk_split")
                ones_set = sem("ones_set")
                rest_in = sem("x_rest_in")
                mask_done = sem("mask_max_ready")
                projected = sem("projected1")
                qk_ready = sem("qk_ready1")
                pads_zero = sem("pads_zero1")
                alibi_ready = sem("alibi_ready")
                ones_ready = sem("ones_ready1")
                x_staged = sem("x_staged1")
                q_staged = sem("q_staged1")
                heads_ready = sem("heads_ready1")
                v_done = sem("v_done1")
                v_ready = sem("v_ready1")
                scores_done = sem("scores_done1")
                scores_biased = sem("scores_biased1")
                max_ready = sem("max_ready1")
                shifted = sem("shifted1")
                exp_done = sem("exp_done1")
                turned = sem("turned1")
                p_t_ready = sem("p_t_ready1")
                pv_done = sem("pv_done1")
                inv_ready = sem("inv_ready1")
                normed = sem("normed1")
                o_turned = sem("o_turned1")
                att_ready = sem("att_ready1")

                n_pairs = B // 2

                def sweep(step):
                    def run(eng):
                        for j in range(3):
                            step(j, j % 2)
                        with eng.Fori(1, n_pairs // 2 - 1) as i:
                            for u in range(2):
                                step(2 * i + 1 + u, 1 - u)
                        for j in range(n_pairs - 1, n_pairs + 2):
                            step(j, j % 2)
                    return run

                def there(j, k):
                    return not isinstance(j, int) or 0 <= j + k < n_pairs

                with nc.Block() as block:
                    @block.sync
                    def _(sp):
                        sp.dma_start(wts[:, WQ1:WV1, :], w_t[:, WQ1:WV1, :]).then_inc(x_in, 16)
                        sp.dma_start(xt[:, 0:HALF], x_t[:, 0:HALF]).then_inc(x_in, 16)
                        sp.dma_start(bias[:, :], bias_cols).then_inc(x_in, 16)
                        sp.dma_start(xt[:, HALF:TOK], x_t[:, HALF:TOK]).then_inc(rest_in, 16)
                        sp.dma_start(wts[:, WV1:8, :], w_t[:, WV1:8, :]).then_inc(rest_in, 16)
                        sp.dma_start(const[:, :], constants).then_inc(consts_in, 16)
                        sp.dma_start(row[:, :], rows).then_inc(consts_in, 16)
                        sp.dma_start(xn[:, :, :], x.rearrange("(t p) d -> p t d", p=P)).then_inc(consts_in, 16)
                        sp.dma_start(mask_sb[:, :], mask).then_inc(mask_in, 16)
                        load_ctx(sp, 0, 0)
                        load_ctx(sp, 1, 1)

                    @block.gpsimd
                    def _(pool):
                        for u in range(2):
                            nc.gpsimd.memset(q_now[u][:, :, S:64], 0.0).then_inc(pads_zero, 1)
                        nc.gpsimd.memset(eps[:, :], EPS).then_inc(pads_zero, 1)
                        nc.gpsimd.memset(ones[:, :], 1.0).then_inc(ones_set, 1)
                        pool.wait_ge(ones_set, 1)
                        nc.gpsimd.memset(q_wide[:, :, :, :, :].rearrange("p a b h s -> p (a b h s)"), 0.0)
                        pool.wait_ge(consts_in, 48)
                        pool.wait_ge(qk_ready, 2)

                        def step(j, u):
                            if isinstance(j, int) and j == 1:
                                pool.wait_ge(qk_ready, 4)
                            if there(j, 0):
                                if there(j, -2):
                                    pool.wait_ge(scores_done, j - 1)
                                nc.gpsimd.tensor_copy(q_now[u][:, :, 0:S],
                                                      q[:, bass.ds(j * PQ, PQ)].rearrange("p (b s) -> p b s", b=2))\
                                         .then_inc(q_staged, 1)
                                for b in range(2):
                                    ks = k[:, bass.ds(j * PQ + b * S, S)]
                                    nc.gpsimd.tensor_tensor(k_heads[u][:, b], ks.unsqueeze(1).to_broadcast([P, H, S]),
                                                            c("head").unsqueeze(2).to_broadcast([P, H, S]),
                                                            ALU.mult).then_inc(heads_ready, 1)

                        sweep(step)(pool)
                        add_output_bias(ROW_BO1)

                        split_r(pool, wts[:, WK2, :], wk_part[:, 0, :], wk_part[:, 1, :], wk_split, 0)
                        for u in range(2):
                            nc.gpsimd.memset(k_part[u][:, :, SK:SKP], 0.0)
                            nc.gpsimd.memset(values[u][:, :, H * VC:VW], 0.0)
                            nc.gpsimd.memset(values[u][:, :, 0:H * VC].rearrange("p t (h e) -> p t h e", e=VC)[:, :, :, DH:VC],
                                             1.0)
                        nc.gpsimd.memset(worst[:, :], 0.0)
                        early_rest(pool, 0)
                        early_lo(pool, 0)

                    @block.tensor
                    def _(pe):
                        pe.wait_ge(x_in, 48)
                        for a in range(2):
                            if a == 1:
                                pe.wait_ge(rest_in, 32)
                            for n, w in enumerate((WQ1, WK1)):
                                nc.tensor.matmul(ps[:, 2 * n + a, 0:HALF], wts[:, w, :],
                                                 xt[:, a * HALF:(a + 1) * HALF],
                                                 start=True, stop=True).then_inc(projected, 1)
                        pe.wait_ge(pads_zero, 2)
                        pe.wait_ge(consts_in, 48)

                        def product_v(j, u):
                            pe.wait_ge(x_staged, j + 1)
                            if there(j, -1):
                                pe.wait_ge(v_ready, j)
                            if there(j, -4):
                                pe.wait_ge(att_ready, j - 3)
                            for b in range(2):
                                last = nc.tensor.matmul(ps[0:PQ, 6, b * P:(b + 1) * P],
                                                        x_now[u][:, b].rearrange("p r s -> p (r s)"),
                                                        wts[:, WV1, :], start=True, stop=True)
                            last.then_inc(v_done, 1)

                        def step(j, u):
                            if there(j, 0):
                                pe.wait_ge(q_staged, j + 1)
                                if isinstance(j, int) and j == 0:
                                    pe.wait_ge(qk_ready, 4)
                                pe.wait_ge(heads_ready, 2 * j + 2)
                                if there(j, -2):
                                    pe.wait_ge(scores_biased, j - 1)
                                for a in range(2):
                                    for b in range(2):
                                        last = nc.tensor.matmul(
                                            ps[64 * b:64 * b + 64, 2 * u + a, 0:HALF], q_now[u][:, b, :],
                                            k_heads[u][:, b, a * 8:a * 8 + 8, :].rearrange("p h s -> p (h s)"),
                                            start=True, stop=True)
                                last.then_inc(scores_done, 1)
                            if isinstance(j, int) and j == n_pairs:
                                pe.wait_ge(scores_biased, n_pairs)
                                early_k(pe, 0)
                            if there(j, -1):
                                pe.wait_ge(exp_done, j)
                                for p in range(PAIRS):
                                    if p % 4 == 0 and there(j, -2):
                                        pe.wait_ge(p_t_ready, 2 * j - 3 + p // 4)
                                    last = nc.tensor.transpose(
                                        ps[0:PQ, 4 + p // 4, (p % 4) * P:(p % 4 + 1) * P],
                                        sc[1 - u][:, 2 * p:2 * p + 2, :].rearrange("p h s -> p (h s)"), eye)
                                    if p % 4 == 3:
                                        last.then_inc(turned, 1)
                            if there(j, 1):
                                product_v(j + 1, 1 - u)
                            if there(j, -2):
                                pe.wait_ge(normed, j - 1)
                                if not there(j, 1):
                                    pe.wait_ge(v_ready, n_pairs)
                                    pe.wait_ge(att_ready, j - 2)
                                nc.tensor.transpose(ps[:, 6, 256:384], o[u][:, :], eye).then_inc(o_turned, 1)
                            if there(j, -1):
                                pe.wait_ge(v_ready, j)
                                if there(j, -2):
                                    pe.wait_ge(normed, j - 1)
                                for p in range(PAIRS):
                                    if p % 4 == 0:
                                        pe.wait_ge(p_t_ready, 2 * j - 1 + p // 4)
                                    for b in range(2):
                                        last = nc.tensor.matmul(
                                            ps[64 * b:64 * b + 64, 7, 2 * VC * p:2 * VC * (p + 1)],
                                            p_t[1 - u][:, p, 64 * b:64 * b + 64],
                                            v_own[1 - u][:, b, 2 * p:2 * p + 2, :].rearrange("p h e -> p (h e)"),
                                            start=True, stop=True)
                                last.then_inc(pv_done, 1)
                            if isinstance(j, int) and j == n_pairs:
                                early_k(pe, 1)

                        product_v(0, 0)
                        sweep(step)(pe)
                        pe.wait_ge(p_t_ready, 2 * n_pairs)
                        early_k(pe, 2)

                    @block.scalar
                    def _(act):
                        def stage_x(j, u):
                            if there(j, -2):
                                act.wait_ge(v_done, j - 1)
                            nc.scalar.copy(x_now[u][:, :, :, :],
                                           xt[:, bass.ds(j * PQ, PQ)].rearrange("p (b s) -> p b s", b=2).unsqueeze(2)
                                           .to_broadcast([P, 2, 2, S])).then_inc(x_staged, 1)

                        act.wait_ge(x_in, 48)
                        act.wait_ge(rest_in, 32)
                        stage_x(0, 0)

                        def step(j, u):
                            if there(j, 1):
                                stage_x(j + 1, 1 - u)
                            if there(j, -1):
                                if there(j, -3):
                                    act.wait_ge(pv_done, j - 2)
                                for a in range(2):
                                    act.wait_ge(turned, 2 * j - 1 + a)
                                    nc.scalar.copy(p_t[1 - u][:, 4 * a:4 * a + 4, :].rearrange("p n m -> p (n m)"),
                                                   ps[0:PQ, 4 + a, :]).then_inc(p_t_ready, 1)
                            if there(j, 0):
                                act.wait_ge(shifted, j + 1)
                                nc.scalar.activation(sc[u][:, :, :], sc[u][:, :, :], ACT.Exp).then_inc(exp_done, 1)

                        sweep(step)(act)
                        early_hi(act, 0)
                        early_mid(act, 0)

                    @block.vector
                    def _(dve):
                        nc.vector.memset(mask_max[:, :], 0.0).then_inc(mask_done, 1)
                        dve.wait_ge(x_in, 48)
                        for a in range(2):
                            dve.wait_ge(projected, 2 * a + 1)
                            nc.vector.tensor_scalar(q[:, a * HALF:(a + 1) * HALF], ps[:, a, 0:HALF],
                                                    bias[:, BQ1:BQ1 + 1], SCALE, ALU.add, ALU.mult)\
                                     .then_inc(qk_ready, 1)
                            dve.wait_ge(projected, 2 * a + 2)
                            nc.vector.tensor_scalar(k[:, a * HALF:(a + 1) * HALF], ps[:, 2 + a, 0:HALF],
                                                    bias[:, BK1:BK1 + 1], None, ALU.add).then_inc(qk_ready, 1)
                        dve.wait_ge(consts_in, 48)
                        nc.vector.tensor_tensor(alibi[:, :, :], c("dist").unsqueeze(1).to_broadcast([P, H, S]),
                                                row[:, ROW_SL:ROW_SL + H].unsqueeze(2).to_broadcast([P, H, S]),
                                                ALU.mult).then_inc(alibi_ready, 1)
                        own = c("own").rearrange("p (h d) -> p h d", d=DH)
                        for u in range(2):
                            for b in range(2):
                                nc.vector.tensor_copy(v_own[u][:, b, :, DH:VC], own[0:PQ, :, 0:1])\
                                         .then_inc(ones_ready, 1)
                        dve.wait_ge(ones_ready, 4)
                        dve.wait_ge(alibi_ready, 1)
                        dve.wait_ge(mask_in, 16)
                        dve.wait_ge(mask_done, 1)
                        nc.vector.tensor_reduce(mask_max[0:PQ, :], mask_sb[:, :], AX.X, ALU.max,
                                                apply_absolute_value=True).then_inc(mask_done, 1)

                        def take_v(j, u):
                            dve.wait_ge(v_done, j + 1)
                            if there(j, -2):
                                dve.wait_ge(pv_done, j - 1)
                            for b in range(2):
                                last = nc.vector.tensor_tensor(
                                    v_own[u][:, b, :, 0:DH],
                                    ps[0:PQ, 6, b * P:(b + 1) * P].rearrange("p (h d) -> p h d", d=DH),
                                    own[0:PQ], ALU.mult)
                            last.then_inc(v_ready, 1)

                        def step(j, u):
                            if there(j, 0):
                                dve.wait_ge(scores_done, j + 1)
                                if there(j, -2):
                                    dve.wait_ge(turned, 2 * j - 2)
                                nc.vector.tensor_tensor(
                                    sc[u][:, :, :].rearrange("p (a h) s -> p a (h s)", a=2),
                                    ps[:, 2 * u:2 * u + 2, 0:HALF],
                                    alibi[:, :, :].rearrange("p (a h) s -> p a (h s)", a=2), ALU.add)\
                                         .then_inc(scores_biased, 1)
                                dve.wait_ge(scores_biased, j + 1)
                                nc.vector.tensor_reduce(row_max[u][:, :], sc[u][:, :, :], AX.X, ALU.max)\
                                         .then_inc(max_ready, 1)
                                dve.wait_ge(max_ready, j + 1)
                                nc.vector.tensor_tensor(sc[u][:, :, :], sc[u][:, :, :],
                                                        row_max[u][:, :].unsqueeze(2).to_broadcast([P, H, S]),
                                                        ALU.subtract).then_inc(shifted, 1)
                            if there(j, -2):
                                dve.wait_ge(o_turned, j - 1)
                                nc.vector.tensor_scalar(
                                    att[:, bass.ds((j - 2) * PQ, PQ)].rearrange("p (b s) -> p b s", b=2),
                                    ps[:, 6, 256:384].rearrange("p (b s) -> p b s", b=2)[:, :, 0:S],
                                    bias[:, BV1:BV1 + 1], None, ALU.add).then_inc(att_ready, 1)
                            if there(j, -1):
                                dve.wait_ge(pv_done, j)
                                pv = ps[:, 7, 0:H * VC].rearrange("p (h e) -> p h e", e=VC)
                                nc.vector.reciprocal(inv[:, :].unsqueeze(2), pv[:, :, DH:VC]).then_inc(inv_ready, 1)
                                dve.wait_ge(inv_ready, j)
                                if there(j, -3):
                                    dve.wait_ge(o_turned, j - 2)
                                nc.vector.tensor_tensor(o[1 - u][:, :].rearrange("p (h d) -> p h d", d=DH),
                                                        pv[:, :, 0:DH],
                                                        inv[:, :].unsqueeze(2).to_broadcast([P, H, DH]),
                                                        ALU.mult).then_inc(normed, 1)
                            if there(j, 1):
                                take_v(j + 1, 1 - u)

                        take_v(0, 0)
                        sweep(step)(dve)

        PARTS_OF_X = ((0, 4), (4, NT))

        class Gather:
            def __init__(self, tag, part):
                a, z = PARTS_OF_X[part]
                self.cols, self.n = slice(a * P, z * P), (z - a) * P
                self.summed, self.inv_ready, self.num_ready, self.att_ready = (
                    sem(f"{n}_{tag}") for n in ("heads_gathered", "inv_ready", "num_ready", "att_ready"))

            def multiply(self, kind, bank):
                for j in range(4):
                    last = nc.tensor.matmul(ps[:, bank, 0:self.n], sel[:, kind, j, :],
                                            outs[:, j, :, :].rearrange("p b s -> p (b s)")[:, self.cols],
                                            start=(j == 0), stop=(j == 3))
                last.then_inc(self.summed, 1)

            def take(self, dve, num_bank, den_bank):
                dve.wait_ge(self.summed, 2)
                inv = xt[:, self.cols]
                nc.vector.reciprocal(inv, ps[:, den_bank, 0:self.n]).then_inc(self.inv_ready, 1)
                dve.wait_ge(self.inv_ready, 1)
                nc.vector.tensor_tensor(att[:, self.cols], ps[:, num_bank, 0:self.n], inv, ALU.mult)\
                         .then_inc(self.num_ready, 1)
                dve.wait_ge(self.num_ready, 1)
                nc.vector.tensor_scalar(att[:, self.cols], att[:, self.cols], bias[:, BV2:BV2 + 1], None,
                                        ALU.add).then_inc(self.att_ready, 1)

        class Norm:
            def __init__(self, tag, y, target, stack):
                self.y, self.target = y, target
                self.stats, self.mv = stack(f"stats_{tag}", [P, NT, 6]), stack(f"mv_{tag}", [P, NT, 2])
                self.std, self.rstd = stack(f"std_{tag}", [P, NT]), stack(f"rstd_{tag}", [P, NT])
                self.stats_ready, self.mv_ready, self.std_ready, self.rstd_ready, self.normal_ready = (
                    sem(f"{n}_{tag}") for n in ("stats_ready", "mv_ready", "std_ready", "rstd_ready", "normal_ready"))

            def moments(self, dve, part):
                tiles = range(*PARTS_OF_X[part])
                for t in tiles:
                    nc.vector.bn_stats(self.stats[:, t, :], self.y[:, t, :]).then_inc(self.stats_ready, 1)
                for t in tiles:
                    dve.wait_ge(self.stats_ready, t + 1)
                    nc.vector.bn_aggr(self.mv[:, t, :], self.stats[:, t, :]).then_inc(self.mv_ready, 1)

            def deviation(self, act, part):
                a, z = PARTS_OF_X[part]
                act.wait_ge(self.mv_ready, z)
                nc.scalar.activation(self.std[:, a:z], self.mv[:, a:z, 1], ACT.Sqrt, bias=eps[:, 0:1])\
                         .then_inc(self.std_ready, 1)

            def apply(self, dve, part):
                a, z = PARTS_OF_X[part]
                dve.wait_ge(self.std_ready, part + 1)
                nc.vector.reciprocal(self.rstd[:, a:z], self.std[:, a:z]).then_inc(self.rstd_ready, 1)
                dve.wait_ge(self.rstd_ready, part + 1)
                for t in range(a, z):
                    nc.vector.tensor_scalar(self.target[:, t, :], self.y[:, t, :],
                                            self.mv[:, t, 0:1], self.rstd[:, t:t + 1],
                                            ALU.subtract, ALU.mult).then_inc(self.normal_ready, 1)

        class Projection:
            def __init__(self, tag, w, y, stack):
                self.w, self.y = w, y
                self.norm = Norm(tag, y, xn, stack)
                self.product, self.y_ready, self.turned, self.xt_ready = (
                    sem(f"{n}_{tag}") for n in ("product", "y_ready", "turned", "xt_ready"))

            def multiply(self, part, bank):
                a, z = PARTS_OF_X[part]
                for t in range(a, z):
                    last = nc.tensor.matmul(ps[:, bank, (t - a) * P:(t - a + 1) * P], att[:, t * P:(t + 1) * P],
                                            wts[:, self.w, :], start=True, stop=True)
                last.then_inc(self.product, 1)

            def take_product(self, dve, part, bank):
                a, z = PARTS_OF_X[part]
                dve.wait_ge(self.product, part + 1)
                nc.vector.tensor_tensor(self.y[:, a:z, :],
                                        ps[:, bank, 0:(z - a) * P].rearrange("p (t d) -> p t d", d=P),
                                        xn[:, a:z, :], ALU.add).then_inc(self.y_ready, 1)
                dve.wait_ge(self.y_ready, part + 1)
                self.norm.moments(dve, part)

            def turn(self, pe, part, bank):
                a, z = PARTS_OF_X[part]
                for t in range(a, z):
                    pe.wait_ge(self.norm.normal_ready, t + 1)
                    last = nc.tensor.transpose(ps[:, bank, (t - a) * P:(t - a + 1) * P], xn[:, t, :], eye)
                last.then_inc(self.turned, 1)

            def take_turned(self, act, part, bank):
                a, z = PARTS_OF_X[part]
                act.wait_ge(self.turned, part + 1)
                nc.scalar.copy(xt[:, a * P:z * P], ps[:, bank, 0:(z - a) * P]).then_inc(self.xt_ready, 1)

        def cross_attention(top_b):
            sx = tensors(top_b)
            k_stack = [sx(f"k_stack_{u}", [ROWS, PAIRS, SKP], BF16) for u in range(2)]
            k_max = [sx(f"k_max_{u}", [P, 1]) for u in range(2)]
            terms = sx("terms", [P, H])
            bound = sx("bound", [P, 1])
            shift = [sx(f"shift_{u}", [P, 1]) for u in range(2)]

            def k_matmul(u, n, bank):
                for w, x_ in PARTS:
                    last = nc.tensor.matmul(ps[:, bank, 0:KC], wk_part[:, w, :],
                                            ctx_part[:, x_, n * KC:(n + 1) * KC],
                                            start=(w + x_ == 0), stop=(w == 1))
                return last

            def v_matmul(u, n, bank):
                for i in range(4):
                    t = 4 * n + i
                    last = nc.tensor.matmul(ps[0:KW, bank, i * P:(i + 1) * P],
                                            ctx_buf[u][:, t * KW:(t + 1) * KW], wts[:, WV2, :],
                                            start=True, stop=True)
                return last

            def v_evacuate(copy, u, n, bank):
                return copy(
                    values[u][0:KW, 4 * n:4 * n + 4, 0:H * VC].rearrange("p t (h e) -> p t h e", e=VC)[:, :, :, 0:DH],
                    ps[0:KW, bank, :].rearrange("p (t h d) -> p t h d", t=4, d=DH))

            def k_split(dve, u, n, bank, count, names):
                hi_ready, rest_ready, mid_ready, bank_read, parts_ready = names
                cols = slice(n * KC, (n + 1) * KC)
                nc.vector.tensor_scalar(k_part[u][:, 0, cols], ps[:, bank, 0:KC], bias[:, BK2:BK2 + 1], None,
                                        ALU.add).then_inc(hi_ready, 1)
                dve.wait_ge(hi_ready, count + 1)
                nc.vector.scalar_tensor_tensor(out=k_rest[0][:, :], in0=ps[:, bank, 0:KC],
                                               scalar=bias[:, BK2:BK2 + 1], in1=k_part[u][:, 0, cols],
                                               op0=ALU.add, op1=ALU.subtract).then_inc(rest_ready, 1)
                dve.wait_ge(rest_ready, count + 1)
                nc.vector.tensor_copy(k_part[u][:, 1, cols], k_rest[0][:, :]).then_inc(mid_ready, 1)
                dve.wait_ge(mid_ready, count + 1)
                nc.vector.tensor_tensor(k_part[u][:, 2, cols], k_rest[0][:, :], k_part[u][:, 1, cols],
                                        ALU.subtract).then_inc(parts_ready, 1)

            with ExitStack() as st:
                sp_ = tensors(st)
                bad = sp_("bad", [P, 2])
                flag_f = sp_("flag_f", [P, 1])
                bad_ready = sem("bad_ready")
                counted = sem("counted")
                flag_ready = sem("flag_ready")
                q_now = [sp_(f"q_now2_{u}", [ROWS, PAIRS, PQ], BF16) for u in range(2)]
                probs = [sp_(f"probs_{r}", [P, 2, HALF]) for r in range(3)]
                gather_a = Gather("first_part", 0)
                y = outs[:, 0, :, :].rearrange("p b s -> p (b s)").rearrange("p (t d) -> p t d", d=P)
                q = outs[:, 1, :, :]
                q_rest = outs[:, 2, :, :]
                first = Projection("self", WO1, y, sp_)
                q_flat = q.rearrange("p b s -> p (b s)")

                q_projected = sem("q_projected2")
                q_ready = sem("q_ready2")
                q_hi = sem("q_hi_ready")
                q_restr = sem("q_rest_ready")
                q_mid = sem("q_mid_ready")
                q_lo = sem("q_lo_ready")
                late_rest = sem("late_q_rest_ready")
                late_lo = sem("late_q_lo_ready")
                qmax_ready = sem("q_max_ready")
                stack_in = [sem("q_stack_first_in"), sem("q_stack_rest_in")]
                v0_ready = sem("early_values")
                Q_CHUNKS = ((0, 2), (2, B))

                kstack_in = [sem("kstack_in_even"), sem("kstack_in_odd")]
                q_now_ready = sem("q_now_ready")
                proj_done = sem("proj_done")
                bank_read = sem("proj_bank_free")
                k_hi = sem("k_hi_ready")
                k_restr = sem("k_rest_ready")
                k_mid = sem("k_mid_ready")
                k_ready = sem("k_parts_ready")
                v_ready = sem("values_ready")
                kmax_ready = sem("k_max_ready")
                terms_ready = sem("terms_ready")
                bound_done = sem("bound_done")
                bound_ready = sem("bound_read")
                shift_ready = sem("shift_ready")
                scores_done = sem("scores_done2")
                exp_done = sem("exp_done2")
                probs_free = sem("probs_free")
                out_free = sem("out_bank_free")
                k_names = (k_hi, k_restr, k_mid, bank_read, k_ready)

                LOOP = B - 4

                def q_rests(subtract, chunk, part, source, done, pool=None):
                    a, z = Q_CHUNKS[chunk]
                    for h in range(2):
                        rows_ = slice(64 * h, 64 * h + 64)
                        target = q_wide[rows_, 2, a:z, h, :] if part else q_rest[rows_, a:z, :]
                        if pool is not None and h:
                            pool.wait_ge(done, 1)
                        subtract(target, source[rows_, a:z, :], q_wide[rows_, part, a:z, h, :], ALU.subtract)\
                            .then_inc(done, 1)

                def batches(eng, body, peel=False):
                    if peel:
                        for b in range(2):
                            body(b, b, 0, True, True, True)
                    with eng.Fori(1 if peel else 0, LOOP // 2) as i:
                        for u in range(2):
                            body(2 * i + u, u, i, True, True, True)
                    for b in range(LOOP, B):
                        body(b, b % 2, b // 2, b + 3 < B, b + 2 < B, b + 1 < B)

                with nc.Block() as block:
                    @block.sync
                    def _(sp):
                        def kstack(u):
                            for n, part in enumerate(K_PART):
                                sp.dma_start(k_stack[u][16 * n:16 * n + 16, :, :], k_part[u][:, part, :])\
                                  .then_inc(kstack_in[u], 16)

                        def qstack(chunk):
                            a, z = Q_CHUNKS[chunk]
                            for part, n in sorted((part, n) for n, part in enumerate(Q_PART)):
                                if chunk and part == 2:
                                    sp.wait_ge(late_lo, 2)
                                else:
                                    sp.wait_ge((q_hi, q_mid, q_lo)[part], 2 * chunk + 2)
                                sp.dma_start(q_stack[16 * n:16 * n + 16, :, a * PQ:z * PQ],
                                             q_wide[:, part, a:z].rearrange("p b h s -> p (b h s)"))\
                                  .then_inc(stack_in[chunk], 16)

                        sp.wait_ge(k0_ready, 3)
                        kstack(0)
                        qstack(0)
                        sp.wait_ge(early_done, 9)
                        load_ctx(sp, 2, 0)
                        sp.wait_ge(k0_ready, 6)
                        kstack(1)

                        def held(value):
                            return value if isinstance(value, int) else sp.snap(value)

                        def body(b, u, i, load, k_next, v_next):
                            third = held(b + 3)
                            values_made = held(6 * b + 3)
                            parts_made = held(3 * b + 3)
                            batch_scored = held(KT * b + KT)
                            if load:
                                sp.wait_ge(proj_done, values_made)
                                load_ctx(sp, third, 1 - u)
                            if isinstance(b, int) and b == 0:
                                qstack(1)
                            if k_next:
                                sp.wait_ge(k_ready, parts_made)
                                sp.wait_ge(scores_done, batch_scored)
                                kstack(u)
                        batches(sp, body, peel=True)
                        sp.wait_ge(proj_done, 6 * (B - 2) + 3)
                        for r in range(3):
                            sp.dma_start(w_exp[r], experts[r]).then_inc(expert_in[r], 16)
                            sp.wait_ge(expert_in[r], 16)

                    @block.gpsimd
                    def _(pool):
                        def take(b, u):
                            nc.gpsimd.tensor_copy(q_now[u][:, :, :], q_stack[:, :, bass.ds(b * PQ, PQ)])\
                                     .then_inc(q_now_ready, 1)
                        for m in (1, 2, 3, 5):
                            early_rest(pool, m)
                            if m == 2:
                                early_lo(pool, 1)
                                early_lo(pool, 2)
                            if m == 3:
                                early_rest(pool, 4)
                                early_lo(pool, 3)
                                early_lo(pool, 4)
                        early_lo(pool, 5)

                        def split_ctx(b, u):
                            split_r(pool, ctx_buf[u][:, :], ctx_part[:, 0, :], ctx_part[:, 1, :], ctx_split,
                                    2 * (b - 2))
                        pool.wait_ge(ctx_in[0], 32)
                        split_ctx(2, 0)
                        pool.wait_ge(q_hi, 4)
                        pool.wait_ge(ctx_split, 2)
                        q_rests(nc.gpsimd.tensor_tensor, 1, 0, q, late_rest, pool)
                        pool.wait_ge(late_rest, 2)
                        pool.wait_ge(q_mid, 4)
                        q_rests(nc.gpsimd.tensor_tensor, 1, 1, q_rest, late_lo, pool)
                        pool.wait_ge(late_lo, 2)

                        def body(b, u, i):
                            if not isinstance(b, int) or b + 3 < B:
                                pool.wait_ge(proj_done, 6 * b + 6)
                                pool.wait_ge(ctx_in[1 - u], 16 * (i + 2 + u))
                                split_ctx(b + 3, 1 - u)
                            if not isinstance(b, int) or b >= 2:
                                pool.wait_ge(scores_done, KT * (b + 1))
                            if isinstance(b, int) and b == 0:
                                pool.wait_ge(stack_in[1], 16 * len(Q_PART))
                            take(b + 2, u)
                        for u in range(2):
                            body(u, u, 0)
                        with pool.Fori(1, B // 2 - 2) as i:
                            for u in range(2):
                                body(2 * i + u, u, i)
                        for u in range(2):
                            body(B - 4 + u, u, B // 2 - 2)
                        pool.wait_ge(first.turned, 2)
                        add_output_bias(ROW_BO2)

                    @block.tensor
                    def _(pe):
                        def scores(u, t, b=None):
                            for p in range(PAIRS):
                                last = nc.tensor.matmul(
                                    ps[:, 2 * (t % 2) + p // 4, (p % 4) * PQ:(p % 4 + 1) * PQ],
                                    k_stack[u][:, p, t * KW:t * KW + P], q_now[u][:, p, :] if b is None else q_stack[:, p, b * PQ:(b + 1) * PQ],
                                    start=True, stop=True)
                            last.then_inc(scores_done, 1)

                        def product(b, u, t):
                            r = t % 3
                            flat = probs[r][0:KW].rearrange("p a n -> p (a n)")
                            for n in range(8):
                                g = n % 4
                                h, w, at = (3 * g, 3 * S, 0) if n < 4 else (12 + g, S, 3 * S)
                                last = nc.tensor.matmul(
                                    ps[32 * g:32 * g + 32, 4 + u, at:at + w],
                                    values[u][0:KW, t, VC * h:VC * h + 32], flat[:, h * S:h * S + w],
                                    start=(t == 0 and n < 4), stop=(t == KT - 1), skip_group_check=True)
                            last.then_inc(probs_free, 1)
                            return last

                        def unit(kind, u, n, m, bank):
                            pe.wait_ge(bank_read, m + 1)
                            last = (k_matmul if kind == "k" else v_matmul)(u, n, bank)
                            last.then_inc(proj_done, 1)

                        def early_v(n):
                            pe.wait_ge(hi0, n + 4)
                            v_matmul(0, n, 5 + n).then_inc(early_done, 1)

                        pe.sem_inc(probs_free, 3)
                        def project_q(part):
                            a, z = PARTS_OF_X[part]
                            pe.wait_ge(first.xt_ready, part + 1)
                            nc.tensor.matmul(ps[:, 5 * part, 0:(z - a) * P], wts[:, WQ2, :], xt[:, a * P:z * P],
                                             start=True, stop=True).then_inc(q_projected, 1)

                        for part in range(2):
                            first.multiply(part, part)
                        for m in range(3, 6):
                            early_k(pe, m)
                        pe.wait_ge(hi0, 2)
                        first.turn(pe, 0, 2)
                        project_q(0)
                        early_v(0)
                        early_v(1)
                        pe.wait_ge(out_free, 2)
                        pe.wait_ge(terms_ready, 1)
                        nc.tensor.matmul(ps[:, 4, 256:256 + H], ones[:, :], terms[:, :],
                                         start=True, stop=True).then_inc(bound_done, 1)
                        early_v(2)
                        pe.wait_ge(v0_ready, 1)
                        first.turn(pe, 1, 5)
                        pe.wait_ge(kstack_in[0], 16 * len(K_PART))
                        pe.wait_ge(stack_in[0], 16 * len(Q_PART))
                        pe.wait_ge(q_ready, 1)
                        scores(0, 0, 0)
                        scores(0, 1, 0)
                        project_q(1)

                        def body(b, u, i, load, k_next, v_next):
                            for t in range(KT):
                                if t == 0:
                                    if isinstance(b, int) and b == 0:
                                        pe.wait_ge(v0_ready, 3)
                                    else:
                                        pe.wait_ge(v_ready, 3 * b)
                                    pe.wait_ge(out_free, b + 1)
                                pe.wait_ge(exp_done, KT * b + t + 1)
                                static = isinstance(b, int)
                                if t + 2 < KT:
                                    scores(u, t + 2, b if static and b < 2 else None)
                                elif v_next:
                                    if t + 2 == KT:
                                        pe.wait_ge(kstack_in[1 - u],
                                                   16 * len(K_PART) * (i + u + 1))
                                        if not static or b > 0:
                                            pe.wait_ge(q_now_ready, b)
                                    scores(1 - u, t + 2 - KT, 1 if static and b == 0 else None)
                                product(b, u, t)
                                if v_next and t in (1, 2, 3):
                                    unit("v", 1 - u, t - 1, 6 * b + t - 1, 6 + t % 2)
                                if not v_next and t in (1, 2):
                                    gather_a.multiply(t - 1, 5 + t)
                                if not v_next and t == 9:
                                    pe.wait_ge(bad_ready, 2)
                                    pe.wait_ge(gather_a.att_ready, 1)
                                    nc.tensor.matmul(ps[:, 6, 0:2], ones[:, :], bad[:, :], start=True, stop=True)\
                                             .then_inc(counted, 1)
                                if v_next and t == 4:
                                    pe.wait_ge(out_free, b + 2)
                                    pe.wait_ge(terms_ready, b + 2)
                                    nc.tensor.matmul(ps[:, 5 - u, 256:256 + H], ones[:, :], terms[:, :],
                                                     start=True, stop=True).then_inc(bound_done, 1)
                                if k_next and t in (5, 6, 7):
                                    if t == 5:
                                        pe.wait_ge(ctx_split, 2 * b + 2)
                                    unit("k", u, t - 5, 6 * b + 3 + t - 5, 6 + (t - 1) % 2)
                        batches(pe, body, peel=True)

                    @block.scalar
                    def _(act):
                        def early_values(n):
                            act.wait_ge(early_done, 7 + n)
                            v_evacuate(nc.scalar.copy, 0, n, 5 + n).then_inc(v0_ready, 1)

                        for m in (1, 2):
                            early_hi(act, m)
                        for m in (1, 2):
                            early_mid(act, m)
                        first.norm.deviation(act, 0)
                        first.take_turned(act, 0, 2)
                        first.norm.deviation(act, 1)
                        for m in (3, 4):
                            early_hi(act, m)
                        for m in (3, 4):
                            early_mid(act, m)
                        early_hi(act, 5)
                        for n in range(3):
                            early_values(n)
                        first.take_turned(act, 1, 5)
                        early_mid(act, 5)

                        def body(b, u):
                            for t in range(KT):
                                if t == 0:
                                    act.wait_ge(shift_ready, b + 1)
                                act.wait_ge(scores_done, KT * b + t + 1)
                                act.wait_ge(probs_free, KT * b + t + 1)
                                s = 2 * (t % 2)
                                nc.scalar.activation(probs[t % 3][:, :, :], ps[:, s:s + 2, 0:HALF], ACT.Exp,
                                                     bias=shift[u][:, 0:1]).then_inc(exp_done, 1)
                        with act.Fori(0, 2) as i:
                            for n in range(8):
                                body(8 * i + n, n % 2)

                    @block.vector
                    def _(dve):
                        def k_unit(u, n, m, count, bank):
                            dve.wait_ge(proj_done, m + 1)
                            k_split(dve, u, n, bank, count, k_names)
                            dve.sem_inc(bank_read, 1)

                        def largest_k(b, u):
                            dve.wait_ge(k_ready, 3 * b - 3)
                            nc.vector.tensor_reduce(k_max[u][:, :], k_part[u][:, 0, 0:SK], AX.X, ALU.max,
                                                    apply_absolute_value=True).then_inc(kmax_ready, 1)

                        def early_largest_k(b):
                            dve.wait_ge(hi0, 3 * b + 3)
                            nc.vector.tensor_reduce(k_max[b][:, :], k_part[b][:, 0, 0:SK], AX.X, ALU.max,
                                                    apply_absolute_value=True).then_inc(kmax_ready, 1)

                        def bound_terms(b, u):
                            dve.wait_ge(kmax_ready, b + 1)
                            nc.vector.tensor_scalar(terms[:, :], c("head2"), k_max[u][:, 0:1],
                                                    q_max[:, bass.ds(b, 1)], ALU.mult, ALU.mult)\
                                     .then_inc(terms_ready, 1)

                        def take_bound(b, u):
                            dve.wait_ge(bound_done, b + 1)
                            nc.vector.tensor_reduce(bound[:, :], ps[:, 4 + u, 256:256 + H], AX.X, ALU.max)\
                                     .then_inc(bound_ready, 1)
                            dve.wait_ge(bound_ready, b + 1)
                            nc.vector.tensor_tensor(worst[:, :], worst[:, :], bound[:, :], ALU.max)
                            nc.vector.tensor_scalar(shift[u][:, :], bound[:, :], -1.01, HEADROOM, ALU.mult, ALU.add)\
                                     .then_inc(shift_ready, 1)

                        def evacuate(b, u):
                            dve.wait_ge(probs_free, KT * b + KT + 3)
                            nc.vector.tensor_copy(outs[:, :, bass.ds(b, 1), :].rearrange("p j b s -> p j (b s)"),
                                                  ps[:, 4 + u, 0:4 * S].rearrange("p (j s) -> p j s", s=S))\
                                     .then_inc(out_free, 1)
                        dve.sem_inc(bank_read, 2)
                        dve.sem_inc(out_free, 2)
                        first.take_product(dve, 0, 0)
                        first.norm.apply(dve, 0)
                        first.take_product(dve, 1, 1)
                        def q_parts(chunk, part, source, done):
                            a, z = Q_CHUNKS[chunk]
                            for h in range(2):
                                rows_ = slice(64 * h, 64 * h + 64)
                                nc.vector.tensor_copy(q_wide[rows_, part, a:z, h, :], source[rows_, a:z, :])\
                                         .then_inc(done, 1)

                        def split_q():
                            q_parts(0, 0, q, q_hi)
                            dve.wait_ge(q_hi, 2)
                            q_rests(nc.vector.tensor_tensor, 0, 0, q, q_restr)
                            dve.wait_ge(q_restr, 2)
                            q_parts(0, 1, q_rest, q_mid)
                            dve.wait_ge(q_mid, 2)
                            q_rests(nc.vector.tensor_tensor, 0, 1, q_rest, q_lo)

                        def take_q(part):
                            a, z = PARTS_OF_X[part]
                            dve.wait_ge(q_projected, part + 1)
                            nc.vector.tensor_scalar(q_flat[:, a * P:z * P], ps[:, 5 * part, 0:(z - a) * P],
                                                    bias[:, BQ2:BQ2 + 1], SCALE, ALU.add, ALU.mult).then_inc(q_ready, 1)
                            dve.wait_ge(q_ready, part + 1)

                        def largest_q(chunk):
                            a, z = Q_CHUNKS[chunk]
                            nc.vector.tensor_reduce(q_max[:, a:z], q[:, a:z, :], AX.X, ALU.max,
                                                    apply_absolute_value=True).then_inc(qmax_ready, 1)

                        take_q(0)
                        split_q()
                        largest_q(0)
                        early_largest_k(0)
                        dve.wait_ge(qmax_ready, 1)
                        bound_terms(0, 0)
                        first.norm.apply(dve, 1)
                        take_bound(0, 0)
                        take_q(1)
                        q_parts(1, 0, q, q_hi)
                        largest_q(1)
                        early_largest_k(1)
                        dve.wait_ge(qmax_ready, 2)

                        def body(b, u, i, load, k_next, v_next, first=False):
                            if isinstance(b, int) and b == 1:
                                dve.wait_ge(late_lo, 2)
                            if not first:
                                evacuate(b - 1, 1 - u)
                            if v_next:
                                bound_terms(b + 1, 1 - u)
                                for n in range(3):
                                    dve.wait_ge(proj_done, 6 * b + 1 + n)
                                    v_evacuate(nc.vector.tensor_copy, 1 - u, n, 6 + (n + 1) % 2).then_inc(v_ready, 1)
                                    dve.wait_ge(v_ready, 3 * b + 1 + n)
                                    dve.sem_inc(bank_read, 1)
                                take_bound(b + 1, 1 - u)
                            if first:
                                dve.wait_ge(late_rest, 2)
                                q_parts(1, 1, q_rest, q_mid)
                            if k_next:
                                for n in range(3):
                                    if n == 0:
                                        dve.wait_ge(kstack_in[u], 16 * len(K_PART) * (i + 1))
                                    k_unit(u, n, 6 * b + 3 + n, 3 * b + n, 6 + n % 2)
                            if k_next:
                                largest_k(b + 2, u)
                        body(0, 0, 0, True, True, True, first=True)
                        body(1, 1, 0, True, True, True)
                        with dve.Fori(1, LOOP // 2) as i:
                            for u in range(2):
                                body(2 * i + u, u, i, True, True, True)
                        for b in range(LOOP, B):
                            body(b, b % 2, b // 2, b + 3 < B, b + 2 < B, b + 1 < B)
                        gather_a.take(dve, 6, 7)

                        nc.vector.tensor_scalar(bad[:, 0:1], worst[:, :], GUARD, None, ALU.is_le).then_inc(bad_ready, 1)
                        nc.vector.tensor_scalar(bad[:, 1:2], mask_max[:, :], 0.0, None, ALU.is_equal)\
                                 .then_inc(bad_ready, 1)
                        dve.wait_ge(counted, 1)
                        nc.vector.tensor_reduce(flag_f[:, :], ps[:, 6, 0:2], AX.X, ALU.min).then_inc(flag_ready, 1)
                        dve.wait_ge(flag_ready, 1)
                        nc.vector.tensor_scalar(flag[:, :], flag_f[:, :], P - 0.5, None, ALU.is_lt)\
                                 .then_inc(flag_ready, 1)
                        evacuate(B - 1, 1)
                        dve.wait_ge(out_free, B + 2)

            return k_stack, k_split

        def general_cross_attention(shared):
            k_stack, k_split = shared
            with ExitStack() as st:
                sg = tensors(st)
                mask_sb = sg("mask_g", [PQ, SK])
                s_all = sg("s_all", [PQ, SK])
                p_t = sg("p_t_g", [KW, KT, PQ])
                row_max = sg("row_max_g", [PQ, 1])
                total = sg("total_g", [PQ, 1])
                inv = sg("inv_g", [PQ, 1])
                picked = sg("picked_g", [16, 2, S])
                folded = sg("folded_g", [16, S])
                gather_g = Gather("general", 0)
                outs_set = sem("outs_set_g")
                experts_again = sem("experts_in_again")

                mask_in = sem("mask_in_g")
                ctx_g = sem("ctx_in_g")
                proj = sem("proj_done_g")
                k_hi, k_restr, k_mid, k_ready, v_ready = (sem(f"{n}_g") for n in
                                                          ("k_hi", "k_rest", "k_mid", "k_parts", "values"))
                stack_in = sem("kstack_in_g")
                scores_done = sem("scores_done_g")
                masked = sem("masked_g")
                max_ready = sem("max_ready_g")
                exp_done = sem("exp_done_g")
                inv_ready = sem("inv_ready_g")
                scaled = sem("scaled_g")
                turned = sem("turned_g")
                p_t_ready = sem("p_t_ready_g")
                pv_done = sem("pv_done_g")
                picked_ready = sem("picked_ready_g")
                folded_ready = sem("folded_ready_g")
                stored = sem("stored_g")
                names = (k_hi, k_restr, k_mid, None, k_ready)

                v_flat = values[0][0:KW, :, 0:P]

                with nc.Block() as block:
                    @block.sync
                    def _(sp):
                        sp.dma_start(mask_sb[:, :], mask).then_inc(mask_in, 16)
                        sp.wait_ge(outs_set, 1)

                        def body(b):
                            def held(value):
                                return value if isinstance(value, int) else sp.snap(value)

                            attended, parts_made = held(PAIRS * b), held(3 * b + 3)
                            folds = [held(PAIRS * b + p + 1) for p in range(PAIRS)]
                            if not isinstance(b, int):
                                sp.wait_ge(pv_done, attended)
                            sp.dma_start(ctx_buf[0][:, :], ctx_t[bass.ds(b, 1)].rearrange("a d k -> d (a k)"))\
                              .then_inc(ctx_g, 16)
                            sp.wait_ge(k_ready, parts_made)
                            for n, part in enumerate(K_PART):
                                sp.dma_start(k_stack[0][16 * n:16 * n + 16, :, :], k_part[0][:, part, :])\
                                  .then_inc(stack_in, 16)
                            for p in range(PAIRS):
                                sp.wait_ge(folded_ready, folds[p])
                                for n in range(2):
                                    first_row, block_ = head_rows(2 * p + n)
                                    sp.dma_start(outs[first_row:first_row + DH, block_, bass.ds(b, 1), :]
                                                 .rearrange("p a s -> p (a s)"),
                                                 folded[DH * n:DH * (n + 1), :]).then_inc(stored, 16)
                        body(0)
                        with sp.Fori(1, B) as b:
                            body(b)
                        sp.wait_ge(stored, 32 * PAIRS * B)
                        for r in range(3):
                            sp.dma_start(w_exp[r], experts[r]).then_inc(experts_again, 16)
                        sp.wait_ge(experts_again, 48)

                    @block.gpsimd
                    def _(pool):
                        nc.gpsimd.memset(outs[:, :, :, :].rearrange("p j b s -> p (j b s)"), 1.0).then_inc(outs_set, 1)

                    @block.tensor
                    def _(pe):
                        def body(b):
                            pe.wait_ge(ctx_g, 16 * b + 16)
                            for n in range(3):
                                if n == 2 or not isinstance(b, int):
                                    pe.wait_ge(k_ready, 3 * b + n - 1 if n < 2 else 3 * b + 1)
                                nc.tensor.matmul(ps[:, 6 + n % 2, 0:KC], wts[:, WK2, :],
                                                 ctx_buf[0][:, n * KC:(n + 1) * KC],
                                                 start=True, stop=True).then_inc(proj, 1)
                            for n in range(3):
                                if n == 0:
                                    pe.wait_ge(k_ready, 3 * b + 3)
                                if n == 2:
                                    pe.wait_ge(v_ready, 3 * b + 1)
                                for t in range(4 * n, 4 * n + 4):
                                    last = nc.tensor.matmul(ps[0:KW, 6 + n % 2, (t % 4) * P:(t % 4 + 1) * P],
                                                            ctx_buf[0][:, t * KW:(t + 1) * KW], wts[:, WV2, :],
                                                            start=True, stop=True)
                                last.then_inc(proj, 1)
                            pe.wait_ge(stack_in, 16 * len(K_PART) * (b + 1))
                            for p in range(PAIRS):
                                j = PAIRS * b + p
                                if p or not isinstance(b, int):
                                    pe.wait_ge(masked, j)
                                for n in range(NKC):
                                    last = nc.tensor.matmul(ps[0:PQ, n, 0:KC],
                                                            q_stack[:, p, bass.ds(b * PQ, PQ)],
                                                            k_stack[0][:, p, n * KC:(n + 1) * KC],
                                                            start=True, stop=True)
                                last.then_inc(scores_done, 1)
                                pe.wait_ge(scaled, j + 1)
                                for t in range(KT):
                                    last = nc.tensor.transpose(ps[0:KW, 3 + t // 4, (t % 4) * PQ:(t % 4 + 1) * PQ],
                                                               s_all[:, t * KW:(t + 1) * KW], eye[0:PQ, 0:PQ])
                                last.then_inc(turned, 1)
                                pe.wait_ge(p_t_ready, j + 1)
                                pe.wait_ge(v_ready, 3 * b + 3)
                                for t in range(KT):
                                    last = nc.tensor.matmul(
                                        ps[0:16, 6, 0:PQ],
                                        v_pair(p, t), p_t[:, t, :], start=(t == 0), stop=(t == KT - 1))
                                last.then_inc(pv_done, 1)
                                pe.wait_ge(picked_ready, j + 1)

                        def v_pair(p, t):
                            return v_flat[:, t, 16 * p:16 * p + 16]
                        body(0)
                        with pe.Fori(1, B) as b:
                            body(b)
                        pe.wait_ge(stored, 32 * PAIRS * B)
                        pe.wait_ge(masked, PAIRS * B)
                        for kind in range(2):
                            gather_g.multiply(kind, kind)

                    @block.scalar
                    def _(act):
                        def body(b):
                            for p in range(PAIRS):
                                act.wait_ge(max_ready, PAIRS * b + p + 1)
                                nc.scalar.activation(s_all[:, :], s_all[:, :], ACT.Exp, bias=row_max[:, 0:1],
                                                     accum_out=total[:, 0:1]).then_inc(exp_done, 1)
                        body(0)
                        with act.Fori(1, B) as b:
                            body(b)

                    @block.vector
                    def _(dve):
                        dve.wait_ge(mask_in, 16)
                        diag = c("diag").rearrange("p (h s) -> p h s", h=2)

                        def body(b):
                            if not isinstance(b, int):
                                dve.wait_ge(stack_in, 16 * len(K_PART) * b)
                            for n in range(3):
                                dve.wait_ge(proj, 6 * b + n + 1)
                                k_split(dve, 0, n, 6 + n % 2, 3 * b + n, names)
                            for n in range(3):
                                dve.wait_ge(proj, 6 * b + 4 + n)
                                nc.vector.tensor_copy(values[0][0:KW, 4 * n:4 * n + 4, 0:P],
                                                      ps[0:KW, 6 + n % 2, :].rearrange("p (t m) -> p t m", t=4))\
                                         .then_inc(v_ready, 1)
                            for p in range(PAIRS):
                                j = PAIRS * b + p
                                dve.wait_ge(scores_done, j + 1)
                                nc.vector.tensor_tensor(s_all[:, :].rearrange("p (n k) -> p n k", k=KC),
                                                        ps[0:PQ, 0:NKC, 0:KC],
                                                        mask_sb[:, :].rearrange("p (n k) -> p n k", k=KC),
                                                        ALU.add).then_inc(masked, 1)
                                dve.wait_ge(masked, j + 1)
                                nc.vector.tensor_reduce(row_max[:, :], s_all[:, :], AX.X, ALU.max, negate=True)\
                                         .then_inc(max_ready, 1)
                                dve.wait_ge(exp_done, j + 1)
                                nc.vector.reciprocal(inv[:, :], total[:, :]).then_inc(inv_ready, 1)
                                dve.wait_ge(inv_ready, j + 1)
                                nc.vector.tensor_scalar(s_all[:, :], s_all[:, :], inv[:, 0:1], None, ALU.mult)\
                                         .then_inc(scaled, 1)
                                dve.wait_ge(turned, j + 1)
                                nc.vector.tensor_copy(p_t[:, :, :].rearrange("p (a n) m -> p a (n m)", a=3),
                                                      ps[0:KW, 3:6, 0:4 * PQ]).then_inc(p_t_ready, 1)
                                dve.wait_ge(pv_done, j + 1)
                                if p or not isinstance(b, int):
                                    dve.wait_ge(stored, 32 * j)
                                nc.vector.tensor_tensor(picked[:, :, :],
                                                        ps[0:16, 6, 0:PQ].rearrange("p (h s) -> p h s", h=2),
                                                        diag[0:16], ALU.mult).then_inc(picked_ready, 1)
                                dve.wait_ge(picked_ready, j + 1)
                                nc.vector.tensor_tensor(folded[:, :], picked[:, 0, :], picked[:, 1, :], ALU.add)\
                                         .then_inc(folded_ready, 1)
                        body(0)
                        with dve.Fori(1, B) as b:
                            body(b)
                        gather_g.take(dve, 0, 1)

        def feed_forward():
            with ExitStack() as st:
                sf = tensors(st)
                hid = [sf(f"hid_{u}", [P, FC, TOK]) for u in range(3)]
                w1_part = [sf(f"w1_part_{r}", [P, 2, F], F32R) for r in range(3)]
                xt_part = sf("xt_part", [P, 2, TOK], F32R)
                y = sf("y_cross", [P, NT, P])
                acc = sf("acc", [P, NT, P])
                rt = sf("router", [P, E])
                b1_sb = sf("b1", [P, NE * FC])
                b2_sb = sf("b2", [NE, P])
                logit = sf("logit", [P, NT, E])
                best = sf("best", [P, NT, 1])
                prob = sf("prob", [P, NT, E])
                total = sf("total", [P, NT, 1])
                hit = sf("hit", [P, NT, E])
                first = sf("first", [P, NT, E])
                comb = sf("comb", [P, NT, NE])
                comb_t = sf("comb_t", [NE, NT, P])
                second = Projection("cross", WO2, y, sf)
                last_norm = Norm("out", acc, xn, sf)
                gather_b = Gather("second_part", 1)

                small_in = sem("small_in")
                hi_ready = sem("x_hi_ready")
                lo_ready = sem("x_lo_ready")
                logits_done = sem("logits_done")
                chain = sem("router_steps")
                exp_done = sem("router_exp_done")
                comb_ready = sem("comb_ready")
                comb_turned = sem("comb_turned")
                comb_t_ready = sem("comb_t_ready")
                b2_done = sem("b2_done")
                acc_start = sem("acc_start")
                w1_split = sem("w1_split")
                up_done = sem("up_done")
                gelu_done = sem("gelu_done")
                down_done = sem("down_done")
                acc_done = sem("acc_done")
                stored = sem("stored")

                def item(part, e):
                    if isinstance(e, int) and e < 3:
                        return 3 * part + e
                    return 2 * e + part

                def tokens(part):
                    a, z = PARTS_OF_X[part]
                    return slice(a * P, z * P)

                CHAIN = 22

                with nc.Block() as block:
                    @block.sync
                    def _(sp):
                        sp.dma_start(rt[:, :], router_t).then_inc(small_in, 16)
                        sp.dma_start(b2_sb[:, :], b2).then_inc(small_in, 16)
                        sp.dma_start(b1_sb[:, :], b1).then_inc(small_in, 16)
                        for e in range(3, NE):
                            sp.wait_ge(down_done, item(1, e - 3) + 1)
                            sp.dma_start(w_exp[e % 3], experts[e]).then_inc(expert_in[e % 3], 16)
                        for part, (a, z) in enumerate(PARTS_OF_X):
                            sp.wait_ge(last_norm.normal_ready, z)
                            sp.dma_start(out[a * P:z * P].rearrange("(t p) d -> p t d", p=P), xn[:, a:z, :])\
                              .then_inc(stored, 16)
                        sp.wait_ge(stored, 32)

                    @block.gpsimd
                    def _(pool):
                        def split_w1(e, r, i):
                            if not (isinstance(e, int) and e < 3):
                                pool.wait_ge(up_done, FC * (item(1, e - 3) + 1))
                            pool.wait_ge(expert_in[r], 16 * (i + 1))
                            split_r(pool, w_exp[r][:, W1_AT:W1_AT + F], w1_part[r][:, 0, :], w1_part[r][:, 1, :],
                                    w1_split, 2 * e)

                        def x_lo(part):
                            cols = tokens(part)
                            pool.wait_ge(second.xt_ready, part + 1)
                            pool.wait_ge(hi_ready, part + 1)
                            nc.gpsimd.tensor_tensor(xt_part[:, 1, cols], xt[:, cols],
                                                    xt_part[:, 0, cols].bitcast(F32), ALU.subtract)\
                                     .then_inc(lo_ready, 1)
                        split_w1(0, 0, 0)
                        x_lo(0)
                        split_w1(1, 1, 0)
                        split_w1(2, 2, 0)
                        x_lo(1)
                        for e in range(3, NE):
                            split_w1(e, e % 3, e // 3)

                    @block.tensor
                    def _(pe):
                        def logits(part):
                            pe.wait_ge(second.xt_ready, part + 1)
                            pe.wait_ge(hi_ready, 1)
                            if part:
                                pe.wait_ge(chain, 1)
                            for t in range(*PARTS_OF_X[part]):
                                last = nc.tensor.matmul(ps[:, 7, t * E:(t + 1) * E], xt[:, t * P:(t + 1) * P], rt[:, :],
                                                        start=True, stop=True)
                            last.then_inc(logits_done, 1)

                        def turn_comb(part):
                            a, z = PARTS_OF_X[part]
                            pe.wait_ge(comb_ready, part + 1)
                            for t in range(a, z):
                                last = nc.tensor.transpose(ps[0:NE, 4 + part, (t - a) * P:(t - a + 1) * P],
                                                           comb[:, t, :], eye)
                            last.then_inc(comb_turned, 1)

                        def mix_b2(part):
                            a, z = PARTS_OF_X[part]
                            pe.wait_ge(comb_t_ready, part + 1)
                            for t in range(a, z):
                                last = nc.tensor.matmul(ps[:, 4 + part, (t - a) * P:(t - a + 1) * P],
                                                        comb_t[:, t, :], b2_sb[:, :], start=True, stop=True)
                            last.then_inc(b2_done, 1)

                        def up(part, e, r):
                            cols = tokens(part)
                            nth = item(part, e)
                            if isinstance(e, int) and e == 0:
                                pe.wait_ge(lo_ready, part + 1)
                            pe.wait_ge(w1_split, 2 * e + 2)
                            for f in range(FC):
                                if not isinstance(nth, int) or nth > 0:
                                    pe.wait_ge(gelu_done, FC * nth + f - 3)
                                for w, x_ in PARTS:
                                    last = nc.tensor.matmul(ps[:, f, 0:cols.stop - cols.start],
                                                            w1_part[r][:, w, f * P:(f + 1) * P],
                                                            xt_part[:, x_, cols],
                                                            start=(w + x_ == 0), stop=(w == 1))
                                last.then_inc(up_done, 1)

                        def down(part, e, r):
                            a, z = PARTS_OF_X[part]
                            nth = item(part, e)
                            pe.wait_ge(gelu_done, FC * nth + FC)
                            if isinstance(e, int) and e == 0:
                                pe.wait_ge(acc_start, part + 1)
                            else:
                                pe.wait_ge(acc_done, nth if isinstance(e, int) and e < 3 else nth - 1)
                            for t in range(a, z):
                                for f in range(FC):
                                    last = nc.tensor.matmul(ps[:, 4 + part, (t - a) * P:(t - a + 1) * P],
                                                            hid[r][:, f, t * P:(t + 1) * P],
                                                            w_exp[r][:, W2_AT + f * P:W2_AT + (f + 1) * P],
                                                            start=(f == 0), stop=(f == FC - 1))
                            last.then_inc(down_done, 1)

                        second.multiply(0, 4)
                        for kind in range(2):
                            gather_b.multiply(kind, 5 + kind)
                        second.turn(pe, 0, 7)
                        pe.wait_ge(small_in, 48)
                        logits(0)
                        up(0, 0, 0)
                        pe.wait_ge(gather_b.att_ready, 1)
                        second.multiply(1, 5)
                        up(0, 1, 1)
                        turn_comb(0)
                        up(0, 2, 2)
                        mix_b2(0)
                        second.turn(pe, 1, 6)
                        down(0, 0, 0)
                        logits(1)
                        down(0, 1, 1)
                        up(1, 0, 0)
                        turn_comb(1)
                        down(0, 2, 2)
                        mix_b2(1)
                        up(1, 1, 1)
                        down(1, 0, 0)
                        up(1, 2, 2)
                        down(1, 1, 1)
                        down(1, 2, 2)
                        up(0, 3, 0)
                        up(1, 3, 0)
                        down(0, 3, 0)
                        for e in range(4, NE):
                            r = e % 3
                            up(0, e, r)
                            down(1, e - 1, (r + 2) % 3)
                            up(1, e, r)
                            down(0, e, r)
                        down(1, NE - 1, (NE - 1) % 3)

                    @block.scalar
                    def _(act):
                        def take_turned(part, bank):
                            cols = tokens(part)
                            if part:
                                act.wait_ge(gather_b.num_ready, 1)
                            second.take_turned(act, part, bank)
                            nc.scalar.copy(xt_part[:, 0, cols], ps[:, bank, 0:cols.stop - cols.start])\
                                     .then_inc(hi_ready, 1)

                        def router_exp(part):
                            a, z = PARTS_OF_X[part]
                            act.wait_ge(chain, CHAIN * part + 3)
                            nc.scalar.activation(prob[:, a:z, :], logit[:, a:z, :], ACT.Exp).then_inc(exp_done, 1)

                        def gelu(part, e, r):
                            cols = tokens(part)
                            nth = item(part, e)
                            for f in range(FC):
                                act.wait_ge(up_done, FC * nth + f + 1)
                                nc.scalar.activation(hid[r][:, f, cols], ps[:, f, 0:cols.stop - cols.start],
                                                     ACT.Gelu_apprx_tanh,
                                                     bias=b1_sb[:, FC * e + f:FC * e + f + 1]).then_inc(gelu_done, 1)
                        second.norm.deviation(act, 0)
                        take_turned(0, 7)
                        router_exp(0)
                        act.wait_ge(small_in, 48)
                        gelu(0, 0, 0)
                        gelu(0, 1, 1)
                        second.norm.deviation(act, 1)
                        gelu(0, 2, 2)
                        take_turned(1, 6)
                        router_exp(1)
                        for e in range(3):
                            gelu(1, e, e)
                        for e in range(3, NE):
                            for part in range(2):
                                gelu(part, e, e % 3)
                        for part in range(2):
                            last_norm.deviation(act, part)

                    @block.vector
                    def _(dve):
                        steps = [0]

                        def step(ins):
                            ins.then_inc(chain, 1)
                            steps[0] += 1
                            dve.wait_ge(chain, steps[0])

                        def route(part):
                            a, z = PARTS_OF_X[part]
                            n = z - a
                            logit_, prob_, hit_, first_ = (v[:, a:z, :] for v in (logit, prob, hit, first))
                            best_, total_ = best[:, a:z, :], total[:, a:z, :]

                            def wide(v):
                                return v.to_broadcast([P, n, E])

                            dve.wait_ge(logits_done, part + 1)
                            step(nc.vector.tensor_tensor(logit_, ps[:, 7, a * E:z * E].rearrange("p (t e) -> p t e", e=E),
                                                         row[:, ROW_RB:ROW_RB + E].unsqueeze(1).to_broadcast([P, n, E]),
                                                         ALU.add))
                            step(nc.vector.tensor_reduce(best[:, a:z, 0], logit_, AX.X, ALU.max))
                            step(nc.vector.tensor_tensor(logit_, logit_, wide(best_), ALU.subtract))
                            dve.wait_ge(exp_done, part + 1)
                            down_ = c("down").unsqueeze(1).to_broadcast([P, n, E])

                            def pick(left, into):
                                step(nc.vector.tensor_reduce(best[:, a:z, 0], left, AX.X, ALU.max))
                                step(nc.vector.tensor_tensor(hit_, left, wide(best_), ALU.is_equal))
                                step(nc.vector.tensor_tensor(hit_, hit_, down_, ALU.mult))
                                step(nc.vector.tensor_reduce(best[:, a:z, 0], hit_, AX.X, ALU.max))
                                step(nc.vector.tensor_tensor(into, hit_, wide(best_), ALU.is_equal))

                            step(nc.vector.tensor_reduce(total[:, a:z, 0], prob_, AX.X, ALU.add))
                            step(nc.vector.reciprocal(best_, total_))
                            step(nc.vector.tensor_tensor(prob_, prob_, wide(best_), ALU.mult))
                            pick(prob_, first_)
                            step(nc.vector.scalar_tensor_tensor(out=logit_, in0=first_, scalar=-2.0,
                                                                in1=prob_, op0=ALU.mult, op1=ALU.add))
                            pick(logit_, hit_)
                            step(nc.vector.tensor_tensor(first_, first_, hit_, ALU.add))
                            step(nc.vector.tensor_tensor(prob_, prob_, first_, ALU.mult))
                            step(nc.vector.tensor_reduce(total[:, a:z, 0], prob_, AX.X, ALU.add))
                            step(nc.vector.reciprocal(best_, total_))
                            step(nc.vector.memset(comb[:, a:z, E:NE], 1.0))
                            nc.vector.tensor_tensor(comb[:, a:z, 0:E], prob_, wide(best_), ALU.mult)\
                                     .then_inc(comb_ready, 1)
                            assert steps[0] == CHAIN * (part + 1)

                        def take_comb(part):
                            a, z = PARTS_OF_X[part]
                            dve.wait_ge(comb_turned, part + 1)
                            nc.vector.tensor_copy(comb_t[:, a:z, :].rearrange("p t m -> p (t m)"),
                                                  ps[0:NE, 4 + part, 0:(z - a) * P]).then_inc(comb_t_ready, 1)

                        def start_acc(part):
                            a, z = PARTS_OF_X[part]
                            dve.wait_ge(b2_done, part + 1)
                            nc.vector.tensor_tensor(acc[:, a:z, :],
                                                    ps[:, 4 + part, 0:(z - a) * P].rearrange("p (t d) -> p t d", d=P),
                                                    xn[:, a:z, :], ALU.add).then_inc(acc_start, 1)

                        def add(part, e):
                            a, z = PARTS_OF_X[part]
                            nth = item(part, e)
                            dve.wait_ge(down_done, nth + 1)
                            if e == 0:
                                dve.wait_ge(acc_start, part + 1)
                            else:
                                dve.wait_ge(acc_done, item(part, e - 1) + 1)
                            for t in range(a, z):
                                last = nc.vector.scalar_tensor_tensor(
                                    out=acc[:, t, :], in0=ps[:, 4 + part, (t - a) * P:(t - a + 1) * P],
                                    scalar=comb[:, t, e:e + 1], in1=acc[:, t, :],
                                    op0=ALU.mult, op1=ALU.add)
                            last.then_inc(acc_done, 1)

                        second.take_product(dve, 0, 4)
                        second.norm.apply(dve, 0)
                        gather_b.take(dve, 5, 6)
                        route(0)
                        second.take_product(dve, 1, 5)
                        take_comb(0)
                        second.norm.apply(dve, 1)
                        start_acc(0)
                        add(0, 0)
                        route(1)
                        add(0, 1)
                        take_comb(1)
                        add(0, 2)
                        start_acc(1)
                        for e in range(3):
                            add(1, e)
                        for e in range(3, NE):
                            for part in range(2):
                                add(part, e)
                                if e == NE - 1:
                                    dve.wait_ge(acc_done, item(part, e) + 1)
                                    last_norm.moments(dve, part)
                                    if part == 0:
                                        last_norm.apply(dve, 0)
                        last_norm.apply(dve, 1)

        self_attention()
        with ExitStack() as cross:
            shared = cross_attention(cross)
            again = nc.values_load(flag[0:1, 0:1], min_val=0, max_val=1)
            with nc.If(again > 0):
                general_cross_attention(shared)
        attention_memory.close()
        feed_forward()


def kernel(x, ctx_1024, mask_1x1xSxS2_ff0, L0_attn_Wq, L0_attn_bq, L0_attn_Wk, L0_attn_bk, L0_attn_Wv,
           L0_attn_bv, L0_attn_Wo, L0_attn_bo, L0_attn_slopes, L0_xattn_Wq, L0_xattn_bq, L0_xattn_Wk,
           L0_xattn_bk, L0_xattn_Wv, L0_xattn_bv, L0_xattn_Wo, L0_xattn_bo, L0_ffn_shared_w1,
           L0_ffn_shared_b1, L0_ffn_shared_w2, L0_ffn_shared_b2, L0_ffn_router_w, L0_ffn_router_b,
           L0_ffn_spec_w1, L0_ffn_spec_b1, L0_ffn_spec_w2, L0_ffn_spec_b2):
    import concourse.bacc as bacc
    from concourse.bass_utils import run_bass_kernel_spmd

    def of(a):
        return np.asarray(a)

    order = np.array([(2 * (p % PAIRS) + p // 64) * DH + (p // PAIRS) % DH for p in range(P)])
    x2 = of(x).reshape(TOK, P)
    wq2, wk2 = of(L0_xattn_Wq)[order], of(L0_xattn_Wk)[order]
    w_t = np.stack([of(w).T for w in (L0_attn_Wq, L0_attn_Wk, L0_attn_Wv, L0_attn_Wo, wq2, wk2,
                                      L0_xattn_Wv, L0_xattn_Wo)], 1)
    bias_cols = np.stack([of(L0_attn_bq), of(L0_attn_bk), of(L0_attn_bv), of(L0_xattn_bq)[order],
                          of(L0_xattn_bk)[order], of(L0_xattn_bv)], 1)
    rows = np.concatenate([of(L0_attn_bo), of(L0_xattn_bo), of(L0_ffn_router_b), of(L0_attn_slopes)])
    w1 = np.concatenate([of(L0_ffn_spec_w1), of(L0_ffn_shared_w1)[None]])
    w2 = np.concatenate([of(L0_ffn_spec_w2), of(L0_ffn_shared_w2)[None]])
    b1 = np.concatenate([of(L0_ffn_spec_b1), of(L0_ffn_shared_b1)[None]])
    b2 = np.concatenate([of(L0_ffn_spec_b2), of(L0_ffn_shared_b2)[None]])
    experts = np.concatenate([
        w1.transpose(0, 2, 1),
        w2.transpose(0, 2, 1).reshape(NE, FC, P, P).transpose(0, 2, 1, 3).reshape(NE, P, F)], 2)
    arrays = {
        "x": x2, "x_t": x2.T, "ctx_t": of(ctx_1024).transpose(0, 2, 1),
        "mask": np.tile(of(mask_1x1xSxS2_ff0).reshape(S, SK), (2, 1)),
        "w_t": w_t, "bias_cols": bias_cols, "rows": np.tile(rows[None], (P, 1)),
        "router_t": of(L0_ffn_router_w).T, "experts": experts,
        "b1": b1.reshape(NE * FC, P).T, "b2": b2, "constants": CONSTANTS,
    }
    arrays = {f"in_{n}": np.ascontiguousarray(a) for n, a in arrays.items()}
    nc = bacc.Bacc("TRN2", target_bir_lowering=False, num_devices=1)
    args = [nc.dram_tensor(n, a.shape, mybir.dt.from_np(a.dtype), kind="ExternalInput").ap()
            for n, a in arrays.items()]
    out = nc.dram_tensor("out_0", (TOK, P), F32, kind="ExternalOutput").ap()
    build(nc, *args, out)
    r = run_bass_kernel_spmd(nc, [arrays], core_ids=[0])
    return r.results[0]["out_0"].reshape(B, S, P)
```
